# Optimizing a Trainium2 kernel written in Bass

```python
import numpy as np
import jax
import jax.numpy as jnp

def _softmax(x, axis=-1):
    return jax.nn.softmax(x, axis=axis)

def _gelu(x):
    return jax.nn.gelu(x, approximate=True)

def _silu(x):
    return jax.nn.silu(x)

def _sigmoid(x):
    return jax.nn.sigmoid(x)

def _layernorm(x, axis=-1, eps=1e-05):
    m = jnp.mean(x, axis=axis, keepdims=True)
    v = jnp.var(x, axis=axis, keepdims=True)
    return (x - m) / jnp.sqrt(v + eps)

def _scatter_add(tgt, idx, src, axis=0):
    return tgt.at[idx].add(src)

def _segment_sum(src, seg, n):
    return jax.ops.segment_sum(src, seg, n)
kernel_name = 'mk_audio_tower_d4_tok_audfeat256_r4_568f11'

def setup_inputs(seed: int=0):
    np.random.seed(seed)
    _w = jnp.asarray

    def _rec_inputs():
        import jax
        import jax.numpy as jnp
        _rk = jax.random.key(seed)
        x = 7.22013e-05 + 1.00017 * jax.random.normal(jax.random.fold_in(_rk, 1), (4, 750, 64), jnp.float32)
        return x
    x = _rec_inputs()

    def _L0_tok_setup():
        import jax, jax.numpy as jnp
        import numpy as np
        WIN = 9
        key = jax.random.key(seed)
        ks = jax.random.split(key, 4)
        N, L, C, U = (8, 1024, 64, 64)
        x = jax.random.normal(ks[0], (N, L, C), dtype=jnp.float32)
        W_qry = jax.random.normal(ks[1], (C, U), dtype=jnp.float32) * 0.05
        W_key = jax.random.normal(ks[2], (C, U), dtype=jnp.float32) * 0.05
        v = jax.random.normal(ks[3], (U,), dtype=jnp.float32) * 0.05
        b = jnp.zeros((U,), dtype=jnp.float32)
        return {'x': x, 'W_qry': W_qry, 'W_key': W_key, 'v': v, 'b': b}
    _L0_tok_all = _L0_tok_setup()
    _L0_tok_in = {k: v for k, v in _L0_tok_all.items() if k in ('W_qry', 'W_key', 'v', 'b')}
    del _L0_tok_all

    def _L0_attn_setup():
        import jax, jax.numpy as jnp
        import numpy as np
        B, L, D = (4, 1024, 64)
        key = jax.random.key(seed)
        kx, kq, kk, kv, ko = jax.random.split(key, 5)
        std = 0.02
        return {'x': jax.random.normal(kx, (B, L, D), dtype=jnp.float32), 'Wq': std * jax.random.normal(kq, (D, D), dtype=jnp.float32), 'Wk': std * jax.random.normal(kk, (D, D), dtype=jnp.float32), 'Wv': std * jax.random.normal(kv, (D, D), dtype=jnp.float32), 'Wo': std * jax.random.normal(ko, (D, D), dtype=jnp.float32)}
    _L0_attn_all = _L0_attn_setup()
    _L0_attn_in = {k: v for k, v in _L0_attn_all.items() if k in ('Wq', 'Wk', 'Wv', 'Wo')}
    del _L0_attn_all

    def _L0_ffn_setup():
        import jax, jax.numpy as jnp
        import numpy as np
        B, S, D, F, E, K = (8, 512, 64, 256, 8, 2)
        key = jax.random.key(seed)
        ks = jax.random.split(key, 10)
        s = 0.02
        return {'x': jax.random.normal(ks[0], (B, S, D), dtype=jnp.float32), 'Wr': jax.random.normal(ks[1], (D, E), dtype=jnp.float32) * s, 'W1s': jax.random.normal(ks[2], (D, F), dtype=jnp.float32) * s, 'b1s': jnp.zeros((F,), dtype=jnp.float32), 'W2s': jax.random.normal(ks[3], (F, D), dtype=jnp.float32) * s, 'b2s': jnp.zeros((D,), dtype=jnp.float32), 'W1p': jax.random.normal(ks[4], (E, D, F), dtype=jnp.float32) * s, 'b1p': jnp.zeros((E, F), dtype=jnp.float32), 'W2p': jax.random.normal(ks[5], (E, F, D), dtype=jnp.float32) * s, 'b2p': jnp.zeros((E, D), dtype=jnp.float32)}
    _L0_ffn_all = _L0_ffn_setup()
    _L0_ffn_in = {k: v for k, v in _L0_ffn_all.items() if k in ('Wr', 'W1s', 'b1s', 'W2s', 'b2s', 'W1p', 'b1p', 'W2p', 'b2p')}
    del _L0_ffn_all

    def _L1_attn_setup():
        import jax, jax.numpy as jnp
        import numpy as np
        import math
        D = 64
        K = 32
        B = 2
        L = 512
        MAX_SEQ = 2048
        PI = math.pi

        def _content_stream(x, Wk1, bk1, Wk2, bk2, Wq1, bq1, Wq2, bq2, Wvc, bvc):
            Bc, Lc, Dc = x.shape
            key_phase = jnp.tanh(jnp.tanh(x @ Wk1 + bk1) @ Wk2 + bk2) * PI
            query_phase = jnp.tanh(jnp.tanh(x @ Wq1 + bq1) @ Wq2 + bq2) * PI
            value = x @ Wvc + bvc
            cos_k = jnp.cos(key_phase)[..., None]
            sin_k = jnp.sin(key_phase)[..., None]
            v_e = value[:, :, None, :]
            mem_real = jnp.cumsum(cos_k * v_e, axis=1)
            mem_imag = jnp.cumsum(sin_k * v_e, axis=1)
            cos_q = jnp.cos(query_phase)[..., None]
            sin_q = jnp.sin(query_phase)[..., None]
            retrieved = (mem_real * cos_q + mem_imag * sin_q).sum(axis=2)
            positions = jnp.arange(1, Lc + 1, dtype=jnp.float32)
            norm = jnp.sqrt(positions * K)[None, :, None]
            return retrieved / norm

        def _pos_stream(x, base_phases, Wvp, bvp):
            Bc, Lc, Dc = x.shape
            phases = base_phases[:Lc][None]
            value = x @ Wvp + bvp
            cos_p = jnp.cos(phases)
            sin_p = jnp.sin(phases)
            mem_real = jnp.cumsum(value * cos_p, axis=1)
            mem_imag = jnp.cumsum(value * sin_p, axis=1)
            retrieved = mem_real * cos_p + mem_imag * sin_p
            positions = jnp.arange(1, Lc + 1, dtype=jnp.float32)
            return retrieved / jnp.sqrt(positions)[None, :, None]
        key = jax.random.key(seed)
        ks = jax.random.split(key, 24)
        s = 0.02
        inp = {}
        inp['x'] = jax.random.normal(ks[0], (B, L, D), dtype=jnp.float32)
        inp['base_phases'] = jax.random.normal(ks[1], (MAX_SEQ, D), dtype=jnp.float32) * PI
        inp['Wk1'] = jax.random.normal(ks[2], (D, D), dtype=jnp.float32) * s
        inp['bk1'] = jnp.zeros((D,), jnp.float32)
        inp['Wk2'] = jax.random.normal(ks[3], (D, K), dtype=jnp.float32) * s
        inp['bk2'] = jnp.zeros((K,), jnp.float32)
        inp['Wq1'] = jax.random.normal(ks[4], (D, D), dtype=jnp.float32) * s
        inp['bq1'] = jnp.zeros((D,), jnp.float32)
        inp['Wq2'] = jax.random.normal(ks[5], (D, K), dtype=jnp.float32) * s
        inp['bq2'] = jnp.zeros((K,), jnp.float32)
        inp['Wvc'] = jax.random.normal(ks[6], (D, D), dtype=jnp.float32) * s
        inp['bvc'] = jnp.zeros((D,), jnp.float32)
        inp['Wvp'] = jax.random.normal(ks[7], (D, D), dtype=jnp.float32) * s
        inp['bvp'] = jnp.zeros((D,), jnp.float32)
        inp['Wg1'] = jax.random.normal(ks[8], (D, D // 4), dtype=jnp.float32) * s
        inp['bg1'] = jnp.zeros((D // 4,), jnp.float32)
        inp['Wg2'] = jax.random.normal(ks[9], (D // 4, 2), dtype=jnp.float32) * s
        inp['bg2'] = jnp.zeros((2,), jnp.float32)
        inp['ln_g'] = jnp.ones((D,), jnp.float32)
        inp['ln_b'] = jnp.zeros((D,), jnp.float32)
        inp['Wo'] = jax.random.normal(ks[10], (D, D), dtype=jnp.float32) * s
        inp['bo'] = jnp.zeros((D,), jnp.float32)
        return inp
    _L1_attn_all = _L1_attn_setup()
    _L1_attn_in = {k: v for k, v in _L1_attn_all.items() if k in ('base_phases', 'Wk1', 'bk1', 'Wk2', 'bk2', 'Wq1', 'bq1', 'Wq2', 'bq2', 'Wvc', 'bvc', 'Wvp', 'bvp', 'Wg1', 'bg1', 'Wg2', 'bg2', 'ln_g', 'ln_b', 'Wo', 'bo')}
    del _L1_attn_all

    def _L1_ffn_setup():
        import jax, jax.numpy as jnp
        import numpy as np
        B, S, H, NH, NE = (4, 256, 64, 4, 4)
        D = H // NH
        EPS = 1e-08

        def layernorm(x, g, b):
            m = jnp.mean(x, axis=-1, keepdims=True)
            v = jnp.mean((x - m) ** 2, axis=-1, keepdims=True)
            return (x - m) / jnp.sqrt(v + EPS) * g + b
        key = jax.random.key(seed)
        ks = jax.random.split(key, 18)
        sc = 0.05
        return {'x': jax.random.normal(ks[0], (B, S, H), jnp.float32), 'hl_w': jax.random.normal(ks[1], (NH, D, H), jnp.float32) * sc, 'hl_b': jax.random.normal(ks[2], (NH, D), jnp.float32) * sc, 'wq': jax.random.normal(ks[3], (NH, NE, D, D), jnp.float32) * sc, 'wk': jax.random.normal(ks[4], (NH, D, D), jnp.float32) * sc, 'wv': jax.random.normal(ks[5], (NH, D, D), jnp.float32) * sc, 'gate_w': jax.random.normal(ks[6], (NH, NE, NE * D), jnp.float32) * sc, 'gate_b': jax.random.normal(ks[7], (NH, NE), jnp.float32) * sc, 'ln_g': jnp.ones((D,), jnp.float32), 'ln_b': jnp.zeros((D,), jnp.float32), 'fc1_w': jax.random.normal(ks[8], (D, D), jnp.float32) * sc, 'fc1_b': jax.random.normal(ks[9], (D,), jnp.float32) * sc, 'fc2_w': jax.random.normal(ks[10], (D, D), jnp.float32) * sc, 'fc2_b': jax.random.normal(ks[11], (D,), jnp.float32) * sc, 'fnorm_g': jnp.ones((D,), jnp.float32), 'fnorm_b': jnp.zeros((D,), jnp.float32), 'fgate_w': jax.random.normal(ks[12], (NH, H), jnp.float32) * sc}
    _L1_ffn_all = _L1_ffn_setup()
    _L1_ffn_in = {k: v for k, v in _L1_ffn_all.items() if k in ('hl_w', 'hl_b', 'wq', 'wk', 'wv', 'gate_w', 'gate_b', 'ln_g', 'ln_b', 'fc1_w', 'fc1_b', 'fc2_w', 'fc2_b', 'fnorm_g', 'fnorm_b', 'fgate_w')}
    del _L1_ffn_all

    def _L2_attn_setup():
        import jax, jax.numpy as jnp
        import numpy as np
        key = jax.random.key(seed)
        k1, k2, k3 = jax.random.split(key, 3)
        d = 64
        x = jax.random.normal(k1, (8, 512, d), dtype=jnp.float32)
        Wq = jax.random.normal(k2, (d, d), dtype=jnp.float32) * d ** (-0.5)
        Wk = jax.random.normal(k3, (d, d), dtype=jnp.float32) * d ** (-0.5)
        return {'x': x, 'Wq': Wq, 'Wk': Wk}
    _L2_attn_all = _L2_attn_setup()
    _L2_attn_in = {k: v for k, v in _L2_attn_all.items() if k in ('Wq', 'Wk')}
    del _L2_attn_all

    def _L2_ffn_setup():
        import jax, jax.numpy as jnp
        import numpy as np
        DIM = 64
        HEADS = 8
        NUM_KEYS = 64
        NUM_KV = NUM_KEYS ** 2
        PK_TOPK = 16
        FINAL_TOPK = 16
        DIM_KEY = DIM // 2
        P = 2

        def _pk(x, Wq_pk, pk_keys):
            b, n, _ = x.shape
            q = (x @ Wq_pk).reshape(b, n, P, HEADS, DIM_KEY).transpose(2, 0, 1, 3, 4)
            sim = jnp.einsum('pbnhd,pkhd->pbnhk', q, pk_keys)
            scores, idx = jax.lax.top_k(sim, PK_TOPK)
            idx0 = idx[0]
            idx1 = idx[1] * NUM_KEYS
            index = (idx0[..., :, None] + idx1[..., None, :]).reshape(b, n, HEADS, PK_TOPK * PK_TOPK)
            score = (scores[0][..., :, None] + scores[1][..., None, :]).reshape(b, n, HEADS, PK_TOPK * PK_TOPK)
            final_scores, pk_idx = jax.lax.top_k(score, FINAL_TOPK)
            final_indices = jnp.take_along_axis(index, pk_idx, axis=-1)
            final_scores = jax.nn.softmax(final_scores, axis=-1)
            return (final_scores, final_indices)
        key = jax.random.key(seed)
        ks = jax.random.split(key, 7)
        b, n = (2, 256)
        std = 0.02
        x = jax.random.normal(ks[0], (b, n, DIM), dtype=jnp.float32)
        Wq_pk = jax.random.normal(ks[1], (DIM, P * HEADS * DIM_KEY), dtype=jnp.float32) * std
        pk_keys = jax.random.normal(ks[2], (P, NUM_KEYS, HEADS, DIM_KEY), dtype=jnp.float32) * std
        Wq = jax.random.normal(ks[3], (DIM, HEADS * DIM), dtype=jnp.float32) * std
        keys_table = jax.random.normal(ks[4], (NUM_KV * HEADS, DIM), dtype=jnp.float32) * std
        values_table = jax.random.normal(ks[5], (NUM_KV * HEADS, DIM), dtype=jnp.float32) * std
        Wo = jax.random.normal(ks[6], (DIM * HEADS, DIM), dtype=jnp.float32) * std
        return {'x': x, 'Wq_pk': Wq_pk, 'pk_keys': pk_keys, 'Wq': Wq, 'keys_table': keys_table, 'values_table': values_table, 'Wo': Wo}
    _L2_ffn_all = _L2_ffn_setup()
    _L2_ffn_in = {k: v for k, v in _L2_ffn_all.items() if k in ('Wq_pk', 'pk_keys', 'Wq', 'keys_table', 'values_table', 'Wo')}
    del _L2_ffn_all

    def _L3_attn_setup():
        import jax, jax.numpy as jnp
        import numpy as np
        EMB, HEADS, DEPTH, SEQ, BATCH = (64, 8, 4, 2048, 4)
        DH = EMB // HEADS
        FF = 4 * EMB
        EPS = 1e-05

        def _layernorm(x, g, b):
            mu = x.mean(-1, keepdims=True)
            var = ((x - mu) ** 2).mean(-1, keepdims=True)
            return (x - mu) * jax.lax.rsqrt(var + EPS) * g + b

        def _linear_attn(x, Wq, Wk, Wv, Wo, bo):
            b, n, dm = x.shape
            split = lambda t: t.reshape(b, n, HEADS, DH).transpose(0, 2, 1, 3)
            scale = DH ** (-0.25)
            q = jax.nn.softmax(split(x @ Wq) * scale, axis=-1)
            k = jax.nn.softmax(split(x @ Wk) * scale, axis=-2)
            v = split(x @ Wv)
            context = jnp.einsum('bhnd,bhne->bhde', k, v)
            out = jnp.einsum('bhnd,bhde->bhne', q, context)
            out = out.transpose(0, 2, 1, 3).reshape(b, n, dm)
            return out @ Wo + bo

        def _forward(x, Wq, Wk, Wv, Wo, bo, ln1_g, ln1_b, W1, b1, W2, b2, ln2_g, ln2_b):
            for i in range(DEPTH):
                h = _layernorm(x, ln1_g[i], ln1_b[i])
                x = x + _linear_attn(h, Wq[i], Wk[i], Wv[i], Wo[i], bo[i])
                h = _layernorm(x, ln2_g[i], ln2_b[i])
                x = x + (jax.nn.gelu(h @ W1[i] + b1[i], approximate=False) @ W2[i] + b2[i])
            return x
        key = jax.random.key(seed)
        ks = jax.random.split(key, 8)
        w = lambda k, shape: jax.random.normal(k, shape, dtype=jnp.float32) * 0.02
        D = DEPTH
        return {'x': jax.random.normal(ks[0], (BATCH, SEQ, EMB), dtype=jnp.float32), 'Wq': w(ks[1], (D, EMB, EMB)), 'Wk': w(ks[2], (D, EMB, EMB)), 'Wv': w(ks[3], (D, EMB, EMB)), 'Wo': w(ks[4], (D, EMB, EMB)), 'bo': jnp.zeros((D, EMB), jnp.float32), 'ln1_g': jnp.ones((D, EMB), jnp.float32), 'ln1_b': jnp.zeros((D, EMB), jnp.float32), 'W1': w(ks[5], (D, EMB, FF)), 'b1': jnp.zeros((D, FF), jnp.float32), 'W2': w(ks[6], (D, FF, EMB)), 'b2': jnp.zeros((D, EMB), jnp.float32), 'ln2_g': jnp.ones((D, EMB), jnp.float32), 'ln2_b': jnp.zeros((D, EMB), jnp.float32)}
    _L3_attn_all = _L3_attn_setup()
    _L3_attn_in = {k: v for k, v in _L3_attn_all.items() if k in ('Wq', 'Wk', 'Wv', 'Wo', 'bo', 'ln1_g', 'ln1_b', 'W1', 'b1', 'W2', 'b2', 'ln2_g', 'ln2_b')}
    del _L3_attn_all

    def _L3_ffn_setup():
        import jax, jax.numpy as jnp
        import numpy as np
        B, T, C = (64, 96, 64)
        NH, NKV = (4, 2)
        HD = C // NH
        NREP = NH // NKV
        NE, TOPK = (8, 2)
        HID = int(8 / 3 * C)
        EPS_RMS = 1e-06

        def _rope_tables(t_len):
            inv_freq = 1.0 / 10000.0 ** (np.arange(0, HD, 2, dtype=np.float32) / HD)
            t = np.arange(t_len, dtype=np.float32)
            freqs = np.outer(t, inv_freq)
            emb = np.concatenate([freqs, freqs], axis=-1)
            return (jnp.asarray(np.cos(emb)), jnp.asarray(np.sin(emb)))

        def _rotate_half(x):
            h = x.shape[-1] // 2
            return jnp.concatenate([-x[..., h:], x[..., :h]], axis=-1)

        def _rmsnorm(v, w):
            return v * jax.lax.rsqrt(jnp.mean(v * v, axis=-1, keepdims=True) + EPS_RMS) * w
        key = jax.random.key(seed)
        ks = jax.random.split(key, 10)
        s = lambda k, shape: jax.random.normal(k, shape, jnp.float32) * 0.02
        return {'x': jax.random.normal(ks[0], (B, T, C), jnp.float32), 'ln1_w': jnp.ones((C,), jnp.float32), 'ln2_w': jnp.ones((C,), jnp.float32), 'wq': s(ks[1], (NH * HD, C)), 'wk': s(ks[2], (NKV * HD, C)), 'wv': s(ks[3], (NKV * HD, C)), 'wo': s(ks[4], (C, C)), 'router_w': s(ks[5], (NE, C)), 'w1': s(ks[6], (NE, HID, C)), 'w2': s(ks[7], (NE, C, HID)), 'w3': s(ks[8], (NE, HID, C))}
    _L3_ffn_all = _L3_ffn_setup()
    _L3_ffn_in = {k: v for k, v in _L3_ffn_all.items() if k in ('ln1_w', 'ln2_w', 'wq', 'wk', 'wv', 'wo', 'router_w', 'w1', 'w2', 'w3')}
    del _L3_ffn_all
    return {'x': x, 'L0_tok_W_qry': _L0_tok_in['W_qry'], 'L0_tok_W_key': _L0_tok_in['W_key'], 'L0_tok_v': _L0_tok_in['v'], 'L0_tok_b': _L0_tok_in['b'], 'L0_attn_Wq': _L0_attn_in['Wq'], 'L0_attn_Wk': _L0_attn_in['Wk'], 'L0_attn_Wv': _L0_attn_in['Wv'], 'L0_attn_Wo': _L0_attn_in['Wo'], 'L0_ffn_Wr': _L0_ffn_in['Wr'], 'L0_ffn_W1s': _L0_ffn_in['W1s'], 'L0_ffn_b1s': _L0_ffn_in['b1s'], 'L0_ffn_W2s': _L0_ffn_in['W2s'], 'L0_ffn_b2s': _L0_ffn_in['b2s'], 'L0_ffn_W1p': _L0_ffn_in['W1p'], 'L0_ffn_b1p': _L0_ffn_in['b1p'], 'L0_ffn_W2p': _L0_ffn_in['W2p'], 'L0_ffn_b2p': _L0_ffn_in['b2p'], 'L1_attn_base_phases': _L1_attn_in['base_phases'], 'L1_attn_Wk1': _L1_attn_in['Wk1'], 'L1_attn_bk1': _L1_attn_in['bk1'], 'L1_attn_Wk2': _L1_attn_in['Wk2'], 'L1_attn_bk2': _L1_attn_in['bk2'], 'L1_attn_Wq1': _L1_attn_in['Wq1'], 'L1_attn_bq1': _L1_attn_in['bq1'], 'L1_attn_Wq2': _L1_attn_in['Wq2'], 'L1_attn_bq2': _L1_attn_in['bq2'], 'L1_attn_Wvc': _L1_attn_in['Wvc'], 'L1_attn_bvc': _L1_attn_in['bvc'], 'L1_attn_Wvp': _L1_attn_in['Wvp'], 'L1_attn_bvp': _L1_attn_in['bvp'], 'L1_attn_Wg1': _L1_attn_in['Wg1'], 'L1_attn_bg1': _L1_attn_in['bg1'], 'L1_attn_Wg2': _L1_attn_in['Wg2'], 'L1_attn_bg2': _L1_attn_in['bg2'], 'L1_attn_ln_g': _L1_attn_in['ln_g'], 'L1_attn_ln_b': _L1_attn_in['ln_b'], 'L1_attn_Wo': _L1_attn_in['Wo'], 'L1_attn_bo': _L1_attn_in['bo'], 'L1_ffn_hl_w': _L1_ffn_in['hl_w'], 'L1_ffn_hl_b': _L1_ffn_in['hl_b'], 'L1_ffn_wq': _L1_ffn_in['wq'], 'L1_ffn_wk': _L1_ffn_in['wk'], 'L1_ffn_wv': _L1_ffn_in['wv'], 'L1_ffn_gate_w': _L1_ffn_in['gate_w'], 'L1_ffn_gate_b': _L1_ffn_in['gate_b'], 'L1_ffn_ln_g': _L1_ffn_in['ln_g'], 'L1_ffn_ln_b': _L1_ffn_in['ln_b'], 'L1_ffn_fc1_w': _L1_ffn_in['fc1_w'], 'L1_ffn_fc1_b': _L1_ffn_in['fc1_b'], 'L1_ffn_fc2_w': _L1_ffn_in['fc2_w'], 'L1_ffn_fc2_b': _L1_ffn_in['fc2_b'], 'L1_ffn_fnorm_g': _L1_ffn_in['fnorm_g'], 'L1_ffn_fnorm_b': _L1_ffn_in['fnorm_b'], 'L1_ffn_fgate_w': _L1_ffn_in['fgate_w'], 'L2_attn_Wq': _L2_attn_in['Wq'], 'L2_attn_Wk': _L2_attn_in['Wk'], 'L2_ffn_Wq_pk': _L2_ffn_in['Wq_pk'], 'L2_ffn_pk_keys': _L2_ffn_in['pk_keys'], 'L2_ffn_Wq': _L2_ffn_in['Wq'], 'L2_ffn_keys_table': _L2_ffn_in['keys_table'], 'L2_ffn_values_table': _L2_ffn_in['values_table'], 'L2_ffn_Wo': _L2_ffn_in['Wo'], 'L3_attn_Wq': _L3_attn_in['Wq'], 'L3_attn_Wk': _L3_attn_in['Wk'], 'L3_attn_Wv': _L3_attn_in['Wv'], 'L3_attn_Wo': _L3_attn_in['Wo'], 'L3_attn_bo': _L3_attn_in['bo'], 'L3_attn_ln1_g': _L3_attn_in['ln1_g'], 'L3_attn_ln1_b': _L3_attn_in['ln1_b'], 'L3_attn_W1': _L3_attn_in['W1'], 'L3_attn_b1': _L3_attn_in['b1'], 'L3_attn_W2': _L3_attn_in['W2'], 'L3_attn_b2': _L3_attn_in['b2'], 'L3_attn_ln2_g': _L3_attn_in['ln2_g'], 'L3_attn_ln2_b': _L3_attn_in['ln2_b'], 'L3_ffn_ln1_w': _L3_ffn_in['ln1_w'], 'L3_ffn_ln2_w': _L3_ffn_in['ln2_w'], 'L3_ffn_wq': _L3_ffn_in['wq'], 'L3_ffn_wk': _L3_ffn_in['wk'], 'L3_ffn_wv': _L3_ffn_in['wv'], 'L3_ffn_wo': _L3_ffn_in['wo'], 'L3_ffn_router_w': _L3_ffn_in['router_w'], 'L3_ffn_w1': _L3_ffn_in['w1'], 'L3_ffn_w2': _L3_ffn_in['w2'], 'L3_ffn_w3': _L3_ffn_in['w3']}

def reference(x, L0_tok_W_qry, L0_tok_W_key, L0_tok_v, L0_tok_b, L0_attn_Wq, L0_attn_Wk, L0_attn_Wv, L0_attn_Wo, L0_ffn_Wr, L0_ffn_W1s, L0_ffn_b1s, L0_ffn_W2s, L0_ffn_b2s, L0_ffn_W1p, L0_ffn_b1p, L0_ffn_W2p, L0_ffn_b2p, L1_attn_base_phases, L1_attn_Wk1, L1_attn_bk1, L1_attn_Wk2, L1_attn_bk2, L1_attn_Wq1, L1_attn_bq1, L1_attn_Wq2, L1_attn_bq2, L1_attn_Wvc, L1_attn_bvc, L1_attn_Wvp, L1_attn_bvp, L1_attn_Wg1, L1_attn_bg1, L1_attn_Wg2, L1_attn_bg2, L1_attn_ln_g, L1_attn_ln_b, L1_attn_Wo, L1_attn_bo, L1_ffn_hl_w, L1_ffn_hl_b, L1_ffn_wq, L1_ffn_wk, L1_ffn_wv, L1_ffn_gate_w, L1_ffn_gate_b, L1_ffn_ln_g, L1_ffn_ln_b, L1_ffn_fc1_w, L1_ffn_fc1_b, L1_ffn_fc2_w, L1_ffn_fc2_b, L1_ffn_fnorm_g, L1_ffn_fnorm_b, L1_ffn_fgate_w, L2_attn_Wq, L2_attn_Wk, L2_ffn_Wq_pk, L2_ffn_pk_keys, L2_ffn_Wq, L2_ffn_keys_table, L2_ffn_values_table, L2_ffn_Wo, L3_attn_Wq, L3_attn_Wk, L3_attn_Wv, L3_attn_Wo, L3_attn_bo, L3_attn_ln1_g, L3_attn_ln1_b, L3_attn_W1, L3_attn_b1, L3_attn_W2, L3_attn_b2, L3_attn_ln2_g, L3_attn_ln2_b, L3_ffn_ln1_w, L3_ffn_ln2_w, L3_ffn_wq, L3_ffn_wk, L3_ffn_wv, L3_ffn_wo, L3_ffn_router_w, L3_ffn_w1, L3_ffn_w2, L3_ffn_w3):
    import jax
    import jax.numpy as jnp

    def _L0_tok_ref(x, W_qry, W_key, v, b):
        import jax, jax.numpy as jnp
        import numpy as np
        WIN = 9
        N, L, C = x.shape
        n_w = L - WIN + 1
        idx = jnp.arange(n_w)[:, None] + jnp.arange(WIN)[None, :]
        x_win = x[:, idx]
        x_ctr = x[:, WIN // 2:WIN // 2 + n_w]
        key = jnp.einsum('nwsc,cu->nwsu', x_win, W_key)
        qry = jnp.einsum('nwc,cu->nwu', x_ctr, W_qry)
        score = jnp.einsum('nwsu,u->nws', jnp.tanh(qry[:, :, None, :] + key + b), v)
        weight = jax.nn.softmax(score, axis=2)
        out = jnp.einsum('nwsc,nws->nwc', x_win, weight)
        return out

    def _L0_attn_ref(x, Wq, Wk, Wv, Wo):
        import jax, jax.numpy as jnp
        import numpy as np
        B, L, D = (4, 1024, 64)
        q = x @ Wq.T
        k = x @ Wk.T
        v = x @ Wv.T
        logits = jnp.einsum('bld,bmd->blm', q, k)
        Lq = x.shape[1]
        causal_mask = jnp.triu(jnp.ones((Lq, Lq), dtype=bool), k=1)
        logits = jnp.where(causal_mask[None], jnp.asarray(0.0, logits.dtype), logits)
        attn = jax.nn.relu(logits)
        row_counts = jnp.maximum(jnp.arange(Lq, dtype=attn.dtype), 1.0)
        attn = attn / row_counts[None, :, None]
        ctx = jnp.einsum('blm,bmd->bld', attn, v)
        return ctx @ Wo.T

    def _L0_ffn_ref(x, Wr, W1s, b1s, W2s, b2s, W1p, b1p, W2p, b2p):
        import jax, jax.numpy as jnp
        import numpy as np
        B, S, D, F, E, K = (8, 512, 64, 256, 8, 2)
        gelu = lambda t: jax.nn.gelu(t, approximate=False)
        shared = gelu(x @ W1s + b1s) @ W2s + b2s
        rw = jax.nn.softmax(x @ Wr, axis=-1)
        topw, topi = jax.lax.top_k(rw, K)
        topw = topw / jnp.sum(topw, axis=-1, keepdims=True)
        mask = jnp.sum(jax.nn.one_hot(topi, E, dtype=topw.dtype) * topw[..., None], axis=-2)
        h = gelu(jnp.einsum('bsd,edf->bsef', x, W1p) + b1p)
        priv = jnp.einsum('bsef,efd->bsed', h, W2p) + b2p
        routed = jnp.einsum('bsed,bse->bsd', priv, mask)
        return shared + routed

    def _L1_attn_ref(x, base_phases, Wk1, bk1, Wk2, bk2, Wq1, bq1, Wq2, bq2, Wvc, bvc, Wvp, bvp, Wg1, bg1, Wg2, bg2, ln_g, ln_b, Wo, bo):
        import jax, jax.numpy as jnp
        import numpy as np
        import math
        D = 64
        K = 32
        B = 2
        L = 512
        MAX_SEQ = 2048
        PI = math.pi

        def _content_stream(x, Wk1, bk1, Wk2, bk2, Wq1, bq1, Wq2, bq2, Wvc, bvc):
            Bc, Lc, Dc = x.shape
            key_phase = jnp.tanh(jnp.tanh(x @ Wk1 + bk1) @ Wk2 + bk2) * PI
            query_phase = jnp.tanh(jnp.tanh(x @ Wq1 + bq1) @ Wq2 + bq2) * PI
            value = x @ Wvc + bvc
            cos_k = jnp.cos(key_phase)[..., None]
            sin_k = jnp.sin(key_phase)[..., None]
            v_e = value[:, :, None, :]
            mem_real = jnp.cumsum(cos_k * v_e, axis=1)
            mem_imag = jnp.cumsum(sin_k * v_e, axis=1)
            cos_q = jnp.cos(query_phase)[..., None]
            sin_q = jnp.sin(query_phase)[..., None]
            retrieved = (mem_real * cos_q + mem_imag * sin_q).sum(axis=2)
            positions = jnp.arange(1, Lc + 1, dtype=jnp.float32)
            norm = jnp.sqrt(positions * K)[None, :, None]
            return retrieved / norm

        def _pos_stream(x, base_phases, Wvp, bvp):
            Bc, Lc, Dc = x.shape
            phases = base_phases[:Lc][None]
            value = x @ Wvp + bvp
            cos_p = jnp.cos(phases)
            sin_p = jnp.sin(phases)
            mem_real = jnp.cumsum(value * cos_p, axis=1)
            mem_imag = jnp.cumsum(value * sin_p, axis=1)
            retrieved = mem_real * cos_p + mem_imag * sin_p
            positions = jnp.arange(1, Lc + 1, dtype=jnp.float32)
            return retrieved / jnp.sqrt(positions)[None, :, None]
        pos_retrieved = _pos_stream(x, base_phases, Wvp, bvp)
        content_retrieved = _content_stream(x, Wk1, bk1, Wk2, bk2, Wq1, bq1, Wq2, bq2, Wvc, bvc)
        gates = jax.nn.softmax(jax.nn.relu(x @ Wg1 + bg1) @ Wg2 + bg2, axis=-1)
        combined = gates[:, :, 0:1] * pos_retrieved + gates[:, :, 1:2] * content_retrieved
        mu = combined.mean(axis=-1, keepdims=True)
        var = ((combined - mu) ** 2).mean(axis=-1, keepdims=True)
        normed = (combined - mu) / jnp.sqrt(var + 1e-05) * ln_g + ln_b
        return x + normed @ Wo + bo

    def _L1_ffn_ref(x, hl_w, hl_b, wq, wk, wv, gate_w, gate_b, ln_g, ln_b, fc1_w, fc1_b, fc2_w, fc2_b, fnorm_g, fnorm_b, fgate_w):
        import jax, jax.numpy as jnp
        import numpy as np
        B, S, H, NH, NE = (4, 256, 64, 4, 4)
        D = H // NH
        EPS = 1e-08

        def layernorm(x, g, b):
            m = jnp.mean(x, axis=-1, keepdims=True)
            v = jnp.mean((x - m) ** 2, axis=-1, keepdims=True)
            return (x - m) / jnp.sqrt(v + EPS) * g + b
        b, s, h = x.shape
        nh, d, _ = wk.shape
        ne = wq.shape[1]
        sx = jnp.einsum('bsh,ndh->bnsd', x, hl_w) + hl_b[None, :, None, :]
        pad = sx == 0
        q = jnp.einsum('bnsd,neod->bneso', sx, wq)
        k = jnp.einsum('bnsd,nod->bnso', sx, wk)
        v = jnp.einsum('bnsd,nod->bnso', sx, wv)
        causal = jnp.where(jnp.tril(jnp.ones((s, s), bool)), 0.0, -jnp.inf).astype(x.dtype)
        scores = jnp.einsum('bnesd,bntd->bnest', q, k) * d ** 0.5 + causal
        att = jax.nn.softmax(scores, axis=-1)
        qkv = jnp.einsum('bnest,bntd->bnesd', att, v)
        qkv = jnp.where(pad[:, :, None], 0.0, qkv)
        out = jnp.transpose(qkv, (0, 1, 3, 2, 4)).reshape(b, nh, s, ne * d)
        gs = jax.nn.softmax(jnp.einsum('bnsf,nef->bnse', out, gate_w) + gate_b[None, :, None, :], axis=-1)
        mixed = jnp.einsum('bnsed,bnse->bnsd', out.reshape(b, nh, s, ne, d), gs)
        resid = sx[jnp.arange(nh), jnp.arange(nh)]
        hn = layernorm(mixed + resid, ln_g, ln_b)
        f_n = jnp.transpose(hn, (0, 2, 1, 3)).reshape(b, s, h)
        fx = f_n.reshape(b, s, nh, d)
        pm = fx == 0
        hx = jnp.where(pm, 0.0, fx @ fc1_w.T + fc1_b)
        hx = jax.nn.relu(hx)
        hx = jnp.where(pm, 0.0, hx @ fc2_w.T + fc2_b)
        hx = layernorm(hx + fx, fnorm_g, fnorm_b)
        fout = hx.reshape(b, s, h)
        fg = jax.nn.softmax(fout @ fgate_w.T, axis=-1)
        return (fout.reshape(b, s, nh, d) * fg[..., None]).reshape(b, s, h)

    def _L2_attn_ref(x, Wq, Wk):
        import jax, jax.numpy as jnp
        import numpy as np
        d = x.shape[-1]
        scale = d ** (-0.5)
        q = jnp.einsum('bnd,ed->bne', x, Wq)
        k = jnp.einsum('bnd,ed->bne', x, Wk)
        sim = jnp.einsum('bid,bjd->bij', q, k) * scale
        attn = jax.nn.softmax(sim, axis=-1)
        out = jnp.einsum('bij,bjd->bid', attn, x)
        return out

    def _L2_ffn_ref(x, Wq_pk, pk_keys, Wq, keys_table, values_table, Wo):
        import jax, jax.numpy as jnp
        import numpy as np
        DIM = 64
        HEADS = 8
        NUM_KEYS = 64
        NUM_KV = NUM_KEYS ** 2
        PK_TOPK = 16
        FINAL_TOPK = 16
        DIM_KEY = DIM // 2
        P = 2

        def _pk(x, Wq_pk, pk_keys):
            b, n, _ = x.shape
            q = (x @ Wq_pk).reshape(b, n, P, HEADS, DIM_KEY).transpose(2, 0, 1, 3, 4)
            sim = jnp.einsum('pbnhd,pkhd->pbnhk', q, pk_keys)
            scores, idx = jax.lax.top_k(sim, PK_TOPK)
            idx0 = idx[0]
            idx1 = idx[1] * NUM_KEYS
            index = (idx0[..., :, None] + idx1[..., None, :]).reshape(b, n, HEADS, PK_TOPK * PK_TOPK)
            score = (scores[0][..., :, None] + scores[1][..., None, :]).reshape(b, n, HEADS, PK_TOPK * PK_TOPK)
            final_scores, pk_idx = jax.lax.top_k(score, FINAL_TOPK)
            final_indices = jnp.take_along_axis(index, pk_idx, axis=-1)
            final_scores = jax.nn.softmax(final_scores, axis=-1)
            return (final_scores, final_indices)
        b, n, d = x.shape
        q = (x @ Wq).reshape(b, n, HEADS, DIM) * DIM ** (-0.5)
        kv_scores, indices = _pk(x, Wq_pk, pk_keys)
        offsets = jnp.arange(HEADS, dtype=indices.dtype) * NUM_KV
        ind = indices + offsets[None, None, :, None]
        k = jnp.einsum('bnhk,bnhkd->bnhd', kv_scores, keys_table[ind])
        v = jnp.einsum('bnhk,bnhkd->bnhd', kv_scores, values_table[ind])
        sim = jnp.einsum('bihd,bjhd->bhij', q, k)
        neg = -jnp.finfo(sim.dtype).max
        causal = jnp.tril(jnp.ones((n, n), dtype=bool))
        sim = jnp.where(causal, sim, neg)
        attn = jax.nn.softmax(sim, axis=-1)
        out = jnp.einsum('bhij,bjhd->bhid', attn, v)
        out = out.transpose(0, 2, 1, 3).reshape(b, n, HEADS * DIM)
        return out @ Wo

    def _L3_attn_ref(x, Wq, Wk, Wv, Wo, bo, ln1_g, ln1_b, W1, b1, W2, b2, ln2_g, ln2_b):
        import jax, jax.numpy as jnp
        import numpy as np
        EMB, HEADS, DEPTH, SEQ, BATCH = (64, 8, 4, 2048, 4)
        DH = EMB // HEADS
        FF = 4 * EMB
        EPS = 1e-05

        def _layernorm(x, g, b):
            mu = x.mean(-1, keepdims=True)
            var = ((x - mu) ** 2).mean(-1, keepdims=True)
            return (x - mu) * jax.lax.rsqrt(var + EPS) * g + b

        def _linear_attn(x, Wq, Wk, Wv, Wo, bo):
            b, n, dm = x.shape
            split = lambda t: t.reshape(b, n, HEADS, DH).transpose(0, 2, 1, 3)
            scale = DH ** (-0.25)
            q = jax.nn.softmax(split(x @ Wq) * scale, axis=-1)
            k = jax.nn.softmax(split(x @ Wk) * scale, axis=-2)
            v = split(x @ Wv)
            context = jnp.einsum('bhnd,bhne->bhde', k, v)
            out = jnp.einsum('bhnd,bhde->bhne', q, context)
            out = out.transpose(0, 2, 1, 3).reshape(b, n, dm)
            return out @ Wo + bo

        def _forward(x, Wq, Wk, Wv, Wo, bo, ln1_g, ln1_b, W1, b1, W2, b2, ln2_g, ln2_b):
            for i in range(DEPTH):
                h = _layernorm(x, ln1_g[i], ln1_b[i])
                x = x + _linear_attn(h, Wq[i], Wk[i], Wv[i], Wo[i], bo[i])
                h = _layernorm(x, ln2_g[i], ln2_b[i])
                x = x + (jax.nn.gelu(h @ W1[i] + b1[i], approximate=False) @ W2[i] + b2[i])
            return x
        return _forward(x, Wq, Wk, Wv, Wo, bo, ln1_g, ln1_b, W1, b1, W2, b2, ln2_g, ln2_b)

    def _L3_ffn_ref(x, ln1_w, ln2_w, wq, wk, wv, wo, router_w, w1, w2, w3):
        import jax, jax.numpy as jnp
        import numpy as np
        B, T, C = (64, 96, 64)
        NH, NKV = (4, 2)
        HD = C // NH
        NREP = NH // NKV
        NE, TOPK = (8, 2)
        HID = int(8 / 3 * C)
        EPS_RMS = 1e-06

        def _rope_tables(t_len):
            inv_freq = 1.0 / 10000.0 ** (np.arange(0, HD, 2, dtype=np.float32) / HD)
            t = np.arange(t_len, dtype=np.float32)
            freqs = np.outer(t, inv_freq)
            emb = np.concatenate([freqs, freqs], axis=-1)
            return (jnp.asarray(np.cos(emb)), jnp.asarray(np.sin(emb)))

        def _rotate_half(x):
            h = x.shape[-1] // 2
            return jnp.concatenate([-x[..., h:], x[..., :h]], axis=-1)

        def _rmsnorm(v, w):
            return v * jax.lax.rsqrt(jnp.mean(v * v, axis=-1, keepdims=True) + EPS_RMS) * w
        Bx, Tx, Cx = x.shape
        h = _rmsnorm(x, ln1_w)
        q = (h @ wq.T).reshape(Bx, Tx, NH, HD).transpose(0, 2, 1, 3)
        k = (h @ wk.T).reshape(Bx, Tx, NKV, HD).transpose(0, 2, 1, 3)
        v = (h @ wv.T).reshape(Bx, Tx, NKV, HD).transpose(0, 2, 1, 3)
        cos, sin = _rope_tables(Tx)
        cos, sin = (cos[None, None], sin[None, None])
        q = q * cos + _rotate_half(q) * sin
        k = k * cos + _rotate_half(k) * sin
        k = jnp.repeat(k, NREP, axis=1)
        v = jnp.repeat(v, NREP, axis=1)
        scores = jnp.einsum('bhtd,bhsd->bhts', q, k) / jnp.sqrt(jnp.float32(HD))
        causal = jnp.tril(jnp.ones((Tx, Tx), dtype=bool))
        scores = jnp.where(causal[None, None], scores, jnp.float32(-1e+30))
        att = jax.nn.softmax(scores, axis=-1)
        y = jnp.einsum('bhts,bhsd->bhtd', att, v).transpose(0, 2, 1, 3).reshape(Bx, Tx, Cx)
        x = x + y @ wo.T
        flat = _rmsnorm(x, ln2_w).reshape(-1, Cx)
        probs = jax.nn.softmax(flat @ router_w.T, axis=-1)
        tp, ti = jax.lax.top_k(probs, TOPK)
        tp = tp / (jnp.sum(tp, axis=-1, keepdims=True) + 1e-09)
        weights = jnp.sum(tp[..., None] * jax.nn.one_hot(ti, NE, dtype=flat.dtype), axis=1)
        out = jnp.zeros_like(flat)
        for e in range(NE):
            hh = jax.nn.silu(flat @ w1[e].T) * (flat @ w3[e].T)
            out = out + weights[:, e:e + 1] * (hh @ w2[e].T)
        return x + out.reshape(Bx, Tx, Cx)
    h = _L0_tok_ref(x, L0_tok_W_qry, L0_tok_W_key, L0_tok_v, L0_tok_b)
    h = h + _L0_attn_ref(_layernorm(h, axis=-1), L0_attn_Wq, L0_attn_Wk, L0_attn_Wv, L0_attn_Wo)
    h = h + _L0_ffn_ref(_layernorm(h, axis=-1), L0_ffn_Wr, L0_ffn_W1s, L0_ffn_b1s, L0_ffn_W2s, L0_ffn_b2s, L0_ffn_W1p, L0_ffn_b1p, L0_ffn_W2p, L0_ffn_b2p)
    h = h + _L1_attn_ref(_layernorm(h, axis=-1), L1_attn_base_phases, L1_attn_Wk1, L1_attn_bk1, L1_attn_Wk2, L1_attn_bk2, L1_attn_Wq1, L1_attn_bq1, L1_attn_Wq2, L1_attn_bq2, L1_attn_Wvc, L1_attn_bvc, L1_attn_Wvp, L1_attn_bvp, L1_attn_Wg1, L1_attn_bg1, L1_attn_Wg2, L1_attn_bg2, L1_attn_ln_g, L1_attn_ln_b, L1_attn_Wo, L1_attn_bo)
    h = h + _L1_ffn_ref(_layernorm(h, axis=-1), L1_ffn_hl_w, L1_ffn_hl_b, L1_ffn_wq, L1_ffn_wk, L1_ffn_wv, L1_ffn_gate_w, L1_ffn_gate_b, L1_ffn_ln_g, L1_ffn_ln_b, L1_ffn_fc1_w, L1_ffn_fc1_b, L1_ffn_fc2_w, L1_ffn_fc2_b, L1_ffn_fnorm_g, L1_ffn_fnorm_b, L1_ffn_fgate_w)
    h = h + _L2_attn_ref(_layernorm(h, axis=-1), L2_attn_Wq, L2_attn_Wk)
    h = h + _L2_ffn_ref(_layernorm(h, axis=-1), L2_ffn_Wq_pk, L2_ffn_pk_keys, L2_ffn_Wq, L2_ffn_keys_table, L2_ffn_values_table, L2_ffn_Wo)
    h = h + _L3_attn_ref(_layernorm(h, axis=-1), L3_attn_Wq, L3_attn_Wk, L3_attn_Wv, L3_attn_Wo, L3_attn_bo, L3_attn_ln1_g, L3_attn_ln1_b, L3_attn_W1, L3_attn_b1, L3_attn_W2, L3_attn_b2, L3_attn_ln2_g, L3_attn_ln2_b)
    h = h + _L3_ffn_ref(_layernorm(h, axis=-1), L3_ffn_ln1_w, L3_ffn_ln2_w, L3_ffn_wq, L3_ffn_wk, L3_ffn_wv, L3_ffn_wo, L3_ffn_router_w, L3_ffn_w1, L3_ffn_w2, L3_ffn_w3)
    return h

_drawn_inputs = setup_inputs


def setup_inputs(seed=0):
    import zlib

    import numpy as np

    out = dict(_drawn_inputs(seed))
    spreads = {'L0_tok_b': (0.0, 0.454),
     'L0_ffn_b1s': (0.0, 0.1),
     'L0_ffn_b2s': (0.0, 0.1),
     'L0_ffn_b1p': (0.0, 0.334),
     'L0_ffn_b2p': (0.0, 0.1),
     'L1_attn_bk1': (0.0, 0.8),
     'L1_attn_bk2': (0.0, 0.8),
     'L1_attn_bq1': (0.0, 0.8),
     'L1_attn_bq2': (0.0, 0.8),
     'L1_attn_bvc': (0.0, 0.1),
     'L1_attn_bvp': (0.0, 2.0),
     'L1_attn_bg1': (0.0, 2.0),
     'L1_attn_bg2': (0.0, 0.8),
     'L1_attn_ln_g': (1.0, 0.6),
     'L1_attn_ln_b': (0.0, 0.478),
     'L1_attn_bo': (0.0, 0.1),
     'L1_ffn_ln_g': (1.0, 0.2),
     'L1_ffn_ln_b': (0.0, 0.317),
     'L1_ffn_fnorm_g': (1.0, 0.2),
     'L1_ffn_fnorm_b': (0.0, 0.289),
     'L3_attn_bo': (0.0, 0.1),
     'L3_attn_ln1_g': (1.0, 0.6),
     'L3_attn_ln1_b': (0.0, 0.8),
     'L3_attn_b1': (0.0, 0.562),
     'L3_attn_b2': (0.0, 0.1),
     'L3_attn_ln2_g': (1.0, 0.6),
     'L3_attn_ln2_b': (0.0, 0.8),
     'L3_ffn_ln1_w': (1.0, 0.6),
     'L3_ffn_ln2_w': (1.0, 0.6)}
    factors = {'L0_attn_Wq': 8.0,
     'L0_attn_Wk': 8.0,
     'L0_attn_Wv': 6.557,
     'L0_attn_Wo': 7.381,
     'L1_attn_base_phases': 8.0,
     'L1_attn_Wk1': 8.0,
     'L1_attn_Wk2': 8.0,
     'L1_attn_Wq1': 8.0,
     'L1_attn_Wq2': 8.0,
     'L1_attn_Wvp': 8.0,
     'L1_attn_Wg1': 24.734,
     'L1_attn_Wg2': 25.747,
     'L1_ffn_wq': 21.418,
     'L1_ffn_wk': 23.018,
     'L1_ffn_gate_w': 54.683,
     'L1_ffn_gate_b': 49.923,
     'L1_ffn_fc1_w': 8.0,
     'L1_ffn_fc1_b': 8.0,
     'L1_ffn_fc2_w': 6.275,
     'L1_ffn_fc2_b': 2.897,
     'L2_ffn_Wq_pk': 8.0,
     'L2_ffn_pk_keys': 8.0,
     'L2_ffn_Wq': 64.0,
     'L2_ffn_keys_table': 64.0,
     'L2_ffn_values_table': 8.0,
     'L2_ffn_Wo': 8.0,
     'L3_attn_Wq': 8.0,
     'L3_attn_Wk': 8.0,
     'L3_attn_Wv': 4.862,
     'L3_attn_Wo': 5.588,
     'L3_attn_W1': 2.741,
     'L3_ffn_wq': 8.0,
     'L3_ffn_wk': 8.0,
     'L3_ffn_wv': 8.0,
     'L3_ffn_wo': 8.0,
     'L3_ffn_router_w': 8.0,
     'L3_ffn_w1': 8.0,
     'L3_ffn_w2': 8.0,
     'L3_ffn_w3': 8.0}
    for name, (base, spread) in spreads.items():
        noise = np.random.default_rng([zlib.crc32(name.encode()), seed]).standard_normal(out[name].shape)
        drawn = base * np.exp(spread * noise) if base else spread * noise
        out[name] = jnp.asarray(drawn.astype(out[name].dtype))
    for name, factor in factors.items():
        out[name] = (out[name] * factor).astype(out[name].dtype)
    return out
```

```python
import numpy as np
from contextlib import ExitStack, contextmanager

import concourse.bass as bass
from concourse import mybir

F32 = mybir.dt.float32
BF16 = mybir.dt.bfloat16
I32 = mybir.dt.int32
U32 = mybir.dt.uint32
ALU = mybir.AluOpType
ACT = mybir.ActivationFunctionType
AX = mybir.AxisListType

NSEQ, LIN, WIN, D = 4, 750, 9, 64
L = LIN - WIN + 1
P, NT = 106, 7
HALF = L // 2
assert P * NT == L
NEG = -1e30
E0, F0 = 8, 256
NH, NE, HD = 4, 4, 16
PKH, PKD, NK = 8, 32, 64
E3, F3 = 8, 170
DEPTH = 4
RUNS = [(0, 16), (1, 8), (2, 5), (3, 4), (4, 3)]
PAIRED = 52
LOWEST = -3.0e38
PI_DOWN = 3.1415925


def _pad(a, rows):
    out = np.zeros((rows,) + a.shape[1:], np.float32)
    out[:a.shape[0]] = a
    return out


def _spread(a):
    rows, heads = a.shape[0], a.shape[1] // HD
    out = np.zeros((rows, heads, 32), np.float32)
    out[:, :, :HD] = a.reshape(rows, heads, HD)
    return out.reshape(rows, heads * 32)


def _rows(v, n=P):
    return np.ascontiguousarray(np.broadcast_to(np.asarray(v).reshape(1, -1), (n, np.asarray(v).size)))


def _block_diagonal(blocks):
    r, c = blocks[0].shape
    out = np.zeros((r * len(blocks), c * len(blocks)), np.float32)
    for i, b in enumerate(blocks):
        out[i * r:(i + 1) * r, i * c:(i + 1) * c] = b
    return out


def constants():
    pos = np.arange(L)
    tiles = lambda v: v.reshape(NT, P).T.astype(np.float32)
    k, q = np.meshgrid(np.arange(P), np.arange(P), indexing="ij")
    inv = 1.0 / 10000.0 ** (np.arange(0, HD, 2, dtype=np.float32) / HD)
    f = np.outer(np.arange(L, dtype=np.float32), inv)
    f = np.concatenate([f, f], -1)
    sign = np.where(np.arange(HD) < HD // 2, -1.0, 1.0)
    four = lambda t: np.ascontiguousarray(_spread(np.tile(t, (1, 4))).T).astype(np.float32)
    return {
        "ident": np.eye(128, dtype=np.float32),
        "later": np.where(q > k, NEG, 0.0).astype(np.float32),
        "keep_t": (q >= k).astype(np.float32),
        "inv_row": tiles(1.0 / np.maximum(pos.astype(np.float32), 1.0)),
        "inv_pos": tiles(1.0 / np.sqrt((pos + 1).astype(np.float32))),
        "inv_pos32": tiles(1.0 / np.sqrt(((pos + 1) * 32).astype(np.float32))),
        "ones": np.ones((1, L), np.float32),
        "half_pi": np.full((128, 1), np.pi / 2, np.float32),
        "experts": _rows(np.tile(np.arange(8, dtype=np.float32), NT)),
        "two_eyes": np.concatenate([np.eye(64), np.eye(64)]).astype(np.float32),
        "blocks8": np.kron(np.eye(8), np.ones((8, 8))).astype(np.float32),
        "cos4": four(np.cos(f)),
        "sin4": four(np.sin(f) * sign),
    }


def layout(i):
    i = {k: np.asarray(v) for k, v in i.items()}
    cat = np.concatenate
    aug = lambda w, b: cat([w, b.reshape(1, -1)], 0)
    w = dict(constants())
    w["tok_q"] = aug(i["L0_tok_W_qry"], i["L0_tok_b"])
    w["tok_k"] = i["L0_tok_W_key"]
    w["tok_v"] = i["L0_tok_v"].reshape(D, 1)
    w["a0_q"], w["a0_k"], w["a0_v"], w["a0_o"] = i["L0_attn_Wq"].T, i["L0_attn_Wk"].T, i["L0_attn_Wv"], i["L0_attn_Wo"].T
    w["m0_r"] = i["L0_ffn_Wr"]
    w1 = cat([i["L0_ffn_W1p"], i["L0_ffn_W1s"][None]], 0)
    b1 = cat([i["L0_ffn_b1p"], i["L0_ffn_b1s"][None]], 0)
    w["m0_w1"] = cat([w1, b1[:, None]], 1).transpose(1, 0, 2).reshape(D + 1, -1)
    w2 = cat([i["L0_ffn_W2p"], i["L0_ffn_W2s"][None]], 0)
    w["m0_w2"] = w2.reshape(E0 + 1, 2, 128, D).transpose(2, 0, 1, 3).reshape(128, -1)
    w["m0_b2"] = cat([i["L0_ffn_b2p"], i["L0_ffn_b2s"][None]], 0).reshape(1, -1)
    for n in "kq":
        w[f"h1_{n}1"] = aug(i[f"L1_attn_W{n}1"], i[f"L1_attn_b{n}1"])
        one = aug(i[f"L1_attn_W{n}2"], i[f"L1_attn_b{n}2"])
        w[f"h1_{n}2"] = cat([one, one], 1)
    w["h1_vc"] = aug(i["L1_attn_Wvc"], i["L1_attn_bvc"])
    vp = aug(i["L1_attn_Wvp"], i["L1_attn_bvp"])
    w["h1_vp"] = cat([vp, vp], 1)
    w["h1_g1"] = aug(i["L1_attn_Wg1"], i["L1_attn_bg1"])
    w["h1_g2"] = aug(i["L1_attn_Wg2"], i["L1_attn_bg2"])
    w["h1_g"], w["h1_b"] = _rows(i["L1_attn_ln_g"]), _rows(i["L1_attn_ln_b"])
    w["h1_o"] = aug(i["L1_attn_Wo"], i["L1_attn_bo"])
    ph = i["L1_attn_base_phases"][:L].T
    w["phases"] = cat([ph, ph], 0)
    hl = aug(i["L1_ffn_hl_w"].reshape(D, D).T, i["L1_ffn_hl_b"])
    w["f1_hl"] = hl
    heads = []
    for n in range(NH):
        q4 = _spread(cat([i["L1_ffn_wq"][n, e].T for e in range(NE)], 1))
        k4 = _spread(np.tile(i["L1_ffn_wk"][n].T, (1, NE)))
        heads.append(cat([hl[:, HD * n:HD * n + HD], _pad(q4, D + 1), _pad(k4, D + 1), _pad(i["L1_ffn_wv"][n].T, D + 1)], 1))
    w["f1_heads"] = cat(heads, 1)
    gw = [i["L1_ffn_gate_w"][n].T for n in range(NH)]
    w["f1_gate"] = cat([_block_diagonal(gw[:2]), _block_diagonal(gw[2:])], 1)
    w["f1_gate_b"] = _rows(i["L1_ffn_gate_b"])
    w["f1_g"], w["f1_b"] = _rows(i["L1_ffn_ln_g"]), _rows(i["L1_ffn_ln_b"])
    w["f1_fg"], w["f1_fb"] = _rows(i["L1_ffn_fnorm_g"]), _rows(i["L1_ffn_fnorm_b"])
    for n in "12":
        w[f"f1_fc{n}"] = aug(_block_diagonal([i[f"L1_ffn_fc{n}_w"].T] * NH), np.tile(i[f"L1_ffn_fc{n}_b"], NH))
    w["f1_fgate"] = i["L1_ffn_fgate_w"].T
    w["a2_q"], w["a2_k"] = i["L2_attn_Wq"].T, i["L2_attn_Wk"].T
    pkq, keys = i["L2_ffn_Wq_pk"], i["L2_ffn_pk_keys"]
    w["pk_q"] = pkq
    w["pk_keys"] = cat([_block_diagonal([keys[p, :, h].T for h in range(4 * g, 4 * g + 4)]) for p in range(2) for g in range(2)], 1)
    w["f3_1"], w["f3_2"] = _rows(i["L3_ffn_ln1_w"]), _rows(i["L3_ffn_ln2_w"])
    swap = (np.arange(HD) + HD // 2) % HD
    wq = i["L3_ffn_wq"].T.reshape(D, NH, HD)
    wk = np.repeat(i["L3_ffn_wk"].T.reshape(D, NH // 2, HD), 2, 1)
    for name, m in (("q", wq), ("k", wk)):
        w[f"f3_{name}"] = _spread(m.reshape(D, -1))
        w[f"f3_{name}s"] = _spread(m[:, :, swap].reshape(D, -1))
    w["f3_v"] = i["L3_ffn_wv"].T
    w["f3_o"] = i["L3_ffn_wo"].T
    w["f3_r"] = i["L3_ffn_router_w"].T
    w["f3_w1"] = i["L3_ffn_w1"].transpose(2, 0, 1).reshape(D, -1)
    w["f3_w3"] = i["L3_ffn_w3"].transpose(2, 0, 1).reshape(D, -1)
    w["f3_w2"] = i["L3_ffn_w2"].transpose(0, 2, 1).reshape(E3, 2, F3 // 2, D).transpose(2, 0, 1, 3).reshape(F3 // 2, -1)
    loop_of = lambda k: (1 if k[:3] in ("tok", "a0_", "m0_", "h1_", "pha") else
                         2 if k[:3] in ("a2_", "pk_", "f3_") or k in ("f1_heads", "f1_gate", "cos4", "sin4") else 0)
    where, packs, shared = {}, [], 0
    for part in range(3):
        names = [k for k in w if loop_of(k) == part]
        at = 0
        pack = np.zeros((128, sum(w[k].shape[1] for k in names)), np.float32)
        for k in names:
            r, c = w[k].shape
            pack[:r, at:at + c] = w[k]
            where[k] = (r, shared + at, c)
            at += c
        packs.append(pack)
        shared = packs[0].shape[1]
    pq = pkq.reshape(D, 2, PKH, PKD)
    hw = np.zeros((PKH, 128, 3 * D), np.float32)
    for h in range(PKH):
        hw[h, :D, :D] = pq[:, :, h].reshape(D, D)
        hw[h, :D, D:2 * D] = i["L2_ffn_Wq"][:, h * D:h * D + D]
        hw[h, D:, 2 * D:] = i["L2_ffn_Wo"][h * D:h * D + D]
    pairs = np.ones((PKH, 2 * PKD + 1, NK // 2, 2, NK), np.float32)
    for h in range(PKH):
        pairs[h, :PKD] = keys[0, :, h].T.reshape(PKD, NK // 2, 2, 1)
        pairs[h, PKD:2 * PKD] = keys[1, :, h].T.reshape(PKD, 1, 1, NK)
    kv = cat([i["L2_ffn_keys_table"], i["L2_ffn_values_table"]], 1).reshape(PKH, NK, NK // 2, 2, 2 * D)
    tables = np.ascontiguousarray(kv.transpose(0, 3, 1, 2, 4)).reshape(PKH, 128, (NK // 2) * 2 * D)
    wrap = lambda a: cat([a, a[:1]], 0)
    lw = np.zeros((DEPTH, 128, 3 * D + D + 4 * D + 2 * D + D + 4 * D), np.float32)
    for l in range(DEPTH):
        at = 0
        for a in (i["L3_attn_Wq"][l], i["L3_attn_Wk"][l], i["L3_attn_Wv"][l], aug(i["L3_attn_Wo"][l], i["L3_attn_bo"][l]),
                  aug(i["L3_attn_W1"][l], i["L3_attn_b1"][l]),
                  i["L3_attn_W2"][l].reshape(2, 128, D).transpose(1, 0, 2).reshape(128, -1), i["L3_attn_b2"][l].reshape(1, D),
                  _rows(i["L3_attn_ln1_g"][l]), _rows(i["L3_attn_ln1_b"][l]), _rows(i["L3_attn_ln2_g"][l]), _rows(i["L3_attn_ln2_b"][l])):
            lw[l, :a.shape[0], at:at + a.shape[1]] = a
            at += a.shape[1]
    return where, {"x": np.ascontiguousarray(i["x"]), "pack_0": packs[0], "pack_1": packs[1], "pack_2": packs[2], "head_weights": wrap(hw),
                   "pairs": wrap(pairs.reshape(PKH, 2 * PKD + 1, NK // 2 * 2 * NK)), "tables": wrap(tables), "layers": lw}


SEMS = ["step_dve", "step_pool", "step_act", "loaded", "loaded_b", "stored", "var_ready", "std_ready", "turned", "copied_a", "copied_d",
        "scores_ready", "max_ready", "probs_ready", "probs_turned", "turned_a", "turned_d", "pv_ready", "out_done",
        "hidden_ready", "hidden_act", "hidden_used", "experts_out", "gated", "prod_ready", "prod_used", "sum_ready",
        "tanh_ready", "phase_ready", "feat_ready", "mask_ready", "value_ready", "dense_ready", "exp_ready", "picked",
        "kv_ready", "kv_done"]


class Tower:

    def __init__(self, nc, ctx, where, dram):
        self.nc, self.ctx, self.where, self.dram = nc, ctx, where, dram
        self.s = {n: ctx.enter_context(nc.semaphore(n)) for n in SEMS}
        self.nums = [s.num for s in self.s.values()]
        self.columns = max(o + c for _, o, c in where.values())
        self.W = self.sb("weights", [128, self.columns])
        self.PS = ctx.enter_context(nc.psum_tensor("psum", [128, 8 * 512], F32))
        self.H = self.sb("h", [P, NT, D])
        self.X = self.sb("xn", [P, NT, D])
        self.XT = self.sb("xt", [D + 1, LIN])
        self.QT = self.sb("qt", [128, LIN])
        self.KT = self.sb("kt", [128, LIN])
        self.V = self.sb("v", [P, NT, D])
        self.Y = self.sb("y", [P, NT, D])
        self.A = self.sb("a", [P, NT, D])
        self.SQ = self.sb("sq", [P, NT, D])
        self.ST = self.sb("stat", [P, 128])
        self.ST2 = self.sb("stat2", [P, 128])
        self.PR = self.sb("probs", [P, 2, L])
        self.PT = self.sb("probs_t", [128, NT, L])
        self.NM = self.sb("neg_max", [P, 8])
        self.RS = self.sb("row_sum", [P, 8])
        self.identb = self.sb("ident_bf16", [P, P], BF16)
        self.laterb = self.sb("later_bf16", [P, P], BF16)

    def sb(self, name, shape, dt=F32):
        return self.ctx.enter_context(self.nc.sbuf_tensor(name, shape, dt))[tuple(slice(0, n) for n in shape)]

    def w(self, name):
        r, o, c = self.where[name]
        return self.W[0:r, o:o + c]

    def bank(self, n, m=1):
        return self.PS[:, 512 * n:512 * (n + m)]

    @contextmanager
    def block(self):
        with self.nc.Block() as block:
            yield block
        with self.nc.Block() as block:
            @block.gpsimd
            def _(pool):
                pool.sem_clear(range(min(self.nums), max(self.nums) + 1))

    def chain(self, engine, sem):
        count = [0]

        def link(ins):
            count[0] += 1
            ins.then_inc(sem, 1)
            engine.wait_ge(sem, count[0])
        return link

    def norm(self, src, dst, groups, width, eps, center=True, gamma=None, beta=None):
        s, nc = self.s, self.nc
        stat, sq = self.ST[:, 0:groups], self.SQ[:, :, :].rearrange("p t d -> p (t d)").rearrange("p (g w) -> p g w", w=width)
        wide = lambda a: a.unsqueeze(2).broadcast_to((P, groups, width))
        over = lambda a: a.unsqueeze(1).broadcast_to((P, groups, width))
        with self.block() as block:
            @block.vector
            def _(dve):
                link = self.chain(dve, s["step_dve"])
                at = src
                if center:
                    link(dve.tensor_reduce(stat, src, AX.X, ALU.add))
                    link(dve.tensor_scalar(stat, stat, 1.0 / width, None, ALU.mult))
                    link(dve.tensor_tensor(dst, src, wide(stat), ALU.subtract))
                    at = dst
                link(dve.tensor_tensor(sq, at, at, ALU.mult))
                link(dve.tensor_reduce(stat, sq, AX.X, ALU.add))
                dve.tensor_scalar(stat, stat, 1.0 / width, eps, ALU.mult, ALU.add).then_inc(s["var_ready"], 1)
                dve.wait_ge(s["std_ready"], 1)
                link(dve.reciprocal(stat, stat))
                link(dve.tensor_tensor(dst, at, wide(stat), ALU.mult))
                if gamma is not None:
                    link(dve.tensor_tensor(dst, dst, over(gamma), ALU.mult))
                if beta is not None:
                    link(dve.tensor_tensor(dst, dst, over(beta), ALU.add))

            @block.scalar
            def _(act):
                act.wait_ge(s["var_ready"], 1)
                act.activation(stat, stat, ACT.Sqrt).then_inc(s["std_ready"], 1)

    def turn(self, src, dst, rows=D):
        s = self.s
        with self.block() as block:
            @block.tensor
            def _(pe):
                for t in range(NT):
                    out = self.bank(t // 4)[0:rows, P * (t % 4):P * (t % 4) + P]
                    pe.transpose(out, src[:, t, :], self.w("ident")[0:P, 0:P]).then_inc(s["turned"], 1)

            @block.scalar
            def _(act):
                act.wait_ge(s["turned"], 4)
                act.activation(dst[0:rows, 0:4 * P], self.bank(0)[0:rows, 0:4 * P], ACT.Copy).then_inc(s["copied_a"], 1)

            @block.vector
            def _(dve):
                dve.wait_ge(s["turned"], NT)
                dve.tensor_copy(dst[0:rows, 4 * P:L], self.bank(1)[0:rows, 0:3 * P]).then_inc(s["copied_d"], 1)

    def project(self, jobs):
        s = self.s
        steps = []
        for kind, wt, src, dst, what in jobs:
            if kind == "c":
                m = wt.shape[1]
                for h in range(2):
                    steps.append(([(lambda b, m=m: b[0:m, 0:HALF], wt, src[:, h * HALF:(h + 1) * HALF])],
                                  lambda b, m=m: b[0:m, 0:HALF], dst[0:m, h * HALF:(h + 1) * HALF], what))
            else:
                m = wt.shape[1]
                mms = [(lambda b, t=t, m=m: b[0:P, t * m:(t + 1) * m], src[:, P * t:P * t + P], wt) for t in range(NT)]
                steps.append((mms, lambda b, m=m: b[0:P, 0:NT * m].rearrange("p (t m) -> p t m", m=m), dst, what))
        NB = 8
        with self.block() as block:
            @block.tensor
            def _(pe):
                for n, (mms, _, _, _) in enumerate(steps):
                    if n >= NB:
                        pe.wait_ge(s["copied_a"] if n % 2 == 0 else s["copied_d"], (n - NB) // 2 + 1)
                    for out, lhs, rhs in mms:
                        last = pe.matmul(out(self.bank(n % NB)), lhs, rhs, start=True, stop=True)
                    last.then_inc(s["prod_ready"], 1)

            def evacuate(n, engine, acts):
                _, view, dst, what = steps[n]
                src = view(self.bank(n % NB))
                engine.wait_ge(s["prod_ready"], n + 1)
                if acts:
                    return engine.activation(dst, src, what or ACT.Copy)
                if what == ACT.Relu:
                    return engine.tensor_scalar(dst, src, 0.0, None, ALU.max)
                return engine.tensor_copy(dst, src)

            assert all(what in (None, ACT.Relu, ACT.Tanh) for *_, what in steps)
            only_act = any(what == ACT.Tanh for *_, what in steps)

            @block.scalar
            def _(act):
                for n in range(len(steps)):
                    if only_act or n % 2 == 0:
                        evacuate(n, act, True).then_inc(s["copied_a"] if n % 2 == 0 else s["copied_d"], 1)

            if not only_act:
                @block.vector
                def _(dve):
                    for n in range(1, len(steps), 2):
                        evacuate(n, dve, False).then_inc(s["copied_d"], 1)

    def softmax_attention(self, units, scale, causal):
        s = self.s
        work = [(u, t) for u in range(len(units)) for t in range(NT)]
        keys = lambda t: (t + 1 if causal else NT)
        late = [g for g, (u, t) in enumerate(work) if keys(t) > 4]
        S = lambda g: self.bank(2 * (g % 2), 2)
        T = lambda c: self.bank(4 + c)
        O = lambda g: self.bank(6 + g % 2)
        n_late = lambda g: sum(1 for x in late if x < g)
        PT = [self.PT[0:P, 0, :], self.PT[0:P, 1, :]]
        with self.block() as block:
            @block.tensor
            def _(pe):
                def scores(g):
                    u, t = work[g]
                    qT, kT, _, _ = units[u]
                    if g >= 2:
                        pe.wait_ge(s["probs_ready"], g - 1)
                    width = keys(t) * P
                    for a in range(0, width, 512):
                        e = min(width, a + 512)
                        last = pe.matmul(S(g)[0:P, a:e], qT[:, P * t:P * t + P], kT[:, a:e],
                                         start=True, stop=not (causal and e > P * t))
                        if causal and e > P * t:
                            m = max(a, P * t)
                            last = pe.matmul(S(g)[0:P, m:e], self.identb[:, :], self.laterb[:, m - P * t:e - P * t],
                                             start=False, stop=True)
                    last.then_inc(s["scores_ready"], 1)

                def weigh(g):
                    u, t = work[g]
                    _, _, v, _ = units[u]
                    d = v.shape[2]
                    pe.wait_ge(s["probs_ready"], g + 1)
                    for k in range(keys(t)):
                        if k == 0 and g >= 1:
                            pe.wait_ge(s["turned_a"], g)
                        if k == 4 and n_late(g) >= 1:
                            pe.wait_ge(s["turned_d"], n_late(g))
                        last = pe.transpose(T(k // 4)[0:P, P * (k % 4):P * (k % 4) + P],
                                            self.PR[:, g % 2, P * k:P * k + P], self.w("ident")[0:P, 0:P])
                        if k == min(4, keys(t)) - 1:
                            last.then_inc(s["probs_turned"], 1)
                        elif k == keys(t) - 1:
                            last.then_inc(s["turned"], 1)
                    if g >= 2:
                        pe.wait_ge(s["out_done"], g - 1)
                    for k in range(keys(t)):
                        if k == 0:
                            pe.wait_ge(s["turned_a"], g + 1)
                        if k == 4:
                            pe.wait_ge(s["turned_d"], n_late(g) + 1)
                        last = pe.matmul(O(g)[0:P, 0:d], PT[g % 2][:, P * k:P * k + P], v[:, k, :],
                                         start=(k == 0), stop=(k == keys(t) - 1))
                    last.then_inc(s["pv_ready"], 1)

                for g in range(len(work) + 1):
                    if g < len(work):
                        scores(g)
                    if g >= 1:
                        weigh(g - 1)

            @block.vector
            def _(dve):
                link = self.chain(dve, s["step_dve"])

                def largest(g):
                    u, t = work[g]
                    dve.wait_ge(s["scores_ready"], g + 1)
                    link(dve.tensor_reduce(self.NM[:, g % 2:g % 2 + 1], S(g)[0:P, 0:keys(t) * P], AX.X, ALU.max))
                    dve.tensor_scalar(self.NM[:, 2 + g % 2:3 + g % 2], self.NM[:, g % 2:g % 2 + 1], -scale, None,
                                      ALU.mult).then_inc(s["max_ready"], 1)

                def finish(g):
                    u, t = work[g]
                    _, _, v, out = units[u]
                    if keys(t) > 4:
                        dve.wait_ge(s["turned"], n_late(g) + 1)
                        dve.tensor_copy(PT[g % 2][:, 4 * P:keys(t) * P], T(1)[0:P, 0:(keys(t) - 4) * P])\
                           .then_inc(s["turned_d"], 1)
                    link(dve.reciprocal(self.RS[:, 2 + g % 2:3 + g % 2], self.RS[:, g % 2:g % 2 + 1]))
                    dve.wait_ge(s["pv_ready"], g + 1)
                    dst, add = out(t)
                    src, r = O(g)[0:P, 0:v.shape[2]], self.RS[:, 2 + g % 2:3 + g % 2]
                    if add is None:
                        dve.tensor_scalar(dst, src, r, None, ALU.mult).then_inc(s["out_done"], 1)
                    else:
                        dve.scalar_tensor_tensor(dst, src, r, add, ALU.mult, ALU.add).then_inc(s["out_done"], 1)

                for g in range(len(work) + 1):
                    if g < len(work):
                        if g >= 2:
                            dve.wait_ge(s["probs_ready"], g - 1)
                        largest(g)
                    if g >= 1:
                        dve.wait_ge(s["probs_ready"], g)
                        finish(g - 1)

            @block.scalar
            def _(act):
                for g in range(len(work) + 1):
                    if g >= 1:
                        u, t = work[g - 1]
                        n = min(4, keys(t)) * P
                        act.wait_ge(s["probs_turned"], g)
                        act.activation(PT[(g - 1) % 2][:, 0:n], T(0)[0:P, 0:n], ACT.Copy).then_inc(s["turned_a"], 1)
                    if g < len(work):
                        u, t = work[g]
                        act.wait_ge(s["max_ready"], g + 1)
                        if g >= 2:
                            act.wait_ge(s["out_done"], g - 1)
                        act.activation(self.PR[:, g % 2, 0:keys(t) * P], S(g)[0:P, 0:keys(t) * P], ACT.Exp,
                                       bias=self.NM[:, 2 + g % 2:3 + g % 2], scale=scale,
                                       accum_out=self.RS[:, g % 2:g % 2 + 1]).then_inc(s["probs_ready"], 1)

    def causal_product(self, qT, kT, v, relu, out):
        s = self.s
        taken = lambda j: s["copied_a"] if j % 2 == 0 else s["copied_d"]
        with self.block() as block:
            @block.tensor
            def _(pe):
                for j in range(NT):
                    if j >= 3:
                        pe.wait_ge(taken(j - 3), (j - 3) // 2 + 1)
                    S = self.bank(2 * (j % 3), 2)
                    for a in range(P * j, L, 512):
                        e = min(L, a + 512)
                        last = pe.matmul(S[0:P, a - P * j:e - P * j], kT[:, P * j:P * j + P], qT[:, a:e],
                                         start=True, stop=True)
                    last.then_inc(s["scores_ready"], 1)
                for t in range(NT):
                    pe.wait_ge(s["mask_ready"], t + 1)
                    for k in range(t + 1):
                        last = pe.matmul(self.bank(7)[0:P, D * t:D * t + D], self.PT[0:P, k, P * t:P * t + P], v[:, k, :],
                                         start=(k == 0), stop=(k == t))
                last.then_inc(s["pv_ready"], 1)

            @block.scalar
            def _(act):
                for j in range(0, NT, 2):
                    act.wait_ge(s["scores_ready"], j + 1)
                    act.activation(self.PT[0:P, j, P * j:L], self.bank(2 * (j % 3), 2)[0:P, 0:L - P * j],
                                   ACT.Relu if relu else ACT.Copy).then_inc(s["copied_a"], 1)

            @block.gpsimd
            def _(pool):
                for j in range(NT):
                    pool.wait_ge(taken(j), j // 2 + 1)
                    diagonal = self.PT[0:P, j, P * j:P * j + P]
                    pool.tensor_tensor(diagonal, diagonal, self.w("keep_t"), ALU.mult).then_inc(s["mask_ready"], 1)

            @block.vector
            def _(dve):
                for j in range(1, NT, 2):
                    dve.wait_ge(s["scores_ready"], j + 1)
                    S = self.bank(2 * (j % 3), 2)[0:P, 0:L - P * j]
                    if relu:
                        dve.tensor_scalar(self.PT[0:P, j, P * j:L], S, 0.0, None, ALU.max).then_inc(s["copied_d"], 1)
                    else:
                        dve.tensor_copy(self.PT[0:P, j, P * j:L], S).then_inc(s["copied_d"], 1)
                dve.wait_ge(s["pv_ready"], 1)
                out(dve, self.chain(dve, s["step_dve"]), self.bank(7)[0:P, 0:NT * D].rearrange("p (t d) -> p t d", d=D))

    def softmax_rows(self, dve, act_sems, link, x, groups, width, scale_into_exp=1.0):
        s = self.s
        m = self.ST[:, 0:groups]
        wide = m.unsqueeze(2).broadcast_to((P, groups, width))
        link(dve.tensor_reduce(m, x, AX.X, ALU.max))
        dve.tensor_tensor(x, x, wide, ALU.subtract).then_inc(s["var_ready"], 1)
        dve.wait_ge(s["std_ready"], 1)
        link(dve.tensor_reduce(m, x, AX.X, ALU.add))
        link(dve.reciprocal(m, m))
        link(dve.tensor_tensor(x, x, wide, ALU.mult))

    def softmax_block(self, x, groups, width, before=None, after=None, scale=1.0):
        s = self.s
        with self.block() as block:
            @block.vector
            def _(dve):
                link = self.chain(dve, s["step_dve"])
                if before is not None:
                    before(dve, link)
                self.softmax_rows(dve, None, link, x, groups, width)
                if after is not None:
                    after(dve, link)

            @block.scalar
            def _(act):
                act.wait_ge(s["var_ready"], 1)
                act.activation(x, x, ACT.Exp, scale=scale).then_inc(s["std_ready"], 1)

    def add(self, dst, a, b):
        with self.block() as block:
            @block.vector
            def _(dve):
                dve.tensor_tensor(dst, a, b, ALU.add).then_inc(self.s["step_dve"], 1)

    def top_two(self, probs, gates, eps):
        s = self.s
        top, idx, pick = self.TOP, self.IDX, self.TOPF
        g3 = lambda a: a.rearrange("p (t e) -> p t e", e=8)
        with self.block() as block:
            @block.vector
            def _(dve):
                link = self.chain(dve, s["step_dve"])
                for t in range(NT):
                    dve.max(top[:, 8 * t:8 * t + 8], probs[:, t, :]).then_inc(s["max_ready"], 1)
                dve.wait_ge(s["max_ready"], NT)
                for t in range(NT):
                    dve.max_index(idx[:, 8 * t:8 * t + 8], top[:, 8 * t:8 * t + 8], probs[:, t, :]).then_inc(s["mask_ready"], 1)
                dve.wait_ge(s["mask_ready"], NT)
                link(dve.tensor_copy(pick, idx))
                at = lambda j: g3(pick)[:, :, j:j + 1].broadcast_to((P, NT, 8))
                e = g3(self.w("experts"))
                m0, m1 = g3(self.ST[:, 0:56]), g3(self.ST2[:, 0:56])
                link(dve.tensor_tensor(m0, e, at(0), ALU.is_equal))
                link(dve.tensor_tensor(m1, e, at(1), ALU.is_equal))
                link(dve.tensor_tensor(m0, m0, m1, ALU.add))
                den = self.ST2[:, 64:64 + NT]
                t3 = g3(top)
                link(dve.tensor_tensor(den.unsqueeze(2), t3[:, :, 0:1], t3[:, :, 1:2], ALU.add))
                if eps:
                    link(dve.tensor_scalar(den, den, eps, None, ALU.add))
                link(dve.reciprocal(den, den))
                link(dve.tensor_tensor(m0, m0, probs, ALU.mult))
                link(dve.tensor_tensor(gates, m0, den.unsqueeze(2).broadcast_to((P, NT, 8)), ALU.mult))

    def window_pool(self, b):
        s, X9, SC = self.s, self.X9, self.ST2[:, 0:NT * WIN]
        with self.block() as block:
            @block.sync
            def _(sp):
                x = self.dram["x"]
                for t in range(NT):
                    src = bass.AP(x.tensor, x.offset + t * P * D, [[LIN * D, NSEQ], [D, P], [1, WIN * D]])
                    sp.dma_start(X9[:, t, :], src[bass.ds(b, 1)].rearrange("o p c -> (o p) c")).then_inc(s["loaded"], 16)

            @block.tensor
            def _(pe):
                pe.wait_ge(s["loaded"], 16 * NT)
                for t in range(NT + 1):
                    src = X9[:, t, 0:D] if t < NT else X9[:, NT - 1, (WIN - 1) * D:]
                    out = self.bank(t // 4)[0:D, P * (t % 4):P * (t % 4) + P]
                    pe.transpose(out, src, self.w("ident")[0:P, 0:P]).then_inc(s["turned"], 1)

            @block.scalar
            def _(act):
                act.wait_ge(s["turned"], 4)
                act.activation(self.XT[0:D, 0:4 * P], self.bank(0)[0:D, 0:4 * P], ACT.Copy).then_inc(s["copied_a"], 1)

            @block.vector
            def _(dve):
                dve.wait_ge(s["turned"], NT + 1)
                dve.tensor_copy(self.XT[0:D, 4 * P:L], self.bank(1)[0:D, 0:3 * P]).then_inc(s["copied_d"], 1)
                dve.tensor_copy(self.XT[0:D, L:LIN], self.bank(1)[0:D, 4 * P - WIN + 1:4 * P]).then_inc(s["copied_d"], 1)
        hk = LIN // 2
        T = [self.PT[0:D, 0, :], self.PT[0:D, 1, :]]
        with self.block() as block:
            @block.tensor
            def _(pe):
                for h in range(2):
                    pe.matmul(self.bank(h)[0:D, 0:hk], self.w("tok_k"), self.XT[0:D, h * hk:(h + 1) * hk],
                              start=True, stop=True).then_inc(s["prod_ready"], 1)
                for h in range(2):
                    a = WIN // 2 + h * HALF
                    pe.matmul(self.bank(2 + h)[0:D, 0:HALF], self.w("tok_q"), self.ones_xt(a, a + HALF),
                              start=True, stop=True).then_inc(s["prod_ready"], 1)
                for w in range(WIN):
                    pe.wait_ge(s["tanh_ready"], w + 1)
                    for t in range(NT):
                        c = t * WIN + w
                        last = pe.matmul(self.bank(4)[0:P, c:c + 1], T[w % 2][:, P * t:P * t + P], self.w("tok_v"),
                                         start=True, stop=True)
                    last.then_inc(s["scores_ready"], 1)

            @block.vector
            def _(dve):
                for h in range(2):
                    dve.wait_ge(s["prod_ready"], h + 1)
                    dve.tensor_copy(self.KT[0:D, h * hk:(h + 1) * hk], self.bank(h)[0:D, 0:hk]).then_inc(s["copied_d"], 1)
                for h in range(2):
                    dve.wait_ge(s["prod_ready"], h + 3)
                    dve.tensor_copy(self.QT[0:D, h * HALF:(h + 1) * HALF], self.bank(2 + h)[0:D, 0:HALF]).then_inc(s["copied_d"], 1)
                dve.wait_ge(s["copied_d"], 4)
                for w in range(WIN):
                    if w >= 2:
                        dve.wait_ge(s["scores_ready"], w - 1)
                    dve.tensor_tensor(T[w % 2], self.QT[0:D, 0:L], self.KT[0:D, w:w + L], ALU.add).then_inc(s["sum_ready"], 1)
                dve.wait_ge(s["scores_ready"], WIN)
                dve.tensor_copy(SC, self.bank(4)[0:P, 0:NT * WIN]).then_inc(s["out_done"], 1)

            @block.scalar
            def _(act):
                for w in range(WIN):
                    act.wait_ge(s["sum_ready"], w + 1)
                    act.activation(T[w % 2], T[w % 2], ACT.Tanh).then_inc(s["tanh_ready"], 1)

        sc3 = SC.rearrange("p (t w) -> p t w", w=WIN)

        def weigh(dve, link):
            x3 = X9[:, :, :].rearrange("p t (w c) -> p (t w) c", c=D)
            link(dve.tensor_tensor(x3, x3, SC.unsqueeze(2).broadcast_to((P, NT * WIN, D)), ALU.mult))
            link(dve.tensor_reduce(self.H[:, :, :], X9[:, :, :].rearrange("p t (w c) -> p t c w", c=D), AX.X, ALU.add))
        self.softmax_block(sc3, NT, WIN, after=weigh)

    def ones_xt(self, a, e):
        return self.XT[0:D + 1, a:e]

    def relu_attention(self):
        s = self.s
        self.norm(self.H[:, :, :], self.X[:, :, :], NT, D, 1e-5)
        self.turn(self.X, self.XT)
        xt = self.XT[0:D, 0:L]
        self.project([("c", self.w("a0_q"), xt, self.QT[0:D, :], None), ("c", self.w("a0_k"), xt, self.KT[0:D, :], None),
                      ("t", self.VO[:, :], xt, self.V[:, :, :], None)])

        def out(dve, link, acc):
            link(dve.tensor_tensor(self.A[:, :, :], acc, self.w("inv_row").unsqueeze(2).broadcast_to((P, NT, D)), ALU.mult))
            link(dve.tensor_tensor(self.H[:, :, :], self.H[:, :, :], self.A[:, :, :], ALU.add))
        self.causal_product(self.QT[0:D, 0:L], self.KT[0:D, 0:L], self.V, True, out)

    def mixture(self, into, gates, chunk, hidden, out_w, out_b, experts, shared, glu):
        s = self.s
        rows = D if glu else D + 1
        G = [[self.GB[:, 2 * i + c, :] for c in range(2)] for i in range(2)]
        n_ready = 4
        with self.block() as block:
            @block.tensor
            def _(pe):
                def up(e):
                    for c in range(2):
                        for h in range(2):
                            n = 4 * e + 2 * c + h
                            if glu:
                                if n >= 2:
                                    pe.wait_ge(s["hidden_used"], n - 1)
                                for i, wt in enumerate(hidden(e, c)):
                                    last = pe.matmul(self.bank(2 * (n % 2) + i)[0:chunk, 0:HALF], wt,
                                                     self.XT[0:rows, h * HALF:(h + 1) * HALF], start=True, stop=True)
                            else:
                                if n >= 4:
                                    pe.wait_ge(s["hidden_act"], n - 3)
                                last = pe.matmul(self.bank(n % 4)[0:chunk, 0:HALF], hidden(e, c),
                                                 self.XT[0:rows, h * HALF:(h + 1) * HALF], start=True, stop=True)
                            last.then_inc(s["hidden_ready"], 1)

                def down(e):
                    pe.wait_ge(s["hidden_used"] if glu else s["hidden_act"], 4 * e + 4)
                    if e >= 2:
                        pe.wait_ge(s["gated"], e - 1)
                    for t in range(NT):
                        o = self.bank(4 + e % 2)[0:P, D * t:D * t + D]
                        for c in range(2):
                            last = pe.matmul(o, G[e % 2][c][0:chunk, P * t:P * t + P], out_w(e, c),
                                             start=(c == 0), stop=(c == 1 and out_b is None))
                        if out_b is not None:
                            last = pe.matmul(o, self.w("ones")[0:1, P * t:P * t + P], out_b(e), start=False, stop=True)
                    last.then_inc(s["experts_out"], 1)

                for e in range(experts + 1):
                    if e < experts:
                        up(e)
                    if e >= 1:
                        down(e - 1)

            @block.scalar
            def _(act):
                for n in range(4 * experts):
                    e, c, h = n // 4, n // 2 % 2, n % 2
                    act.wait_ge(s["hidden_ready"], n + 1)
                    if e >= 2 and n % 4 == 0:
                        act.wait_ge(s["experts_out"], e - 1)
                    if glu:
                        act.activation(G[e % 2][c][0:chunk, h * HALF:(h + 1) * HALF], self.bank(2 * (n % 2))[0:chunk, 0:HALF],
                                       ACT.Silu).then_inc(s["hidden_act"], 1)
                    else:
                        act.activation(G[e % 2][c][0:chunk, h * HALF:(h + 1) * HALF], self.bank(n % 4)[0:chunk, 0:HALF],
                                       ACT.Gelu).then_inc(s["hidden_act"], 1)

            @block.vector
            def _(dve):
                link = self.chain(dve, s["step_dve"])

                def gate(e):
                    dve.wait_ge(s["experts_out"], e + 1)
                    o = self.bank(4 + e % 2)[0:P, 0:NT * D].rearrange("p (t d) -> p t d", d=D)
                    if e == shared:
                        dve.tensor_tensor(into, into, o, ALU.add).then_inc(s["gated"], 1)
                        dve.wait_ge(s["gated"], e + 1)
                        return
                    dve.tensor_tensor(self.A[:, :, :], o, gates[:, :, e:e + 1].broadcast_to((P, NT, D)), ALU.mult)\
                       .then_inc(s["gated"], 1)
                    dve.wait_ge(s["gated"], e + 1)
                    link(dve.tensor_tensor(into, into, self.A, ALU.add))

                for e in range(experts + 1):
                    if glu and e < experts:
                        for n in range(4 * e, 4 * e + 4):
                            c, h = n // 2 % 2, n % 2
                            g = G[e % 2][c][0:chunk, h * HALF:(h + 1) * HALF]
                            dve.wait_ge(s["hidden_act"], n + 1)
                            dve.tensor_tensor(g, g, self.bank(2 * (n % 2) + 1)[0:chunk, 0:HALF], ALU.mult).then_inc(s["hidden_used"], 1)
                    if e >= 1:
                        gate(e - 1)

    def first_mixture(self):
        self.norm(self.H[:, :, :], self.X[:, :, :], NT, D, 1e-5)
        self.turn(self.X, self.XT)
        self.project([("t", self.w("m0_r"), self.XT[0:D, 0:L], self.RT[:, :, :], None)])
        self.softmax_block(self.RT[:, :, :], NT, 8)
        self.top_two(self.RT[:, :, :], self.GT[:, :, :], 0.0)
        w1, w2, b2 = self.w("m0_w1"), self.w("m0_w2"), self.w("m0_b2")
        self.mixture(self.H, self.GT, 128, lambda e, c: w1[:, F0 * e + 128 * c:F0 * e + 128 * c + 128],
                     lambda e, c: w2[:, D * (2 * e + c):D * (2 * e + c) + D],
                     lambda e: b2[:, D * e:D * e + D], E0 + 1, E0, False)


    def phase_tables(self):
        s, ph, k, r = self.s, self.w("phases"), self.QT[:, 0:L], self.TRIG
        round_up = 12582912.0
        parts = [6.28125, 0.0019352436065673828, 6.357301884918343e-08]
        with self.block() as block:
            @block.vector
            def _(dve):
                link = self.chain(dve, s["step_dve"])
                link(dve.tensor_scalar(k, ph, 0.15915494309189535, None, ALU.mult))
                link(dve.tensor_scalar(k, k, round_up, None, ALU.add))
                link(dve.tensor_scalar(k, k, -round_up, None, ALU.add))
                link(dve.scalar_tensor_tensor(r, k, -parts[0], ph, ALU.mult, ALU.add))
                link(dve.scalar_tensor_tensor(r, k, -parts[1], r, ALU.mult, ALU.add))
                link(dve.scalar_tensor_tensor(r, k, -parts[2], r, ALU.mult, ALU.add))
                dve.tensor_scalar(r, r, PI_DOWN, -PI_DOWN, ALU.min, ALU.max).then_inc(s["phase_ready"], 1)

            @block.scalar
            def _(act):
                act.wait_ge(s["phase_ready"], 1)
                act.activation(r[0:D, :], r[0:D, :], ACT.Abs).then_inc(s["step_act"], 1)
                act.wait_ge(s["step_act"], 1)
                act.activation(r[0:D, :], r[0:D, :], ACT.Sin, bias=self.w("half_pi")[0:D, :], scale=-1.0).then_inc(s["step_act"], 1)
                act.activation(r[D:128, :], r[D:128, :], ACT.Sin).then_inc(s["step_act"], 1)

    def memory(self):
        s = self.s
        xt1 = self.XT[:, 0:L]
        self.norm(self.H, self.X, NT, D, 1e-5)
        self.turn(self.X, self.XT)
        self.project([("c", self.w("h1_k1"), xt1, self.C1, ACT.Tanh), ("c", self.w("h1_q1"), xt1, self.C2, ACT.Tanh)])
        self.project([("c", self.w("h1_k2"), self.C1, self.KT, ACT.Tanh), ("c", self.w("h1_q2"), self.C2, self.QT, ACT.Tanh)])
        with self.block() as block:
            @block.scalar
            def _(act):
                for u in (self.KT, self.QT):
                    act.activation(u[0:32, 0:L], u[0:32, 0:L], ACT.Abs).then_inc(s["step_act"], 1)
                act.wait_ge(s["step_act"], 2)
                for u in (self.KT, self.QT):
                    act.activation(u[0:32, 0:L], u[0:32, 0:L], ACT.Sin, bias=self.w("half_pi")[0:32, :],
                                   scale=-PI_DOWN).then_inc(s["step_act"], 1)
                    act.activation(u[32:64, 0:L], u[32:64, 0:L], ACT.Sin, scale=PI_DOWN).then_inc(s["step_act"], 1)
        self.project([("t", self.w("h1_vc"), xt1, self.V, None), ("c", self.w("h1_vp"), xt1, self.MV, None),
                      ("c", self.w("h1_g1"), xt1, self.G1, ACT.Relu)])

        def content(dve, link, acc):
            link(dve.tensor_tensor(self.Y, acc, self.w("inv_pos32").unsqueeze(2).broadcast_to((P, NT, D)), ALU.mult))
        M = self.MP
        with self.block() as block:
            @block.vector
            def _(dve):
                link = self.chain(dve, s["step_dve"])
                link(dve.tensor_tensor(M, self.MV, self.TRIG, ALU.mult))
                link(dve.tensor_tensor_scan(self.MS, self.ONES, M, 0.0, ALU.mult, ALU.add))
                link(dve.tensor_tensor(M, self.MS, self.TRIG, ALU.mult))
        self.project([("t", self.w("two_eyes"), M, self.A, None), ("t", self.w("h1_g2"), self.G1, self.GL2, None)])
        self.causal_product(self.QT[0:D, 0:L], self.KT[0:D, 0:L], self.V, False, content)

        def combine(dve, link):
            g = lambda j: self.GL2[:, :, j:j + 1].broadcast_to((P, NT, D))
            link(dve.tensor_tensor(self.A, self.A, self.w("inv_pos").unsqueeze(2).broadcast_to((P, NT, D)), ALU.mult))
            link(dve.tensor_tensor(self.A, self.A, g(0), ALU.mult))
            link(dve.tensor_tensor(self.Y, self.Y, g(1), ALU.mult))
            link(dve.tensor_tensor(self.Y, self.Y, self.A, ALU.add))
        self.softmax_block(self.GL2, NT, 2, after=combine)
        self.norm(self.Y, self.A, NT, D, 1e-5, gamma=self.w("h1_g"), beta=self.w("h1_b"))
        self.turn(self.A, self.C1)
        self.project([("t", self.w("h1_o"), self.C1, self.A, None)])
        with self.block() as block:
            @block.vector
            def _(dve):
                link = self.chain(dve, s["step_dve"])
                link(dve.tensor_tensor(self.H, self.H, self.X, ALU.add))
                link(dve.tensor_tensor(self.H, self.H, self.A, ALU.add))

    def head_inputs(self):
        self.norm(self.H, self.X, NT, D, 1e-5)
        self.turn(self.X, self.XT)
        self.project([("t", self.w("f1_hl"), self.XT[:, 0:L], self.SX, None)])

    def keep_sequence(self, b):
        s = self.s
        with self.block() as block:
            @block.vector
            def _(dve):
                dve.tensor_copy(self.HA[:, bass.ds(b, 1)], self.H.rearrange("p t d -> p (t d)").unsqueeze(1)).then_inc(s["step_dve"], 1)
                dve.tensor_copy(self.RES[:, bass.ds(b, 1)].rearrange("p o t d -> p (o t) d"), self.SX[:, :, bass.ds(b * HD, HD)]).then_inc(s["step_dve"], 1)

    def fetch_sequence(self, b):
        s = self.s
        with self.block() as block:
            @block.vector
            def _(dve):
                dve.tensor_copy(self.H.rearrange("p t d -> p (t d)").unsqueeze(1), self.HA[:, bass.ds(b, 1)]).then_inc(s["step_dve"], 1)

    def expert_heads(self):
        s = self.s
        self.head_inputs()
        HW = self.HW1
        with self.nc.Fori(0, NH) as n:
            with self.block() as block:
                @block.vector
                def _(dve):
                    dve.tensor_copy(HW, self.w("f1_heads")[:, bass.ds(n * 288, 288)]).then_inc(s["step_dve"], 1)
            self.project([("c", HW[:, 0:HD], self.XT[:, 0:L], self.SN, None)])
            sn = self.SN[0:HD, :]
            self.project([("c", HW[0:HD, 16:144], sn, self.QT, None), ("c", HW[0:HD, 144:272], sn, self.KT, None),
                          ("t", HW[0:HD, 272:288], sn, self.VN, None)])
            self.softmax_attention(
                [(self.QT[32 * e:32 * e + HD, :], self.KT[32 * e:32 * e + HD, 0:L], self.VN,
                  lambda t, e=e: (self.QN[:, t, HD * e:HD * e + HD], None)) for e in range(NE)], float(HD) ** 0.5, True)
            with self.block() as block:
                @block.vector
                def _(dve):
                    dve.tensor_copy(self.QKV[:, :, bass.ds(n, 1), :], self.QN.unsqueeze(2)).then_inc(s["step_dve"], 1)
        with self.block() as block:
            @block.vector
            def _(dve):
                link = self.chain(dve, s["step_dve"])
                link(dve.tensor_scalar(self.A, self.SX, 0.0, None, ALU.not_equal))
                for e in range(NE):
                    q = self.QKV.rearrange("p t n (e d) -> p (t n) e d", e=NE)[:, :, e, :]
                    dve.tensor_tensor(q, q, self.A.rearrange("p t (n d) -> p (t n) d", d=HD), ALU.mult).then_inc(s["mask_ready"], 1)
        for g in range(2):
            self.turn(self.QKV[:, :, 2 * g:2 * g + 2, :].rearrange("p t n f -> p t (n f)"), self.QT if g == 0 else self.KT, rows=128)
        gate = self.w("f1_gate")
        self.project([("t", gate[:, 0:8], self.QT, self.GL[:, :, 0:8], None), ("t", gate[:, 8:16], self.KT, self.GL[:, :, 8:16], None)])
        over = lambda a, m: a.unsqueeze(1).broadcast_to((P, m, a.shape[1]))

        def bias(dve, link):
            link(dve.tensor_tensor(self.GL, self.GL, over(self.w("f1_gate_b"), NT), ALU.add))

        def mix(dve, link):
            q = self.QKV.rearrange("p t n (e d) -> p (t n e) d", e=NE)
            g = self.GL.rearrange("p t g -> p (t g)").unsqueeze(2).broadcast_to((P, NT * NH * NE, HD))
            link(dve.tensor_tensor(q, q, g, ALU.mult))
            link(dve.tensor_reduce(self.A.rearrange("p t (n d) -> p (t n) d", d=HD),
                                   self.QKV.rearrange("p t n (e d) -> p (t n) d e", e=NE), AX.X, ALU.add))
            a4 = self.A.rearrange("p t (n d) -> p t n d", d=HD)
            link(dve.tensor_tensor(a4, a4, self.RES.rearrange("p n t d -> p t n d"), ALU.add))
        self.softmax_block(self.GL.rearrange("p t (n e) -> p (t n) e", e=NE), NT * NH, NE, before=bias, after=mix)
        heads = lambda a: a.rearrange("p t (n d) -> p (t n) d", d=HD)
        self.norm(heads(self.A), heads(self.Y), NT * NH, HD, 1e-8, gamma=self.w("f1_g"), beta=self.w("f1_b"))
        self.turn(self.Y, self.C1)
        self.project([("c", self.w("f1_fc1"), self.C1, self.C2, ACT.Relu)])
        with self.block() as block:
            @block.vector
            def _(dve):
                dve.scalar_tensor_tensor(self.C2[0:D, :], self.C1[0:D, :], 0.0, self.C2[0:D, :], ALU.not_equal, ALU.mult)\
                   .then_inc(s["step_dve"], 1)
        self.project([("t", self.w("f1_fc2"), self.C2, self.A, None)])
        with self.block() as block:
            @block.vector
            def _(dve):
                link = self.chain(dve, s["step_dve"])
                link(dve.scalar_tensor_tensor(self.A, self.Y, 0.0, self.A, ALU.not_equal, ALU.mult))
                link(dve.tensor_tensor(self.A, self.A, self.Y, ALU.add))
        self.norm(heads(self.A), heads(self.Y), NT * NH, HD, 1e-8, gamma=self.w("f1_fg"), beta=self.w("f1_fb"))
        self.turn(self.Y, self.C1)
        self.project([("t", self.w("f1_fgate"), self.C1[0:D, :], self.GL2b, None)])

        def out(dve, link):
            g = self.GL2b.rearrange("p t n -> p (t n)").unsqueeze(2).broadcast_to((P, NT * NH, HD))
            link(dve.tensor_tensor(heads(self.Y), heads(self.Y), g, ALU.mult))
            link(dve.tensor_tensor(self.H, self.H, self.Y, ALU.add))
        self.softmax_block(self.GL2b, NT, NH, after=out)


    def plain_attention(self):
        self.norm(self.H, self.X, NT, D, 1e-5)
        self.turn(self.X, self.XT)
        xt = self.XT[0:D, 0:L]
        self.project([("c", self.w("a2_q"), xt, self.QT, None), ("c", self.w("a2_k"), xt, self.KT, None)])
        self.softmax_attention([(self.QT[0:D, :], self.KT[0:D, 0:L], self.X, lambda t: (self.H[:, t, :], self.H[:, t, :]))],
                               float(D) ** -0.5, False)

    def pair_cuts(self):
        s = self.s
        q = [self.PT[:, c, :] for c in range(4)]
        self.project([("c", self.w("pk_q")[:, 128 * c:128 * c + 128], self.XT[0:D, 0:L], q[c], None) for c in range(4)])
        sims = [self.PT[0:P, 4 + i, :] for i in range(3)]
        SIM = self.PT[0:P, 4:7, :].rearrange("p a l -> p (a l)")
        sim = lambda t: SIM[:, 1024 * (t % 2):1024 * (t % 2) + 1024]
        keys = self.w("pk_keys")
        with self.block() as block:
            @block.tensor
            def _(pe):
                for t in range(NT):
                    if t >= 2:
                        pe.wait_ge(s["copied_a"], t - 1)
                    for c in range(4):
                        last = pe.matmul(self.bank(2 * (t % 2) + c // 2)[0:P, 256 * (c % 2):256 * (c % 2) + 256],
                                         q[c][:, P * t:P * t + P], keys[:, 256 * c:256 * c + 256], start=True, stop=True)
                    last.then_inc(s["scores_ready"], 1)

            @block.scalar
            def _(act):
                for t in range(NT):
                    act.wait_ge(s["scores_ready"], t + 1)
                    if t >= 2:
                        act.wait_ge(s["out_done"], t - 1)
                    act.activation(sim(t), self.bank(2 * (t % 2), 2)[0:P, :], ACT.Copy).then_inc(s["copied_a"], 1)

            @block.vector
            def _(dve):
                link = self.chain(dve, s["step_dve"])
                for t in range(NT):
                    dve.wait_ge(s["copied_a"], t + 1)
                    x = lambda g: sim(t)[:, NK * g:NK * g + NK]
                    sides, heads = range(2 * PKH), range(PKH)
                    for g in sides:
                        last = dve.max(self.V16[:, g, 0:8], x(g))
                    link(last)
                    for g in sides:
                        last = dve.match_replace(out=x(g), in_to_replace=self.V16[:, g, 0:8], in_values=x(g), imm_value=LOWEST)
                    link(last)
                    for g in sides:
                        last = dve.max(self.V16[:, g, 8:16], x(g))
                    link(last)
                    for g in sides:
                        last = dve.match_replace(out=x(g), in_to_replace=self.V16[:, g, 8:16], in_values=x(g), imm_value=LOWEST)
                    link(last)
                    link(dve.tensor_reduce(self.V16[:, :, 16], sim(t).rearrange("p (g k) -> p g k", k=NK), AX.X, ALU.max))
                    s0, s1 = self.V16[:, 0:PKH, :], self.V16[:, PKH:, :]
                    at = 0
                    for a, n in RUNS:
                        dve.tensor_tensor(self.CAND[:, :, at:at + n], s0[:, :, a:a + 1].broadcast_to((P, PKH, n)),
                                          s1[:, :, 0:n], ALU.add)
                        at += n
                    for a in (5, 6, 7):
                        dve.tensor_tensor(self.CAND[:, :, at:at + 2], s0[:, :, a:a + 1].broadcast_to((P, PKH, 2)),
                                          s1[:, :, 0:2], ALU.add)
                        at += 2
                    for a in (0, 16):
                        dve.tensor_tensor(self.CAND[:, :, at:at + 1], s0[:, :, a:a + 1], s1[:, :, 16 - a:17 - a], ALU.add)
                        at += 1
                    link(dve.tensor_tensor(self.CAND[:, :, at:at + 8], s0[:, :, 8:16], s1[:, :, 0:1].broadcast_to((P, PKH, 8)), ALU.add))
                    for r in range(3):
                        for h in heads:
                            last = dve.max(self.T24[:, h, 8 * r:8 * r + 8], self.CAND[:, h, :])
                        link(last)
                        if r < 2:
                            for h in heads:
                                last = dve.match_replace(out=self.CAND[:, h, :], in_to_replace=self.T24[:, h, 8 * r:8 * r + 8],
                                                         in_values=self.CAND[:, h, :], imm_value=LOWEST)
                            link(last)
                    cut = self.CUT[:, t, :].unsqueeze(2)
                    link(dve.tensor_tensor(cut, self.T24[:, :, 15:16], self.T24[:, :, 16:17], ALU.add))
                    link(dve.tensor_scalar(cut, cut, 0.5, None, ALU.mult))
                    link(dve.tensor_scalar(self.T24[:, :, 0:1], self.T24[:, :, 0:1], -80.0, None, ALU.add))
                    link(dve.tensor_tensor(cut, cut, self.T24[:, :, 0:1], ALU.max))
                    dve.tensor_scalar(cut, cut, -1.0, None, ALU.mult).then_inc(s["out_done"], 1)

    def load_head(self, sp, h, i, sem):
        sp.dma_start(self.PAIRS[i], self.dram["pairs"][bass.ds(h, 1)].rearrange("o p c -> (o p) c")).then_inc(sem, 16)
        sp.dma_start(self.TABLES[i], self.dram["tables"][bass.ds(h, 1)].rearrange("o p c -> (o p) c")).then_inc(sem, 16)
        sp.dma_start(self.HWH[i], self.dram["head_weights"][bass.ds(h, 1)].rearrange("o p c -> (o p) c")).then_inc(sem, 16)

    def key_head(self, h, nxt, i):
        s = self.s
        pairs, tables, hw = self.PAIRS[i], self.TABLES[i], self.HWH[i]
        QM = self.QT
        self.project([("c", hw[0:D, 0:D], self.XT[0:D, 0:L], QM, None)])
        with self.block() as block:
            @block.vector
            def _(dve):
                dve.tensor_copy(self.CUTH.unsqueeze(2), self.CUT[:, :, bass.ds(h, 1)]).then_inc(s["mask_ready"], 1)

            @block.tensor
            def _(pe):
                pe.wait_ge(s["mask_ready"], 1)
                for t in range(NT):
                    last = pe.matmul(self.bank(t // 4)[D:D + 1, P * (t % 4):P * (t % 4) + P], self.CUTH[:, t:t + 1],
                                     self.w("ident")[0:P, 0:P], start=True, stop=True)
                last.then_inc(s["turned"], 1)

            @block.scalar
            def _(act):
                act.wait_ge(s["turned"], 1)
                act.activation(QM[D:D + 1, 0:4 * P], self.bank(0)[D:D + 1, 0:4 * P], ACT.Copy).then_inc(s["copied_a"], 1)
                act.activation(QM[D:D + 1, 4 * P:L], self.bank(1)[D:D + 1, 0:3 * P], ACT.Copy).then_inc(s["copied_a"], 1)
        NC = NK // 2
        GBF = self.GB.rearrange("p a l -> p (a l)")
        E = lambda n: GBF[:, HALF * (n % 4):HALF * (n % 4) + HALF]
        PK = lambda n: GBF[:, HALF * (4 + n % 4):HALF * (4 + n % 4) + HALF]
        Z = lambda n: self.bank(n % 4)[0:128, 0:HALF]
        ahead = 3
        cols = lambda half: slice(half * HALF, half * HALF + HALF)
        with self.block() as block:
            @block.sync
            def _(sp):
                self.load_head(sp, nxt, 1 - i, s["loaded"])
                sp.wait_ge(s["loaded"], 48)

            @block.tensor
            def _(pe):
                for n in range(2 * NC + ahead):
                    if n < 2 * NC:
                        c, half = n % NC, n // NC
                        if n >= 4:
                            pe.wait_ge(s["picked"], n - 3)
                        pe.matmul(Z(n), pairs[:, 128 * c:128 * c + 128], QM[0:D + 1, cols(half)],
                                  start=True, stop=True).then_inc(s["dense_ready"], 1)
                    m = n - ahead
                    if m >= 0:
                        c, half = m % NC, m // NC
                        pe.wait_ge(s["picked"], m + 1)
                        pe.matmul(self.bank(4 + half)[0:128, 0:HALF], tables[:, 128 * c:128 * c + 128], PK(m),
                                  start=(c == 0), stop=(c == NC - 1)).then_inc(s["pv_ready"], 1)
                for half in range(2):
                    pe.wait_ge(s["sum_ready"], NC * (half + 1))
                    pe.matmul(self.bank(6 + half)[0:128, 0:HALF], self.ONE, self.ZS[:, cols(half)],
                              start=True, stop=True).then_inc(s["kv_ready"], 1)

            @block.scalar
            def _(act):
                for n in range(2 * NC):
                    act.wait_ge(s["dense_ready"], n + 1)
                    if n >= 4:
                        act.wait_ge(s["picked"], n - 3)
                    act.activation(E(n), Z(n), ACT.Exp).then_inc(s["exp_ready"], 1)

            @block.vector
            def _(dve):
                link = self.chain(dve, s["step_dve"])
                for n in range(2 * NC):
                    dve.wait_ge(s["exp_ready"], n + 1)
                    if n >= 4:
                        dve.wait_ge(s["pv_ready"], n - 3)
                        dve.wait_ge(s["sum_ready"], n - 3)
                    dve.scalar_tensor_tensor(PK(n), Z(n), 0.0, E(n), ALU.is_ge, ALU.mult).then_inc(s["picked"], 1)
                for half in range(2):
                    dve.wait_ge(s["kv_ready"], half + 1)
                    link(dve.reciprocal(self.ZS[:, cols(half)], self.bank(6 + half)[0:128, 0:HALF]))
                    link(dve.tensor_tensor(self.KVT[:, cols(half)], self.bank(4 + half)[0:128, 0:HALF], self.ZS[:, cols(half)], ALU.mult))

            @block.gpsimd
            def _(pool):
                for n in range(2 * NC):
                    c, half = n % NC, n // NC
                    pool.wait_ge(s["picked"], n + 1)
                    z = self.ZS[:, cols(half)]
                    if c == 0:
                        pool.tensor_copy(z, PK(n)).then_inc(s["sum_ready"], 1)
                    else:
                        pool.wait_ge(s["sum_ready"], n)
                        pool.tensor_tensor(z, z, PK(n), ALU.add).then_inc(s["sum_ready"], 1)
        self.project([("c", hw[0:D, D:2 * D], self.XT[0:D, 0:L], self.QT, None),
                      ("t", hw[D:128, 2 * D:3 * D], self.KVT[D:128, :], self.V, None)])
        self.softmax_attention([(self.QT[0:D, :], self.KVT[0:D, :], self.V, lambda t: (self.H[:, t, :], self.H[:, t, :]))],
                               float(D) ** -0.5, True)

    def product_keys(self):
        self.norm(self.H, self.X, NT, D, 1e-5)
        self.turn(self.X, self.XT)
        self.pair_cuts()
        with self.nc.Fori(0, PKH // 2) as g:
            self.key_head(g * 2, g * 2 + 1, 0)
            self.key_head(g * 2 + 1, g * 2 + 2, 1)

    def inner_layer(self, l):
        s, W = self.s, self.LW
        dh = D // 8
        scale = float(dh) ** -0.25
        with self.block() as block:
            @block.sync
            def _(sp):
                sp.dma_start(W, self.dram["layers"][bass.ds(l, 1)].rearrange("o p c -> (o p) c")).then_inc(s["loaded"], 16)
                sp.wait_ge(s["loaded"], 16)
        self.norm(self.R, self.X, NT, D, 1e-5, gamma=W[0:P, 704:768], beta=W[0:P, 768:832])
        self.turn(self.X, self.XT)
        xt = self.XT[0:D, 0:L]
        self.project([("t", W[0:D, 0:64], xt, self.A, None), ("c", W[0:D, 64:128], xt, self.KT, None),
                      ("t", W[0:D, 128:192], xt, self.V, None)])
        self.softmax_block(self.A.rearrange("p t (h d) -> p (t h) d", d=dh), NT * 8, dh, scale=scale)
        self.turn(self.A, self.C1)
        KM, KT = self.KM, self.KT[0:D, 0:L]
        with self.block() as block:
            @block.vector
            def _(dve):
                link = self.chain(dve, s["step_dve"])
                link(dve.tensor_reduce(KM[:, 0:1], KT, AX.X, ALU.max))
                dve.tensor_scalar(KM[:, 1:2], KM[:, 0:1], -scale, None, ALU.mult).then_inc(s["max_ready"], 1)
                dve.wait_ge(s["exp_ready"], 1)
                link(dve.reciprocal(KM[:, 3:4], KM[:, 2:3]))
                dve.wait_ge(s["turned"], 1)
                dve.tensor_copy(self.Y, self.bank(0)[0:P, 0:NT * D].rearrange("p (t d) -> p t d", d=D)).then_inc(s["copied_d"], 1)
                dve.wait_ge(s["prod_ready"], 1)
                dve.tensor_tensor(self.CT, self.bank(1)[0:D, 0:D], self.w("blocks8"), ALU.mult).then_inc(s["mask_ready"], 1)
                dve.wait_ge(s["prod_ready"], 2)
                dve.tensor_scalar(self.CW[0:D, :], self.bank(2)[0:D, 0:D], KM[:, 3:4], None, ALU.mult).then_inc(s["out_done"], 1)
                dve.tensor_copy(self.CW[D:D + 1, :], W[D:D + 1, 192:256]).then_inc(s["out_done"], 1)

            @block.scalar
            def _(act):
                act.wait_ge(s["max_ready"], 1)
                act.activation(KT, KT, ACT.Exp, bias=KM[:, 1:2], scale=scale, accum_out=KM[:, 2:3]).then_inc(s["exp_ready"], 1)

            @block.tensor
            def _(pe):
                pe.wait_ge(s["exp_ready"], 1)
                for t in range(NT):
                    last = pe.transpose(self.bank(0)[0:P, D * t:D * t + D], KT[:, P * t:P * t + P], self.w("ident")[0:D, 0:D])
                last.then_inc(s["turned"], 1)
                pe.wait_ge(s["copied_d"], 1)
                for t in range(NT):
                    last = pe.matmul(self.bank(1)[0:D, 0:D], self.V[:, t, :], self.Y[:, t, :], start=(t == 0), stop=(t == NT - 1))
                last.then_inc(s["prod_ready"], 1)
                pe.wait_ge(s["mask_ready"], 1)
                pe.matmul(self.bank(2)[0:D, 0:D], self.CT, W[0:D, 192:256], start=True, stop=True).then_inc(s["prod_ready"], 1)
        self.project([("t", self.CW, self.C1, self.A, None)])
        self.add(self.R, self.R, self.A)
        self.norm(self.R, self.X, NT, D, 1e-5, gamma=W[0:P, 832:896], beta=W[0:P, 896:960])
        self.turn(self.X, self.XT)
        self.mixture(self.R, None, 128, lambda e, c: W[0:D + 1, 256 + 128 * c:384 + 128 * c],
                     lambda e, c: W[:, 512 + D * c:576 + D * c], lambda e: W[0:1, 640:704], 1, 0, False)

    def inner_transformer(self):
        self.norm(self.H, self.R, NT, D, 1e-5)
        with self.nc.Fori(0, DEPTH) as l:
            self.inner_layer(l)
        self.add(self.H, self.H, self.R)

    def last_part(self):
        s = self.s
        self.norm(self.H, self.R, NT, D, 1e-5)
        self.norm(self.R, self.X, NT, D, 1e-6, center=False, gamma=self.w("f3_1"))
        self.turn(self.X, self.XT)
        xt = self.XT[0:D, 0:L]
        qs, ks = self.GB[:, 0, :], self.GB[:, 1, :]
        self.project([("c", self.w("f3_q"), xt, self.QT, None), ("c", self.w("f3_qs"), xt, qs, None),
                      ("c", self.w("f3_k"), xt, self.KT, None), ("c", self.w("f3_ks"), xt, ks, None),
                      ("t", self.w("f3_v"), xt, self.V[:, :, 0:32], None)])
        with self.block() as block:
            @block.vector
            def _(dve):
                link = self.chain(dve, s["step_dve"])
                for x, sw in ((self.QT[:, 0:L], qs), (self.KT[:, 0:L], ks)):
                    link(dve.tensor_tensor(x, x, self.w("cos4"), ALU.mult))
                    link(dve.tensor_tensor(sw, sw, self.w("sin4"), ALU.mult))
                    link(dve.tensor_tensor(x, x, sw, ALU.add))
        self.softmax_attention(
            [(self.QT[32 * h:32 * h + HD, :], self.KT[32 * h:32 * h + HD, 0:L], self.V[:, :, HD * (h // 2):HD * (h // 2) + HD],
              lambda t, h=h: (self.A[:, t, HD * h:HD * h + HD], None)) for h in range(NH)], float(HD) ** -0.5, True)
        self.turn(self.A, self.C1)
        self.project([("t", self.w("f3_o"), self.C1[0:D, :], self.A, None)])
        self.add(self.R, self.R, self.A)
        self.norm(self.R, self.X, NT, D, 1e-6, center=False, gamma=self.w("f3_2"))
        self.turn(self.X, self.XT)
        self.project([("t", self.w("f3_r"), self.XT[0:D, 0:L], self.RT, None)])
        self.softmax_block(self.RT, NT, 8)
        self.top_two(self.RT, self.GT, 1e-9)
        w1, w3, w2, ch = self.w("f3_w1"), self.w("f3_w3"), self.w("f3_w2"), F3 // 2
        up = lambda w, e, c: w[:, F3 * e + ch * c:F3 * e + ch * c + ch]
        self.mixture(self.R, self.GT, ch, lambda e, c: (up(w1, e, c), up(w3, e, c)),
                     lambda e, c: w2[:, D * (2 * e + c):D * (2 * e + c) + D], None, E3, None, True)
        self.add(self.H, self.H, self.R)


def build(nc, where, dram, out, stages=99, dbg=None):
    ctx = ExitStack()
    with ctx:
        t = Tower(nc, ctx, where, dram)
        s = t.s
        t.VO = t.sb("a0_vo", [D, D])
        t.RT = t.sb("router", [P, NT, 8])
        t.GT = t.sb("gates", [P, NT, 8])
        t.TOP = t.sb("top", [P, 8 * NT])
        t.TOPF = t.sb("top_at", [P, 8 * NT])
        t.IDX = t.sb("top_index", [P, 8 * NT], U32)
        t.GB = t.sb("hidden", [128, 4, L])
        t.HA = t.sb("h_all", [P, NSEQ, NT * D])
        STREAM = NK // 2 * 128
        t.PAIRS = [t.sb(f"pairs_{i}", [2 * PKD + 1, STREAM]) for i in range(2)]
        t.TABLES = [t.sb(f"tables_{i}", [128, STREAM]) for i in range(2)]
        t.X9 = t.TABLES[0][0:P, 0:NT * WIN * D].rearrange("p (t c) -> p t c", t=NT)
        t.TRIG, t.MP, t.MV, t.MS, t.ONES = (t.TABLES[1][:, i * L:(i + 1) * L] for i in range(5))
        t.G1 = t.PAIRS[0][0:HD + 1, 0:L]
        t.ONE = t.sb("ones_square", [128, 128])
        t.HWH = [t.sb(f"key_head_weights_{i}", [128, 3 * D]) for i in range(2)]
        t.V16 = t.sb("key_scores_top", [P, 2 * PKH, 17])
        t.CAND = t.sb("pair_scores", [P, PKH, PAIRED])
        t.T24 = t.sb("pair_scores_top", [P, PKH, 24])
        t.CUT = t.sb("pair_cut", [P, NT, PKH])
        t.CUTH = t.sb("pair_cut_head", [P, NT])
        t.ZS = t.sb("pair_sums", [128, L])
        t.KVT = t.sb("picked_kv", [128, L])
        t.LW = t.sb("layer_weights", [128, 960])
        t.R = t.sb("inner_stream", [P, NT, D])
        t.KM = t.sb("key_stats", [D, 4])
        t.CT = t.sb("context_t", [D, D])
        t.CW = t.sb("context_out", [D + 1, D])
        t.C1 = t.sb("hidden_1", [D + 1, L])
        t.C2 = t.sb("hidden_2", [D + 1, L])
        t.GL2 = t.sb("gate_two", [P, NT, 2])
        t.GL2b = t.sb("gate_heads", [P, NT, NH])
        t.GL = t.sb("gate_experts", [P, NT, NH * NE])
        t.SX = t.sb("head_inputs", [P, NT, D])
        t.RES = t.sb("head_residuals", [P, NH, NT, HD])
        t.HW1 = t.sb("head_weights", [D + 1, 288])
        t.SN = t.sb("head_input_t", [HD, L])
        t.VN = t.sb("head_values", [P, NT, HD])
        t.QN = t.sb("head_out", [P, NT, D])
        t.QKV = t.PT.rearrange("p a l -> p (a l)")[0:P, 3 * L:3 * L + NT * NH * D].rearrange("p (t n f) -> p t n f", t=NT, n=NH)
        with t.block() as block:
            @block.sync
            def _(sp):
                first = dram["pack_0"].shape[1]
                sp.dma_start(t.W[:, 0:first], dram["pack_0"]).then_inc(s["loaded"], 16)
                sp.dma_start(t.W[:, first:first + dram["pack_1"].shape[1]], dram["pack_1"]).then_inc(s["loaded"], 16)

            @block.gpsimd
            def _(pool):
                link = t.chain(pool, s["step_pool"])
                for rows in (t.XT[D:D + 1, :], t.C1[D:D + 1, :], t.C2[D:D + 1, :], t.G1, t.ONES, t.ONE):
                    link(pool.memset(rows, 1.0))

            @block.vector
            def _(dve):
                dve.wait_ge(s["loaded"], 32)
                dve.tensor_copy(t.identb[:, :], t.w("ident")[0:P, 0:P]).then_inc(s["step_dve"], 1)
                dve.tensor_copy(t.laterb[:, :], t.w("later")).then_inc(s["step_dve"], 1)
                dve.wait_ge(s["prod_ready"], 1)
                dve.tensor_copy(t.VO[:, :], t.bank(0)[0:D, 0:D]).then_inc(s["step_dve"], 1)

            @block.tensor
            def _(pe):
                pe.wait_ge(s["loaded"], 32)
                pe.matmul(t.bank(0)[0:D, 0:D], t.w("a0_v"), t.w("a0_o"), start=True, stop=True).then_inc(s["prod_ready"], 1)

        t.phase_tables()

        def store(b):
            with t.block() as block:
                @block.sync
                def _(sp):
                    sp.dma_start(out[bass.ds(b, 1)].rearrange("o (t p) d -> (o p) t d", p=P), t.H[:, :, :]).then_inc(s["stored"], 16)
                    sp.wait_ge(s["stored"], 16)

        with nc.Fori(0, NSEQ) as b:
            t.window_pool(b)
            if stages >= 2:
                t.relu_attention()
            if stages >= 3:
                t.first_mixture()
            if stages >= 4:
                t.memory()
            if stages >= 5:
                t.head_inputs()
                t.keep_sequence(b)
            else:
                store(b)
        if stages >= 5:
            with t.block() as block:
                @block.sync
                def _(sp):
                    first = dram["pack_0"].shape[1]
                    sp.dma_start(t.W[:, first:first + dram["pack_2"].shape[1]], dram["pack_2"]).then_inc(s["loaded"], 16)
                    t.load_head(sp, 0, 0, s["loaded"])
                    sp.wait_ge(s["loaded"], 64)
            with nc.Fori(0, NSEQ) as b:
                t.fetch_sequence(b)
                t.expert_heads()
                if stages >= 6:
                    t.plain_attention()
                if stages >= 7:
                    t.product_keys()
                if stages >= 8:
                    t.inner_transformer()
                if stages >= 9:
                    t.last_part()
                store(b)


def kernel(**inputs):
    import concourse.bacc as bacc
    from concourse.bass_utils import run_bass_kernel_spmd

    where, arrays = layout(inputs)
    nc = bacc.Bacc("TRN2", target_bir_lowering=False, num_devices=1)
    dram = {k: nc.dram_tensor(f"in_{k}", a.shape, F32, kind="ExternalInput").ap() for k, a in arrays.items()}
    out = nc.dram_tensor("out", (NSEQ, L, D), F32, kind="ExternalOutput").ap()
    build(nc, where, dram, out)
    r = run_bass_kernel_spmd(nc, [{f"in_{k}": a for k, a in arrays.items()}], core_ids=[0])
    return r.results[0]["out"]
```

```python
import numpy as np
from contextlib import ExitStack, contextmanager

import concourse.bass as bass
from concourse import mybir

F32 = mybir.dt.float32
BF16 = mybir.dt.bfloat16
I32 = mybir.dt.int32
U32 = mybir.dt.uint32
ALU = mybir.AluOpType
ACT = mybir.ActivationFunctionType
AX = mybir.AxisListType

NSEQ, LIN, WIN, D = 4, 750, 9, 64
L = LIN - WIN + 1
P, NT = 106, 7
HALF = L // 2
assert P * NT == L
NEG = -1e30
E0, F0 = 8, 256
NH, NE, HD = 4, 4, 16
PKH, PKD, NK = 8, 32, 64
E3, F3 = 8, 170
DEPTH = 4
RUNS = [(0, 16), (1, 8), (2, 5), (3, 4), (4, 3)]
PAIRED = 52
LOWEST = -3.0e38
PI_DOWN = 3.1415925


def _pad(a, rows):
    out = np.zeros((rows,) + a.shape[1:], np.float32)
    out[:a.shape[0]] = a
    return out


def _spread(a):
    rows, heads = a.shape[0], a.shape[1] // HD
    out = np.zeros((rows, heads, 32), np.float32)
    out[:, :, :HD] = a.reshape(rows, heads, HD)
    return out.reshape(rows, heads * 32)


def _rows(v, n=P):
    return np.ascontiguousarray(np.broadcast_to(np.asarray(v).reshape(1, -1), (n, np.asarray(v).size)))


def _block_diagonal(blocks):
    r, c = blocks[0].shape
    out = np.zeros((r * len(blocks), c * len(blocks)), np.float32)
    for i, b in enumerate(blocks):
        out[i * r:(i + 1) * r, i * c:(i + 1) * c] = b
    return out


def constants():
    pos = np.arange(L)
    tiles = lambda v: v.reshape(NT, P).T.astype(np.float32)
    k, q = np.meshgrid(np.arange(P), np.arange(P), indexing="ij")
    inv = 1.0 / 10000.0 ** (np.arange(0, HD, 2, dtype=np.float32) / HD)
    f = np.outer(np.arange(L, dtype=np.float32), inv)
    f = np.concatenate([f, f], -1)
    sign = np.where(np.arange(HD) < HD // 2, -1.0, 1.0)
    four = lambda t: np.ascontiguousarray(_spread(np.tile(t, (1, 4))).T).astype(np.float32)
    return {
        "ident": np.eye(128, dtype=np.float32),
        "later": np.where(q > k, NEG, 0.0).astype(np.float32),
        "keep_t": (q >= k).astype(np.float32),
        "inv_row": tiles(1.0 / np.maximum(pos.astype(np.float32), 1.0)),
        "inv_pos": tiles(1.0 / np.sqrt((pos + 1).astype(np.float32))),
        "inv_pos32": tiles(1.0 / np.sqrt(((pos + 1) * 32).astype(np.float32))),
        "ones": np.ones((1, L), np.float32),
        "half_pi": np.full((128, 1), np.pi / 2, np.float32),
        "experts": _rows(np.tile(np.arange(8, dtype=np.float32), NT)),
        "two_eyes": np.concatenate([np.eye(64), np.eye(64)]).astype(np.float32),
        "four_eyes": np.tile(np.eye(32, HD), (4, 1)).astype(np.float32),
        "blocks8": np.kron(np.eye(8), np.ones((8, 8))).astype(np.float32),
        "cos4": four(np.cos(f)),
        "sin4": four(np.sin(f) * sign),
    }


def layout(i):
    i = {k: np.asarray(v) for k, v in i.items()}
    cat = np.concatenate
    aug = lambda w, b: cat([w, b.reshape(1, -1)], 0)
    w = dict(constants())
    w["tok_q"] = aug(i["L0_tok_W_qry"], i["L0_tok_b"])
    w["tok_k"] = i["L0_tok_W_key"]
    w["tok_v"] = i["L0_tok_v"].reshape(D, 1)
    w["a0_q"], w["a0_k"], w["a0_v"], w["a0_o"] = i["L0_attn_Wq"].T, i["L0_attn_Wk"].T, i["L0_attn_Wv"], i["L0_attn_Wo"].T
    w["m0_r"] = i["L0_ffn_Wr"]
    w1 = cat([i["L0_ffn_W1p"], i["L0_ffn_W1s"][None]], 0)
    b1 = cat([i["L0_ffn_b1p"], i["L0_ffn_b1s"][None]], 0)
    w["m0_w1"] = cat([w1, b1[:, None]], 1).transpose(1, 0, 2).reshape(D + 1, -1)
    w2 = cat([i["L0_ffn_W2p"], i["L0_ffn_W2s"][None]], 0)
    w["m0_w2"] = w2.reshape(E0 + 1, 2, 128, D).transpose(2, 0, 1, 3).reshape(128, -1)
    w["m0_b2"] = cat([i["L0_ffn_b2p"], i["L0_ffn_b2s"][None]], 0)
    for n in "kq":
        w[f"h1_{n}1"] = aug(i[f"L1_attn_W{n}1"], i[f"L1_attn_b{n}1"])
        one = aug(i[f"L1_attn_W{n}2"], i[f"L1_attn_b{n}2"])
        w[f"h1_{n}2"] = cat([one, one], 1)
    w["h1_vc"] = aug(i["L1_attn_Wvc"], i["L1_attn_bvc"])
    vp = aug(i["L1_attn_Wvp"], i["L1_attn_bvp"])
    w["h1_vp"] = cat([vp, vp], 1)
    w["h1_g1"] = aug(i["L1_attn_Wg1"], i["L1_attn_bg1"])
    w["h1_g2"] = aug(i["L1_attn_Wg2"], i["L1_attn_bg2"])
    w["h1_g"], w["h1_b"] = _rows(i["L1_attn_ln_g"]), _rows(i["L1_attn_ln_b"])
    w["h1_o"] = aug(i["L1_attn_Wo"], i["L1_attn_bo"])
    ph = i["L1_attn_base_phases"][:L].T
    w["phases"] = cat([ph, ph], 0)
    hl = aug(i["L1_ffn_hl_w"].reshape(D, D).T, i["L1_ffn_hl_b"])
    w["f1_hl"] = hl
    heads = []
    for n in range(NH):
        q4 = _spread(cat([i["L1_ffn_wq"][n, e].T for e in range(NE)], 1))
        k4 = _spread(np.tile(i["L1_ffn_wk"][n].T, (1, NE)))
        own = np.zeros((D, 2 * 128 + 32), np.float32)
        own[HD * n:HD * n + HD, :2 * 128 + HD] = cat([q4, k4, i["L1_ffn_wv"][n].T], 1)
        heads.append(own)
    w["f1_heads"] = cat(heads, 1)
    gw = [i["L1_ffn_gate_w"][n].T for n in range(NH)]
    w["f1_gate"] = cat([_block_diagonal(gw[:2]), _block_diagonal(gw[2:])], 1)
    w["f1_gate_b"] = _rows(i["L1_ffn_gate_b"])
    w["f1_g"], w["f1_b"] = _rows(i["L1_ffn_ln_g"]), _rows(i["L1_ffn_ln_b"])
    w["f1_fg"], w["f1_fb"] = _rows(i["L1_ffn_fnorm_g"]), _rows(i["L1_ffn_fnorm_b"])
    for n in "12":
        w[f"f1_fc{n}"] = aug(_block_diagonal([i[f"L1_ffn_fc{n}_w"].T] * NH), np.tile(i[f"L1_ffn_fc{n}_b"], NH))
    w["f1_fgate"] = i["L1_ffn_fgate_w"].T
    w["a2_q"], w["a2_k"] = i["L2_attn_Wq"].T, i["L2_attn_Wk"].T
    pkq, keys = i["L2_ffn_Wq_pk"], i["L2_ffn_pk_keys"]
    w["pk_q"] = pkq
    w["pk_keys"] = cat([_block_diagonal([keys[p, :, h].T for h in range(4 * g, 4 * g + 4)]) for p in range(2) for g in range(2)], 1)
    w["f3_1"], w["f3_2"] = _rows(i["L3_ffn_ln1_w"]), _rows(i["L3_ffn_ln2_w"])
    swap = (np.arange(HD) + HD // 2) % HD
    wq = i["L3_ffn_wq"].T.reshape(D, NH, HD)
    wk = np.repeat(i["L3_ffn_wk"].T.reshape(D, NH // 2, HD), 2, 1)
    for name, m in (("q", wq), ("k", wk)):
        w[f"f3_{name}"] = _spread(m.reshape(D, -1))
        w[f"f3_{name}s"] = _spread(m[:, :, swap].reshape(D, -1))
    w["f3_v"] = i["L3_ffn_wv"].T
    w["f3_o"] = i["L3_ffn_wo"].T
    w["f3_r"] = i["L3_ffn_router_w"].T
    w["f3_w1"] = i["L3_ffn_w1"].transpose(2, 0, 1).reshape(D, -1)
    w["f3_w3"] = i["L3_ffn_w3"].transpose(2, 0, 1).reshape(D, -1)
    w["f3_w2"] = i["L3_ffn_w2"].transpose(0, 2, 1).reshape(E3, 2, F3 // 2, D).transpose(2, 0, 1, 3).reshape(F3 // 2, -1)
    loop_of = lambda k: (1 if k[:3] in ("tok", "a0_", "m0_", "h1_", "pha") else
                         2 if k[:3] in ("a2_", "pk_", "f3_") or k in ("f1_heads", "f1_gate", "cos4", "sin4") else 0)
    where, packs, shared = {}, [], 0
    for part in range(3):
        names = [k for k in w if loop_of(k) == part]
        at = 0
        pack = np.zeros((128, sum(w[k].shape[1] for k in names)), np.float32)
        for k in names:
            r, c = w[k].shape
            pack[:r, at:at + c] = w[k]
            where[k] = (r, shared + at, c)
            at += c
        packs.append(pack)
        shared = packs[0].shape[1]
    pq = pkq.reshape(D, 2, PKH, PKD)
    hw = np.zeros((PKH, 128, 7 * D), np.float32)
    for h in range(PKH):
        hw[h, :D, :D] = i["L2_ffn_Wq"][:, h * D:h * D + D]
        hw[h, :D, D:2 * D] = pq[:, :, h].reshape(D, D)
        hw[h, D:, 2 * D:3 * D] = i["L2_ffn_Wo"][h * D:h * D + D]
        hw[h, D:D + PKD, 3 * D:4 * D] = keys[0, :, h].T
        hw[h, D + PKD:, 4 * D:5 * D] = keys[1, :, h].T
        hw[h, h, 5 * D:6 * D] = 1.0
    kv = cat([i["L2_ffn_keys_table"], i["L2_ffn_values_table"]], 1).reshape(PKH, NK, NK // 2, 2, 2 * D)
    tables = np.ascontiguousarray(kv.transpose(0, 3, 1, 2, 4)).reshape(PKH, 128, (NK // 2) * 2 * D)
    wrap = lambda a: cat([a, a[:2]], 0)
    lw = np.zeros((DEPTH, 128, 3 * D + D + 4 * D + 2 * D + D + 4 * D), np.float32)
    for l in range(DEPTH):
        at = 0
        for a in (i["L3_attn_Wq"][l], i["L3_attn_Wk"][l], i["L3_attn_Wv"][l], aug(i["L3_attn_Wo"][l], i["L3_attn_bo"][l]),
                  aug(i["L3_attn_W1"][l], i["L3_attn_b1"][l]),
                  i["L3_attn_W2"][l].reshape(2, 128, D).transpose(1, 0, 2).reshape(128, -1), aug(np.zeros((D, D), np.float32), i["L3_attn_b2"][l]),
                  _rows(i["L3_attn_ln1_g"][l]), _rows(i["L3_attn_ln1_b"][l]), _rows(i["L3_attn_ln2_g"][l]), _rows(i["L3_attn_ln2_b"][l])):
            lw[l, :a.shape[0], at:at + a.shape[1]] = a
            at += a.shape[1]
    return where, {"x": np.ascontiguousarray(i["x"]), "pack_0": packs[0], "pack_1": packs[1], "pack_2": packs[2], "head_weights": wrap(hw),
                   "tables": wrap(tables), "layers": lw}


SEMS = ["step_dve", "step_pool", "step_act", "loaded", "loaded_b", "stored", "var_ready", "std_ready", "turned", "copied_a", "copied_d",
        "scores_ready", "max_ready", "probs_ready", "probs_turned", "turned_a", "turned_d", "pv_ready", "out_done",
        "hidden_ready", "hidden_act", "hidden_used", "experts_out", "gated", "prod_ready", "prod_used", "sum_ready",
        "tanh_ready", "phase_ready", "feat_ready", "mask_ready", "value_ready", "dense_ready", "exp_ready", "picked",
        "kv_ready", "kv_done"]


class Tower:

    def __init__(self, nc, ctx, where, dram):
        self.nc, self.ctx, self.where, self.dram = nc, ctx, where, dram
        self.s = {n: ctx.enter_context(nc.semaphore(n)) for n in SEMS}
        self.nums = [s.num for s in self.s.values()]
        self.columns = max(o + c for _, o, c in where.values())
        self.W = self.sb("weights", [128, self.columns])
        self.PS = ctx.enter_context(nc.psum_tensor("psum", [128, 8 * 512], F32))
        self.H = self.sb("h", [P, NT, D])
        self.X = self.sb("xn", [P, NT, D])
        self.XT = self.sb("xt", [128, LIN])
        self.QT = self.sb("qt", [128, LIN])
        self.KT = self.sb("kt", [128, LIN])
        self.V = self.sb("v", [P, NT, D])
        self.Y = self.sb("y", [P, NT, D])
        self.A = self.sb("a", [P, NT, D])
        self.SQ = self.sb("sq", [P, NT, D])
        self.ST = self.sb("stat", [P, 128])
        self.ST2 = self.sb("stat2", [P, 128])
        self.PR = self.sb("probs", [P, 2, L])
        self.PT = self.sb("probs_t", [128, NT, L])
        self.NM = self.sb("neg_max", [P, 8])
        self.RS = self.sb("row_sum", [P, 16])
        self.OTS = self.sb("out_turned", [128, 2, P])
        self.identb = self.sb("ident_bf16", [P, P], BF16)
        self.laterb = self.sb("later_bf16", [P, P], BF16)

    def sb(self, name, shape, dt=F32):
        return self.ctx.enter_context(self.nc.sbuf_tensor(name, shape, dt))[tuple(slice(0, n) for n in shape)]

    def w(self, name):
        r, o, c = self.where[name]
        return self.W[0:r, o:o + c]

    def wx(self, name):
        _, o, c = self.where[name]
        return self.W[:, o:o + c]

    def bank(self, n, m=1):
        return self.PS[:, 512 * n:512 * (n + m)]

    @contextmanager
    def block(self):
        with self.nc.Block() as block:
            yield block
        with self.nc.Block() as block:
            @block.gpsimd
            def _(pool):
                pool.sem_clear(range(min(self.nums), max(self.nums) + 1))

    def chain(self, engine, sem):
        count = [0]

        def link(ins):
            count[0] += 1
            ins.then_inc(sem, 1)
            engine.wait_ge(sem, count[0])
        return link

    def norm(self, src, dst, groups, width, eps, center=True, gamma=None, beta=None):
        s, nc = self.s, self.nc
        stat, sq = self.ST[:, 0:groups], self.SQ[:, :, :].rearrange("p t d -> p (t d)").rearrange("p (g w) -> p g w", w=width)
        wide = lambda a: a.unsqueeze(2).broadcast_to((P, groups, width))
        over = lambda a: a.unsqueeze(1).broadcast_to((P, groups, width))
        with self.block() as block:
            @block.vector
            def _(dve):
                link = self.chain(dve, s["step_dve"])
                at = src
                if center:
                    link(dve.tensor_reduce(stat, src, AX.X, ALU.add))
                    link(dve.tensor_scalar(stat, stat, 1.0 / width, None, ALU.mult))
                    link(dve.tensor_tensor(dst, src, wide(stat), ALU.subtract))
                    at = dst
                link(dve.tensor_tensor(sq, at, at, ALU.mult))
                link(dve.tensor_reduce(stat, sq, AX.X, ALU.add))
                dve.tensor_scalar(stat, stat, 1.0 / width, eps, ALU.mult, ALU.add).then_inc(s["var_ready"], 1)
                dve.wait_ge(s["std_ready"], 1)
                link(dve.reciprocal(stat, stat))
                link(dve.tensor_tensor(dst, at, wide(stat), ALU.mult))
                if gamma is not None:
                    link(dve.tensor_tensor(dst, dst, over(gamma), ALU.mult))
                if beta is not None:
                    link(dve.tensor_tensor(dst, dst, over(beta), ALU.add))

            @block.scalar
            def _(act):
                act.wait_ge(s["var_ready"], 1)
                act.activation(stat, stat, ACT.Sqrt).then_inc(s["std_ready"], 1)

    def turn(self, src, dst, rows=D):
        s = self.s
        with self.block() as block:
            @block.tensor
            def _(pe):
                for t in range(NT):
                    out = self.bank(t // 4)[0:rows, P * (t % 4):P * (t % 4) + P]
                    pe.transpose(out, src[:, t, :], self.w("ident")[0:P, 0:P]).then_inc(s["turned"], 1)

            @block.scalar
            def _(act):
                act.wait_ge(s["turned"], 4)
                act.activation(dst[0:rows, 0:4 * P], self.bank(0)[0:rows, 0:4 * P], ACT.Copy).then_inc(s["copied_a"], 1)

            @block.vector
            def _(dve):
                dve.wait_ge(s["turned"], NT)
                dve.tensor_copy(dst[0:rows, 4 * P:L], self.bank(1)[0:rows, 0:3 * P]).then_inc(s["copied_d"], 1)

    def project(self, jobs):
        s = self.s
        steps = []
        for kind, wt, src, dst, what in jobs:
            if kind == "c":
                m = wt.shape[1]
                for h in range(2):
                    steps.append(([(lambda b, m=m: b[0:m, 0:HALF], wt, src[:, h * HALF:(h + 1) * HALF])],
                                  lambda b, m=m: b[0:m, 0:HALF], dst[0:m, h * HALF:(h + 1) * HALF], what))
            else:
                m = wt.shape[1]
                mms = [(lambda b, t=t, m=m: b[0:P, t * m:(t + 1) * m], src[:, P * t:P * t + P], wt) for t in range(NT)]
                steps.append((mms, lambda b, m=m: b[0:P, 0:NT * m].rearrange("p (t m) -> p t m", m=m), dst, what))
        NB = 8
        with self.block() as block:
            @block.tensor
            def _(pe):
                for n, (mms, _, _, _) in enumerate(steps):
                    if n >= NB:
                        pe.wait_ge(s["copied_a"] if n % 2 == 0 else s["copied_d"], (n - NB) // 2 + 1)
                    for out, lhs, rhs in mms:
                        last = pe.matmul(out(self.bank(n % NB)), lhs, rhs, start=True, stop=True)
                    last.then_inc(s["prod_ready"], 1)

            def evacuate(n, engine, acts):
                _, view, dst, what = steps[n]
                src = view(self.bank(n % NB))
                engine.wait_ge(s["prod_ready"], n + 1)
                if acts:
                    return engine.activation(dst, src, what or ACT.Copy)
                if what == ACT.Relu:
                    return engine.tensor_scalar(dst, src, 0.0, None, ALU.max)
                return engine.tensor_copy(dst, src)

            assert all(what in (None, ACT.Relu, ACT.Tanh) for *_, what in steps)
            only_act = any(what == ACT.Tanh for *_, what in steps)

            @block.scalar
            def _(act):
                for n in range(len(steps)):
                    if only_act or n % 2 == 0:
                        evacuate(n, act, True).then_inc(s["copied_a"] if n % 2 == 0 else s["copied_d"], 1)

            if not only_act:
                @block.vector
                def _(dve):
                    for n in range(1, len(steps), 2):
                        evacuate(n, dve, False).then_inc(s["copied_d"], 1)

    def softmax_attention(self, units, scale, causal, loads=None, n_loads=0):
        s = self.s
        order = (6, 0, 5, 1, 4, 2, 3) if causal else range(NT)
        work = [(u, t) for u in range(len(units)) for t in order]
        N = len(work)
        keys = lambda g: (work[g][1] + 1 if causal else NT)
        late = [keys(g) > 4 for g in range(N)]
        n_late = lambda g: sum(late[:max(g, 0)])
        S = lambda g: self.bank(2 * (g % 2), 2)
        T = lambda c: self.bank(4 + c)
        OT, OUT = self.bank(6), self.bank(7)
        PT = [self.PT[0:P, b, :] for b in range(3)]
        wide = units[0][2].shape[2]
        groups = 128 // wide
        d = HD if groups == 4 else D
        eyes = self.w("four_eyes" if groups == 4 else "two_eyes")
        rows = lambda g: wide * min(groups, keys(g))
        sums = lambda u: self.RS[:, 8 * (u % 2):8 * (u % 2) + NT]
        with self.block() as block:
            if loads is not None:
                @block.sync
                def _(sp):
                    loads(sp)
                    sp.wait_ge(s["loaded"], n_loads)

            @block.tensor
            def _(pe):
                def scores(g):
                    u, t = work[g]
                    qT, kT = units[u][:2]
                    if g >= 2:
                        pe.wait_ge(s["probs_ready"], g - 1)
                    width = keys(g) * P
                    for a in range(0, width, 512):
                        e = min(width, a + 512)
                        last = pe.matmul(S(g)[0:P, a:e], qT[:, P * t:P * t + P], kT[:, a:e],
                                         start=True, stop=not (causal and e > P * t))
                        if causal and e > P * t:
                            m = max(a, P * t)
                            last = pe.matmul(S(g)[0:P, m:e], self.identb[:, :], self.laterb[:, m - P * t:e - P * t],
                                             start=False, stop=True)
                    last.then_inc(s["scores_ready"], 1)

                def turn(g):
                    pe.wait_ge(s["probs_ready"], g + 1)
                    for k in range(keys(g)):
                        if k == 0 and g >= 1:
                            pe.wait_ge(s["turned_a"], g)
                        if k == 4 and n_late(g):
                            pe.wait_ge(s["turned_d"], n_late(g))
                        last = pe.transpose(T(k // 4)[0:P, P * (k % 4):P * (k % 4) + P],
                                            self.PR[:, g % 2, P * k:P * k + P], self.w("ident")[0:P, 0:P])
                        if k == min(4, keys(g)) - 1:
                            last.then_inc(s["probs_turned"], 1)
                        elif k == keys(g) - 1:
                            last.then_inc(s["turned"], 1)

                def weigh(g):
                    v = units[work[g][0]][2]
                    pe.wait_ge(s["turned_a"], g + 1)
                    if g >= 1:
                        pe.wait_ge(s["copied_d"], g)
                    for k in range(keys(g)):
                        if k == 4:
                            pe.wait_ge(s["turned_d"], n_late(g + 1))
                        at = wide * (k % groups)
                        last = pe.matmul(OT[at:at + wide, 0:P], v[:, k, :], PT[g % 3][:, P * k:P * k + P],
                                         start=(k < groups), stop=(k >= keys(g) - groups))
                    last.then_inc(s["pv_ready"], 1)

                def unturn(g):
                    u, t = work[g]
                    pe.wait_ge(s["copied_d"], g + 1)
                    if g % NT == 0 and u:
                        pe.wait_ge(s["out_done"], u)
                    pe.matmul(OUT[0:P, d * t:d * t + d], self.OTS[0:rows(g), g % 2, :], eyes[0:rows(g), :],
                              start=True, stop=True).then_inc(s["kv_ready"], 1)

                for i in range(N + 4):
                    if i < N:
                        scores(i)
                    if 0 <= i - 2 < N:
                        turn(i - 2)
                    if 0 <= i - 3 < N:
                        weigh(i - 3)
                    if 0 <= i - 4 < N:
                        unturn(i - 4)

            @block.vector
            def _(dve):
                link = self.chain(dve, s["step_dve"])

                def largest(g):
                    if g >= 2:
                        dve.wait_ge(s["probs_ready"], g - 1)
                    dve.wait_ge(s["scores_ready"], g + 1)
                    link(dve.tensor_reduce(self.NM[:, g % 2:g % 2 + 1], S(g)[0:P, 0:keys(g) * P], AX.X, ALU.max))
                    dve.tensor_scalar(self.NM[:, 2 + g % 2:3 + g % 2], self.NM[:, g % 2:g % 2 + 1], -scale, None,
                                      ALU.mult).then_inc(s["max_ready"], 1)

                def take(g):
                    dve.wait_ge(s["pv_ready"], g + 1)
                    if g >= 2:
                        dve.wait_ge(s["kv_ready"], g - 1)
                    dve.tensor_copy(self.OTS[0:rows(g), g % 2, :], OT[0:rows(g), 0:P]).then_inc(s["copied_d"], 1)

                def finish(u):
                    v, out, add = units[u][2:]
                    dve.wait_ge(s["kv_ready"], NT * (u + 1))
                    dve.wait_ge(s["probs_ready"], NT * (u + 1))
                    o = OUT[0:P, 0:NT * d].rearrange("p (t d) -> p t d", t=NT)
                    link(dve.reciprocal(sums(u), sums(u)))
                    r = sums(u).unsqueeze(2).broadcast_to((P, NT, d))
                    if add is None:
                        dve.tensor_tensor(out, o, r, ALU.mult).then_inc(s["out_done"], 1)
                    else:
                        dve.tensor_tensor(self.SQ, o, r, ALU.mult).then_inc(s["out_done"], 1)
                        dve.wait_ge(s["out_done"], u + 1)
                        link(dve.tensor_tensor(out, self.SQ, add, ALU.add))

                for i in range(N + 5):
                    if i < N:
                        largest(i)
                    if 0 <= i - 3 < N:
                        take(i - 3)
                    if 0 <= i - 5 and (i - 5) % NT == NT - 1:
                        finish((i - 5) // NT)
                    if 0 <= i - 2 < N and late[i - 2]:
                        g = i - 2
                        dve.wait_ge(s["turned"], n_late(g + 1))
                        if g >= 3:
                            dve.wait_ge(s["pv_ready"], g - 2)
                        dve.tensor_copy(PT[g % 3][:, 4 * P:keys(g) * P], T(1)[0:P, 0:(keys(g) - 4) * P])\
                           .then_inc(s["turned_d"], 1)

            @block.scalar
            def _(act):
                for i in range(N + 2):
                    if i >= 2:
                        g = i - 2
                        n = min(4, keys(g)) * P
                        act.wait_ge(s["probs_turned"], g + 1)
                        if g >= 3:
                            act.wait_ge(s["pv_ready"], g - 2)
                        act.activation(PT[g % 3][:, 0:n], T(0)[0:P, 0:n], ACT.Copy).then_inc(s["turned_a"], 1)
                    if i < N:
                        act.wait_ge(s["max_ready"], i + 1)
                        if i >= 2 and late[i - 2]:
                            act.wait_ge(s["turned"], n_late(i - 1))
                        u, t = work[i]
                        if t == order[0] and u >= 2:
                            act.wait_ge(s["out_done"], u - 1)
                        act.activation(self.PR[:, i % 2, 0:keys(i) * P], S(i)[0:P, 0:keys(i) * P], ACT.Exp,
                                       bias=self.NM[:, 2 + i % 2:3 + i % 2], scale=scale, accum_out=sums(u)[:, t:t + 1]).then_inc(s["probs_ready"], 1)

    def causal_product(self, qT, kT, v, relu, out):
        s = self.s
        taken = lambda j: s["copied_a"] if j % 2 == 0 else s["copied_d"]
        with self.block() as block:
            @block.tensor
            def _(pe):
                for j in range(NT):
                    if j >= 3:
                        pe.wait_ge(taken(j - 3), (j - 3) // 2 + 1)
                    S = self.bank(2 * (j % 3), 2)
                    for a in range(P * j, L, 512):
                        e = min(L, a + 512)
                        last = pe.matmul(S[0:P, a - P * j:e - P * j], kT[:, P * j:P * j + P], qT[:, a:e],
                                         start=True, stop=True)
                    last.then_inc(s["scores_ready"], 1)
                for t in range(NT):
                    pe.wait_ge(s["mask_ready"], t + 1)
                    for k in range(t + 1):
                        last = pe.matmul(self.bank(7)[0:P, D * t:D * t + D], self.PT[0:P, k, P * t:P * t + P], v[:, k, :],
                                         start=(k == 0), stop=(k == t))
                last.then_inc(s["pv_ready"], 1)

            @block.scalar
            def _(act):
                for j in range(0, NT, 2):
                    act.wait_ge(s["scores_ready"], j + 1)
                    act.activation(self.PT[0:P, j, P * j:L], self.bank(2 * (j % 3), 2)[0:P, 0:L - P * j],
                                   ACT.Relu if relu else ACT.Copy).then_inc(s["copied_a"], 1)

            @block.gpsimd
            def _(pool):
                for j in range(NT):
                    pool.wait_ge(taken(j), j // 2 + 1)
                    diagonal = self.PT[0:P, j, P * j:P * j + P]
                    pool.tensor_tensor(diagonal, diagonal, self.w("keep_t"), ALU.mult).then_inc(s["mask_ready"], 1)

            @block.vector
            def _(dve):
                for j in range(1, NT, 2):
                    dve.wait_ge(s["scores_ready"], j + 1)
                    S = self.bank(2 * (j % 3), 2)[0:P, 0:L - P * j]
                    if relu:
                        dve.tensor_scalar(self.PT[0:P, j, P * j:L], S, 0.0, None, ALU.max).then_inc(s["copied_d"], 1)
                    else:
                        dve.tensor_copy(self.PT[0:P, j, P * j:L], S).then_inc(s["copied_d"], 1)
                dve.wait_ge(s["pv_ready"], 1)
                out(dve, self.chain(dve, s["step_dve"]), self.bank(7)[0:P, 0:NT * D].rearrange("p (t d) -> p t d", d=D))

    def softmax_rows(self, dve, act_sems, link, x, groups, width, scale_into_exp=1.0):
        s = self.s
        m = self.ST[:, 0:groups]
        wide = m.unsqueeze(2).broadcast_to((P, groups, width))
        link(dve.tensor_reduce(m, x, AX.X, ALU.max))
        dve.tensor_tensor(x, x, wide, ALU.subtract).then_inc(s["var_ready"], 1)
        dve.wait_ge(s["std_ready"], 1)
        link(dve.tensor_reduce(m, x, AX.X, ALU.add))
        link(dve.reciprocal(m, m))
        link(dve.tensor_tensor(x, x, wide, ALU.mult))

    def softmax_block(self, x, groups, width, before=None, after=None, scale=1.0):
        s = self.s
        with self.block() as block:
            @block.vector
            def _(dve):
                link = self.chain(dve, s["step_dve"])
                if before is not None:
                    before(dve, link)
                self.softmax_rows(dve, None, link, x, groups, width)
                if after is not None:
                    after(dve, link)

            @block.scalar
            def _(act):
                act.wait_ge(s["var_ready"], 1)
                act.activation(x, x, ACT.Exp, scale=scale).then_inc(s["std_ready"], 1)

    def zero(self, *views):
        with self.block() as block:
            @block.gpsimd
            def _(pool):
                link = self.chain(pool, self.s["step_pool"])
                for v in views:
                    link(pool.memset(v, 0.0))

    def head_operands(self, n):
        s, HW, x = self.s, self.HW1, self.SN
        cols = lambda h: slice(h * HALF, h * HALF + HALF)
        with self.block() as block:
            @block.tensor
            def _(pe):
                pe.wait_ge(s["loaded"], 1)
                for h in range(2):
                    pe.matmul(self.bank(h)[:, 0:HALF], HW[:, 0:128], x[:, cols(h)], start=True, stop=True).then_inc(s["prod_ready"], 1)
                for h in range(2):
                    pe.matmul(self.bank(2 + h)[:, 0:HALF], HW[:, 128:256], x[:, cols(h)], start=True, stop=True).then_inc(s["prod_ready"], 1)
                for t in range(NT):
                    last = pe.matmul(self.bank(4)[0:P, 32 * t:32 * t + 32], x[:, P * t:P * t + P], HW[:, 256:288], start=True, stop=True)
                last.then_inc(s["prod_ready"], 1)

            @block.scalar
            def _(act):
                act.wait_ge(s["prod_ready"], 1)
                for e in range(NE):
                    rows = slice(32 * e, 32 * e + HD)
                    act.activation(self.GB[rows, e, cols(0)], self.bank(0)[rows, 0:HALF], ACT.Copy).then_inc(s["copied_a"], 1)
                act.wait_ge(s["prod_ready"], 3)
                act.activation(self.KT[:, cols(0)], self.bank(2)[:, 0:HALF], ACT.Copy).then_inc(s["copied_a"], 1)

            @block.vector
            def _(dve):
                dve.tensor_copy(HW, self.wx("f1_heads")[:, bass.ds(n * 288, 288)]).then_inc(s["loaded"], 1)
                dve.wait_ge(s["prod_ready"], 2)
                for e in range(NE):
                    rows = slice(32 * e, 32 * e + HD)
                    dve.tensor_copy(self.GB[rows, e, cols(1)], self.bank(1)[rows, 0:HALF]).then_inc(s["copied_d"], 1)
                dve.wait_ge(s["prod_ready"], 4)
                dve.tensor_copy(self.KT[:, cols(1)], self.bank(3)[:, 0:HALF]).then_inc(s["copied_d"], 1)
                dve.wait_ge(s["prod_ready"], 5)
                dve.tensor_copy(self.VN[:, :, 0:32], self.bank(4)[0:P, 0:32 * NT].rearrange("p (t d) -> p t d", t=NT)).then_inc(s["copied_d"], 1)

    def add(self, dst, a, b):
        with self.block() as block:
            @block.vector
            def _(dve):
                dve.tensor_tensor(dst, a, b, ALU.add).then_inc(self.s["step_dve"], 1)

    def top_two(self, probs, gates, eps):
        s = self.s
        top, idx, pick = self.TOP, self.IDX, self.TOPF
        g3 = lambda a: a.rearrange("p (t e) -> p t e", e=8)
        with self.block() as block:
            @block.vector
            def _(dve):
                link = self.chain(dve, s["step_dve"])
                for t in range(NT):
                    dve.max(top[:, 8 * t:8 * t + 8], probs[:, t, :]).then_inc(s["max_ready"], 1)
                dve.wait_ge(s["max_ready"], NT)
                for t in range(NT):
                    dve.max_index(idx[:, 8 * t:8 * t + 8], top[:, 8 * t:8 * t + 8], probs[:, t, :]).then_inc(s["mask_ready"], 1)
                dve.wait_ge(s["mask_ready"], NT)
                link(dve.tensor_copy(pick, idx))
                at = lambda j: g3(pick)[:, :, j:j + 1].broadcast_to((P, NT, 8))
                e = g3(self.w("experts"))
                m0, m1 = g3(self.ST[:, 0:56]), g3(self.ST2[:, 0:56])
                link(dve.tensor_tensor(m0, e, at(0), ALU.is_equal))
                link(dve.tensor_tensor(m1, e, at(1), ALU.is_equal))
                link(dve.tensor_tensor(m0, m0, m1, ALU.add))
                den = self.ST2[:, 64:64 + NT]
                t3 = g3(top)
                link(dve.tensor_tensor(den.unsqueeze(2), t3[:, :, 0:1], t3[:, :, 1:2], ALU.add))
                if eps:
                    link(dve.tensor_scalar(den, den, eps, None, ALU.add))
                link(dve.reciprocal(den, den))
                link(dve.tensor_tensor(m0, m0, probs, ALU.mult))
                link(dve.tensor_tensor(gates, m0, den.unsqueeze(2).broadcast_to((P, NT, 8)), ALU.mult))

    def window_pool(self, b):
        s, X9, SC = self.s, self.X9, self.ST2[:, 0:NT * WIN]
        with self.block() as block:
            @block.sync
            def _(sp):
                x = self.dram["x"]
                for t in range(NT):
                    src = bass.AP(x.tensor, x.offset + t * P * D, [[LIN * D, NSEQ], [D, P], [1, WIN * D]])
                    sp.dma_start(X9[:, t, :], src[bass.ds(b, 1)].rearrange("o p c -> (o p) c")).then_inc(s["loaded"], 16)

            @block.tensor
            def _(pe):
                pe.wait_ge(s["loaded"], 16 * NT)
                for t in range(NT + 1):
                    src = X9[:, t, 0:D] if t < NT else X9[:, NT - 1, (WIN - 1) * D:]
                    out = self.bank(t // 4)[0:D, P * (t % 4):P * (t % 4) + P]
                    pe.transpose(out, src, self.w("ident")[0:P, 0:P]).then_inc(s["turned"], 1)

            @block.scalar
            def _(act):
                act.wait_ge(s["turned"], 4)
                act.activation(self.XT[0:D, 0:4 * P], self.bank(0)[0:D, 0:4 * P], ACT.Copy).then_inc(s["copied_a"], 1)

            @block.vector
            def _(dve):
                dve.wait_ge(s["turned"], NT + 1)
                dve.tensor_copy(self.XT[0:D, 4 * P:L], self.bank(1)[0:D, 0:3 * P]).then_inc(s["copied_d"], 1)
                dve.tensor_copy(self.XT[0:D, L:LIN], self.bank(1)[0:D, 4 * P - WIN + 1:4 * P]).then_inc(s["copied_d"], 1)
        hk = LIN // 2
        T = [self.PT[0:D, 0, :], self.PT[0:D, 1, :]]
        with self.block() as block:
            @block.tensor
            def _(pe):
                for h in range(2):
                    pe.matmul(self.bank(h)[0:D, 0:hk], self.w("tok_k"), self.XT[0:D, h * hk:(h + 1) * hk],
                              start=True, stop=True).then_inc(s["prod_ready"], 1)
                for h in range(2):
                    a = WIN // 2 + h * HALF
                    pe.matmul(self.bank(2 + h)[0:D, 0:HALF], self.w("tok_q"), self.ones_xt(a, a + HALF),
                              start=True, stop=True).then_inc(s["prod_ready"], 1)
                for w in range(WIN):
                    pe.wait_ge(s["tanh_ready"], w + 1)
                    for t in range(NT):
                        c = t * WIN + w
                        last = pe.matmul(self.bank(4)[0:P, c:c + 1], T[w % 2][:, P * t:P * t + P], self.w("tok_v"),
                                         start=True, stop=True)
                    last.then_inc(s["scores_ready"], 1)

            @block.vector
            def _(dve):
                for h in range(2):
                    dve.wait_ge(s["prod_ready"], h + 1)
                    dve.tensor_copy(self.KT[0:D, h * hk:(h + 1) * hk], self.bank(h)[0:D, 0:hk]).then_inc(s["copied_d"], 1)
                for h in range(2):
                    dve.wait_ge(s["prod_ready"], h + 3)
                    dve.tensor_copy(self.QT[0:D, h * HALF:(h + 1) * HALF], self.bank(2 + h)[0:D, 0:HALF]).then_inc(s["copied_d"], 1)
                dve.wait_ge(s["copied_d"], 4)
                for w in range(WIN):
                    if w >= 2:
                        dve.wait_ge(s["scores_ready"], w - 1)
                    dve.tensor_tensor(T[w % 2], self.QT[0:D, 0:L], self.KT[0:D, w:w + L], ALU.add).then_inc(s["sum_ready"], 1)
                dve.wait_ge(s["scores_ready"], WIN)
                dve.tensor_copy(SC, self.bank(4)[0:P, 0:NT * WIN]).then_inc(s["out_done"], 1)

            @block.scalar
            def _(act):
                for w in range(WIN):
                    act.wait_ge(s["sum_ready"], w + 1)
                    act.activation(T[w % 2], T[w % 2], ACT.Tanh).then_inc(s["tanh_ready"], 1)

        sc3 = SC.rearrange("p (t w) -> p t w", w=WIN)

        def weigh(dve, link):
            x3 = X9[:, :, :].rearrange("p t (w c) -> p (t w) c", c=D)
            link(dve.tensor_tensor(x3, x3, SC.unsqueeze(2).broadcast_to((P, NT * WIN, D)), ALU.mult))
            link(dve.tensor_reduce(self.H[:, :, :], X9[:, :, :].rearrange("p t (w c) -> p t c w", c=D), AX.X, ALU.add))
        self.softmax_block(sc3, NT, WIN, after=weigh)

    def ones_xt(self, a, e):
        return self.XT[0:D + 1, a:e]

    def relu_attention(self):
        s = self.s
        self.norm(self.H[:, :, :], self.X[:, :, :], NT, D, 1e-5)
        self.turn(self.X, self.XT)
        xt = self.XT[:, 0:L]
        self.project([("c", self.wx("a0_q"), xt, self.QT[0:D, :], None), ("c", self.wx("a0_k"), xt, self.KT[0:D, :], None),
                      ("t", self.VO[:, :], self.XT[0:D, 0:L], self.V[:, :, :], None)])

        def out(dve, link, acc):
            link(dve.tensor_tensor(self.A[:, :, :], acc, self.w("inv_row").unsqueeze(2).broadcast_to((P, NT, D)), ALU.mult))
            link(dve.tensor_tensor(self.H[:, :, :], self.H[:, :, :], self.A[:, :, :], ALU.add))
        self.causal_product(self.QT[0:D, 0:L], self.KT[0:D, 0:L], self.V, True, out)

    def mixture(self, into, gated, chunk, hidden, out_w, bias, experts, glu):
        s = self.s
        N = 4 * experts
        U = lambda n: self.bank(2 * (n % 2), 2)
        B = lambda j: self.bank(4 + j % 2)[0:chunk, 0:HALF]
        O = lambda h: self.bank(6 + h)[0:D, 0:HALF]
        G = lambda n: self.GB[:, n % 4, 0:HALF]
        cols = lambda h: slice(h * HALF, (h + 1) * HALF)
        ready = s["hidden_used"] if gated or glu else s["hidden_act"]
        with self.block() as block:
            @block.tensor
            def _(pe):
                if bias is not None:
                    for h in range(2):
                        pe.matmul(O(h), bias[0], bias[1][:, cols(h)], start=True, stop=False)
                for n in range(N + 2):
                    if n < N:
                        e, h, c, j = n // 4, n // 2 % 2, n % 2, n // 2
                        if n >= 2:
                            pe.wait_ge(s["hidden_used"] if glu else s["hidden_act"], n - 1)
                        for i, wt in enumerate(hidden(e, c)):
                            last = pe.matmul(U(n)[0:chunk, 512 * i:512 * i + HALF], wt, self.XT[:, cols(h)], start=True, stop=True)
                        last.then_inc(s["hidden_ready"], 1)
                        if gated and c == 0:
                            if j >= 2:
                                pe.wait_ge(s["hidden_used"], 2 * j - 2)
                            pe.matmul(B(j), self.w("ident")[:, e:e + 1].broadcast_to((128, chunk)), self.GATES[:, cols(h)],
                                      start=True, stop=True).then_inc(s["scores_ready"], 1)
                    m = n - 2
                    if m >= 0:
                        e, h, c = m // 4, m // 2 % 2, m % 2
                        pe.wait_ge(ready, m + 1)
                        pe.matmul(O(h), out_w(e, c), G(m), start=(bias is None and e == 0 and c == 0),
                                  stop=(e == experts - 1 and c == 1)).then_inc(s["pv_ready"], 1)
                pe.wait_ge(s["copied_a"], 1)
                pe.wait_ge(s["copied_d"], 1)
                for t in range(NT):
                    last = pe.transpose(self.bank(0)[0:P, D * t:D * t + D], self.C2[0:D, P * t:P * t + P], self.w("ident")[0:D, 0:D])
                last.then_inc(s["turned"], 1)

            @block.scalar
            def _(act):
                for n in range(N):
                    act.wait_ge(s["hidden_ready"], n + 1)
                    if n >= 4:
                        act.wait_ge(s["pv_ready"], n - 3)
                    act.activation(G(n)[0:chunk, :], U(n)[0:chunk, 0:HALF], ACT.Silu if glu else ACT.Gelu)\
                       .then_inc(s["hidden_act"], 1)
                act.wait_ge(s["pv_ready"], N)
                act.activation(self.C2[0:D, cols(0)], O(0), ACT.Copy).then_inc(s["copied_a"], 1)

            @block.vector
            def _(dve):
                link = self.chain(dve, s["step_dve"])
                for n in range(N):
                    g = G(n)[0:chunk, :]
                    if gated or glu:
                        dve.wait_ge(s["hidden_act"], n + 1)
                    if glu:
                        link(dve.tensor_tensor(g, g, U(n)[0:chunk, 512:512 + HALF], ALU.mult))
                    if gated:
                        dve.wait_ge(s["scores_ready"], n // 2 + 1)
                        dve.tensor_tensor(g, g, B(n // 2), ALU.mult).then_inc(s["hidden_used"], 1)
                dve.wait_ge(s["pv_ready"], N)
                dve.tensor_copy(self.C2[0:D, cols(1)], O(1)).then_inc(s["copied_d"], 1)
                dve.wait_ge(s["turned"], 1)
                link(dve.tensor_tensor(into, into, self.bank(0)[0:P, 0:NT * D].rearrange("p (t d) -> p t d", d=D), ALU.add))

    def turn_gates(self):
        with self.block() as block:
            @block.gpsimd
            def _(pool):
                pool.memset(self.GATES, 1.0).then_inc(self.s["step_pool"], 1)
        self.turn(self.GT, self.GATES, rows=8)

    def first_mixture(self):
        self.norm(self.H[:, :, :], self.X[:, :, :], NT, D, 1e-5)
        self.turn(self.X, self.XT)
        self.project([("t", self.wx("m0_r"), self.XT[:, 0:L], self.RT[:, :, :], None)])
        self.softmax_block(self.RT[:, :, :], NT, 8)
        self.top_two(self.RT[:, :, :], self.GT[:, :, :], 0.0)
        self.turn_gates()
        w1, w2 = self.wx("m0_w1"), self.w("m0_w2")
        self.mixture(self.H, True, 128, lambda e, c: (w1[:, F0 * e + 128 * c:F0 * e + 128 * c + 128],),
                     lambda e, c: w2[:, D * (2 * e + c):D * (2 * e + c) + D], (self.wx("m0_b2"), self.GATES), E0 + 1, False)

    def phase_tables(self):
        s, ph, k, r = self.s, self.w("phases"), self.QT[:, 0:L], self.TRIG
        round_up = 12582912.0
        parts = [6.28125, 0.0019352436065673828, 6.357301884918343e-08]
        with self.block() as block:
            @block.vector
            def _(dve):
                link = self.chain(dve, s["step_dve"])
                link(dve.tensor_scalar(k, ph, 0.15915494309189535, None, ALU.mult))
                link(dve.tensor_scalar(k, k, round_up, None, ALU.add))
                link(dve.tensor_scalar(k, k, -round_up, None, ALU.add))
                link(dve.scalar_tensor_tensor(r, k, -parts[0], ph, ALU.mult, ALU.add))
                link(dve.scalar_tensor_tensor(r, k, -parts[1], r, ALU.mult, ALU.add))
                link(dve.scalar_tensor_tensor(r, k, -parts[2], r, ALU.mult, ALU.add))
                dve.tensor_scalar(r, r, PI_DOWN, -PI_DOWN, ALU.min, ALU.max).then_inc(s["phase_ready"], 1)

            @block.scalar
            def _(act):
                act.wait_ge(s["phase_ready"], 1)
                act.activation(r[0:D, :], r[0:D, :], ACT.Abs).then_inc(s["step_act"], 1)
                act.wait_ge(s["step_act"], 1)
                act.activation(r[0:D, :], r[0:D, :], ACT.Sin, bias=self.w("half_pi")[0:D, :], scale=-1.0).then_inc(s["step_act"], 1)
                act.activation(r[D:128, :], r[D:128, :], ACT.Sin).then_inc(s["step_act"], 1)

    def memory(self):
        s = self.s
        xt1 = self.XT[:, 0:L]
        self.norm(self.H, self.X, NT, D, 1e-5)
        self.turn(self.X, self.XT)
        self.project([("c", self.wx("h1_k1"), xt1, self.C1, ACT.Tanh), ("c", self.wx("h1_q1"), xt1, self.C2, ACT.Tanh)])
        self.project([("c", self.wx("h1_k2"), self.C1, self.KT, ACT.Tanh), ("c", self.wx("h1_q2"), self.C2, self.QT, ACT.Tanh)])
        with self.block() as block:
            @block.scalar
            def _(act):
                for u in (self.KT, self.QT):
                    act.activation(u[0:32, 0:L], u[0:32, 0:L], ACT.Abs).then_inc(s["step_act"], 1)
                act.wait_ge(s["step_act"], 2)
                for u in (self.KT, self.QT):
                    act.activation(u[0:32, 0:L], u[0:32, 0:L], ACT.Sin, bias=self.w("half_pi")[0:32, :],
                                   scale=-PI_DOWN).then_inc(s["step_act"], 1)
                    act.activation(u[32:64, 0:L], u[32:64, 0:L], ACT.Sin, scale=PI_DOWN).then_inc(s["step_act"], 1)
        self.project([("t", self.wx("h1_vc"), xt1, self.V, None), ("c", self.wx("h1_vp"), xt1, self.MV, None),
                      ("c", self.wx("h1_g1"), xt1, self.G1, ACT.Relu)])

        def content(dve, link, acc):
            link(dve.tensor_tensor(self.Y, acc, self.w("inv_pos32").unsqueeze(2).broadcast_to((P, NT, D)), ALU.mult))
        M = self.MP
        with self.block() as block:
            @block.vector
            def _(dve):
                link = self.chain(dve, s["step_dve"])
                link(dve.tensor_tensor(M, self.MV, self.TRIG, ALU.mult))
                link(dve.tensor_tensor_scan(self.MS, self.ONES, M, 0.0, ALU.mult, ALU.add))
                link(dve.tensor_tensor(M, self.MS, self.TRIG, ALU.mult))
        self.project([("t", self.w("two_eyes"), M, self.A, None), ("t", self.w("h1_g2"), self.G1, self.GL2, None)])
        self.causal_product(self.QT[0:D, 0:L], self.KT[0:D, 0:L], self.V, False, content)

        def combine(dve, link):
            g = lambda j: self.GL2[:, :, j:j + 1].broadcast_to((P, NT, D))
            link(dve.tensor_tensor(self.A, self.A, self.w("inv_pos").unsqueeze(2).broadcast_to((P, NT, D)), ALU.mult))
            link(dve.tensor_tensor(self.A, self.A, g(0), ALU.mult))
            link(dve.tensor_tensor(self.Y, self.Y, g(1), ALU.mult))
            link(dve.tensor_tensor(self.Y, self.Y, self.A, ALU.add))
        self.softmax_block(self.GL2, NT, 2, after=combine)
        self.norm(self.Y, self.A, NT, D, 1e-5, gamma=self.w("h1_g"), beta=self.w("h1_b"))
        self.turn(self.A, self.C1)
        self.project([("t", self.wx("h1_o"), self.C1, self.A, None)])
        with self.block() as block:
            @block.vector
            def _(dve):
                link = self.chain(dve, s["step_dve"])
                link(dve.tensor_tensor(self.H, self.H, self.X, ALU.add))
                link(dve.tensor_tensor(self.H, self.H, self.A, ALU.add))

    def head_inputs(self):
        self.norm(self.H, self.X, NT, D, 1e-5)
        self.turn(self.X, self.XT)
        self.project([("t", self.wx("f1_hl"), self.XT[:, 0:L], self.SX, None)])

    def keep_sequence(self, b):
        s = self.s
        with self.block() as block:
            @block.vector
            def _(dve):
                dve.tensor_copy(self.HA[:, bass.ds(b, 1)], self.H.rearrange("p t d -> p (t d)").unsqueeze(1)).then_inc(s["step_dve"], 1)
                dve.tensor_copy(self.RES[:, bass.ds(b, 1)].rearrange("p o t d -> p (o t) d"), self.SX[:, :, bass.ds(b * HD, HD)]).then_inc(s["step_dve"], 1)

    def fetch_sequence(self, b):
        s = self.s
        with self.block() as block:
            @block.vector
            def _(dve):
                dve.tensor_copy(self.H.rearrange("p t d -> p (t d)").unsqueeze(1), self.HA[:, bass.ds(b, 1)]).then_inc(s["step_dve"], 1)

    def expert_heads(self):
        s = self.s
        self.head_inputs()
        self.project([("c", self.wx("f1_hl"), self.XT[:, 0:L], self.SN, None)])
        self.zero(self.GB)
        with self.nc.Fori(0, NH) as n:
            self.head_operands(n)
            self.softmax_attention([(self.GB[:, e, :], self.KT[:, 0:L], self.VN[:, :, 0:32],
                                     self.QN[:, :, HD * e:HD * e + HD], None) for e in range(NE)], float(HD) ** 0.5, True)
            with self.block() as block:
                @block.vector
                def _(dve):
                    dve.tensor_copy(self.QKV[:, :, bass.ds(n, 1), :], self.QN.unsqueeze(2)).then_inc(s["step_dve"], 1)
        with self.block() as block:
            @block.vector
            def _(dve):
                link = self.chain(dve, s["step_dve"])
                link(dve.tensor_scalar(self.A, self.SX, 0.0, None, ALU.not_equal))
                for e in range(NE):
                    q = self.QKV.rearrange("p t n (e d) -> p (t n) e d", e=NE)[:, :, e, :]
                    dve.tensor_tensor(q, q, self.A.rearrange("p t (n d) -> p (t n) d", d=HD), ALU.mult).then_inc(s["mask_ready"], 1)
        for g in range(2):
            self.turn(self.QKV[:, :, 2 * g:2 * g + 2, :].rearrange("p t n f -> p t (n f)"), self.QT if g == 0 else self.KT, rows=128)
        gate = self.w("f1_gate")
        self.project([("t", gate[:, 0:8], self.QT, self.GL[:, :, 0:8], None), ("t", gate[:, 8:16], self.KT, self.GL[:, :, 8:16], None)])
        over = lambda a, m: a.unsqueeze(1).broadcast_to((P, m, a.shape[1]))

        def bias(dve, link):
            link(dve.tensor_tensor(self.GL, self.GL, over(self.w("f1_gate_b"), NT), ALU.add))

        def mix(dve, link):
            q = self.QKV.rearrange("p t n (e d) -> p (t n e) d", e=NE)
            g = self.GL.rearrange("p t g -> p (t g)").unsqueeze(2).broadcast_to((P, NT * NH * NE, HD))
            link(dve.tensor_tensor(q, q, g, ALU.mult))
            link(dve.tensor_reduce(self.A.rearrange("p t (n d) -> p (t n) d", d=HD),
                                   self.QKV.rearrange("p t n (e d) -> p (t n) d e", e=NE), AX.X, ALU.add))
            a4 = self.A.rearrange("p t (n d) -> p t n d", d=HD)
            link(dve.tensor_tensor(a4, a4, self.RES.rearrange("p n t d -> p t n d"), ALU.add))
        self.softmax_block(self.GL.rearrange("p t (n e) -> p (t n) e", e=NE), NT * NH, NE, before=bias, after=mix)
        heads = lambda a: a.rearrange("p t (n d) -> p (t n) d", d=HD)
        self.norm(heads(self.A), heads(self.Y), NT * NH, HD, 1e-8, gamma=self.w("f1_g"), beta=self.w("f1_b"))
        self.turn(self.Y, self.C1)
        self.project([("c", self.wx("f1_fc1"), self.C1, self.C2, ACT.Relu)])
        with self.block() as block:
            @block.vector
            def _(dve):
                dve.scalar_tensor_tensor(self.C2[0:D, :], self.C1[0:D, :], 0.0, self.C2[0:D, :], ALU.not_equal, ALU.mult)\
                   .then_inc(s["step_dve"], 1)
        self.project([("t", self.wx("f1_fc2"), self.C2, self.A, None)])
        with self.block() as block:
            @block.vector
            def _(dve):
                link = self.chain(dve, s["step_dve"])
                link(dve.scalar_tensor_tensor(self.A, self.Y, 0.0, self.A, ALU.not_equal, ALU.mult))
                link(dve.tensor_tensor(self.A, self.A, self.Y, ALU.add))
        self.norm(heads(self.A), heads(self.Y), NT * NH, HD, 1e-8, gamma=self.w("f1_fg"), beta=self.w("f1_fb"))
        self.turn(self.Y, self.C1)
        self.project([("t", self.wx("f1_fgate"), self.C1, self.GL2b, None)])

        def out(dve, link):
            g = self.GL2b.rearrange("p t n -> p (t n)").unsqueeze(2).broadcast_to((P, NT * NH, HD))
            link(dve.tensor_tensor(heads(self.Y), heads(self.Y), g, ALU.mult))
            link(dve.tensor_tensor(self.H, self.H, self.Y, ALU.add))
        self.softmax_block(self.GL2b, NT, NH, after=out)


    def plain_attention(self):
        self.zero(self.QT[D:128, :], self.KT[D:128, :])
        self.norm(self.H, self.X, NT, D, 1e-5)
        self.turn(self.X, self.XT)
        xt = self.XT[:, 0:L]
        self.project([("c", self.wx("a2_q"), xt, self.QT, None), ("c", self.wx("a2_k"), xt, self.KT, None)])
        self.softmax_attention([(self.QT, self.KT[:, 0:L], self.X, self.H, self.H)], float(D) ** -0.5, False)

    def pair_cuts(self):
        s = self.s
        q = [self.PT[:, c, :] for c in range(4)]
        self.project([("c", self.wx("pk_q")[:, 128 * c:128 * c + 128], self.XT[:, 0:L], q[c], None) for c in range(4)])
        sims = [self.PT[0:P, 4 + i, :] for i in range(3)]
        SIM = self.PT[0:P, 4:7, :].rearrange("p a l -> p (a l)")
        sim = lambda t: SIM[:, 1024 * (t % 2):1024 * (t % 2) + 1024]
        keys = self.w("pk_keys")
        with self.block() as block:
            @block.tensor
            def _(pe):
                for t in range(NT):
                    if t >= 2:
                        pe.wait_ge(s["copied_a"], t - 1)
                    for c in range(4):
                        last = pe.matmul(self.bank(2 * (t % 2) + c // 2)[0:P, 256 * (c % 2):256 * (c % 2) + 256],
                                         q[c][:, P * t:P * t + P], keys[:, 256 * c:256 * c + 256], start=True, stop=True)
                    last.then_inc(s["scores_ready"], 1)

            @block.scalar
            def _(act):
                for t in range(NT):
                    act.wait_ge(s["scores_ready"], t + 1)
                    if t >= 2:
                        act.wait_ge(s["out_done"], t - 1)
                    act.activation(sim(t), self.bank(2 * (t % 2), 2)[0:P, :], ACT.Copy).then_inc(s["copied_a"], 1)

            @block.vector
            def _(dve):
                link = self.chain(dve, s["step_dve"])
                for t in range(NT):
                    dve.wait_ge(s["copied_a"], t + 1)
                    x = lambda g: sim(t)[:, NK * g:NK * g + NK]
                    sides, heads = range(2 * PKH), range(PKH)
                    for g in sides:
                        last = dve.max(self.V16[:, g, 0:8], x(g))
                    link(last)
                    for g in sides:
                        last = dve.match_replace(out=x(g), in_to_replace=self.V16[:, g, 0:8], in_values=x(g), imm_value=LOWEST)
                    link(last)
                    for g in sides:
                        last = dve.max(self.V16[:, g, 8:16], x(g))
                    link(last)
                    for g in sides:
                        last = dve.match_replace(out=x(g), in_to_replace=self.V16[:, g, 8:16], in_values=x(g), imm_value=LOWEST)
                    link(last)
                    link(dve.tensor_reduce(self.V16[:, :, 16], sim(t).rearrange("p (g k) -> p g k", k=NK), AX.X, ALU.max))
                    s0, s1 = self.V16[:, 0:PKH, :], self.V16[:, PKH:, :]
                    at = 0
                    for a, n in RUNS:
                        dve.tensor_tensor(self.CAND[:, :, at:at + n], s0[:, :, a:a + 1].broadcast_to((P, PKH, n)),
                                          s1[:, :, 0:n], ALU.add)
                        at += n
                    for a in (5, 6, 7):
                        dve.tensor_tensor(self.CAND[:, :, at:at + 2], s0[:, :, a:a + 1].broadcast_to((P, PKH, 2)),
                                          s1[:, :, 0:2], ALU.add)
                        at += 2
                    for a in (0, 16):
                        dve.tensor_tensor(self.CAND[:, :, at:at + 1], s0[:, :, a:a + 1], s1[:, :, 16 - a:17 - a], ALU.add)
                        at += 1
                    link(dve.tensor_tensor(self.CAND[:, :, at:at + 8], s0[:, :, 8:16], s1[:, :, 0:1].broadcast_to((P, PKH, 8)), ALU.add))
                    for r in range(3):
                        for h in heads:
                            last = dve.max(self.T24[:, h, 8 * r:8 * r + 8], self.CAND[:, h, :])
                        link(last)
                        if r < 2:
                            for h in heads:
                                last = dve.match_replace(out=self.CAND[:, h, :], in_to_replace=self.T24[:, h, 8 * r:8 * r + 8],
                                                         in_values=self.CAND[:, h, :], imm_value=LOWEST)
                            link(last)
                    cut = self.CUT[:, t, :].unsqueeze(2)
                    link(dve.tensor_tensor(cut, self.T24[:, :, 15:16], self.T24[:, :, 16:17], ALU.add))
                    link(dve.tensor_scalar(cut, cut, 0.5, None, ALU.mult))
                    link(dve.tensor_scalar(self.T24[:, :, 0:1], self.T24[:, :, 0:1], -80.0, None, ALU.add))
                    link(dve.tensor_tensor(cut, cut, self.T24[:, :, 0:1], ALU.max))
                    dve.tensor_scalar(cut, cut, -1.0, None, ALU.mult).then_inc(s["out_done"], 1)

    def load_heads(self, sp, g, sem):
        for j in range(2):
            sp.dma_start(self.TABLES[j], self.dram["tables"][bass.ds(2 * g + j, 1)].rearrange("o p c -> (o p) c")).then_inc(sem, 16)
            sp.dma_start(self.HWH[j], self.dram["head_weights"][bass.ds(2 * g + j, 1)].rearrange("o p c -> (o p) c")).then_inc(sem, 16)

    def key_scores(self):
        s = self.s
        QM = [self.ZS, self.KT[:, 0:L]]
        units = [(j, h) for j in range(2) for h in range(2)]
        cols = lambda h: slice(h * HALF, h * HALF + HALF)
        part = lambda u, k: self.SPLIT[:, u, k, :]
        rest = lambda u: self.GB.rearrange("p a l -> p (a l)")[:, HALF * u:HALF * u + HALF]
        with self.block() as block:
            @block.tensor
            def _(pe):
                for u, (j, h) in enumerate(units):
                    pe.matmul(self.bank(4 + u)[0:128, 0:HALF], self.HWH[j][:, 0:2 * D], self.XT[:, cols(h)],
                              start=True, stop=True).then_inc(s["prod_ready"], 1)
                for u, (j, h) in enumerate(units):
                    out, hw = self.bank(u)[0:128, 0:HALF], self.HWH[j]
                    pe.wait_ge(s["turned_d"], u + 1)
                    pe.matmul(out, hw[:, 3 * D:5 * D], QM[j][:, cols(h)], start=True, stop=False)
                    pe.matmul(out, hw[0:PKH, 5 * D:7 * D], self.CUTT[:, cols(h)], start=False, stop=True)\
                      .then_inc(s["scores_ready"], 1)

            @block.scalar
            def _(act):
                for u, (j, h) in enumerate(units):
                    act.wait_ge(s["turned_d"], u + 1)
                    act.activation(self.AQ[j][0:D, cols(h)], QM[j][0:D, cols(h)], ACT.Copy).then_inc(s["turned_a"], 1)
                for u in range(4):
                    act.wait_ge(s["scores_ready"], u + 1)
                    act.activation(part(u, 0), self.bank(u)[0:128, 0:HALF], ACT.Copy).then_inc(s["copied_a"], 1)
                for u in range(4):
                    act.wait_ge(s["copied_d"], u + 1)
                    act.activation(part(u, 1), rest(u), ACT.Copy).then_inc(s["exp_ready"], 1)

            @block.vector
            def _(dve):
                for u, (j, h) in enumerate(units):
                    dve.wait_ge(s["prod_ready"], u + 1)
                    dve.tensor_copy(QM[j][:, cols(h)], self.bank(4 + u)[0:128, 0:HALF]).then_inc(s["turned_d"], 1)
                for u in range(4):
                    dve.wait_ge(s["copied_a"], u + 1)
                    dve.tensor_tensor(rest(u), self.bank(u)[0:128, 0:HALF], part(u, 0), ALU.subtract).then_inc(s["copied_d"], 1)
                for u in range(4):
                    dve.wait_ge(s["exp_ready"], u + 1)
                    dve.tensor_tensor(part(u, 2), rest(u), part(u, 1), ALU.subtract).then_inc(s["out_done"], 1)

    def key_pair(self, g):
        s = self.s
        self.key_scores()
        NC = NK // 2
        N = 4 * NC
        GBF = self.GB.rearrange("p a l -> p (a l)")
        E = lambda n: GBF[:, HALF * (n % 4):HALF * (n % 4) + HALF]
        PK = lambda n: GBF[:, HALF * (4 + n % 4):HALF * (4 + n % 4) + HALF]
        Z = lambda n: self.bank(n % 4)[0:128, 0:HALF]
        KV = lambda u: self.bank(4 + u % 2)[0:128, 0:HALF]
        SUM = lambda u: self.bank(6 + u % 2)[0:128, 0:HALF]
        cols = lambda u: slice((u % 2) * HALF, (u % 2) * HALF + HALF)
        ahead, lag = 3, 3
        with self.block() as block:
            @block.tensor
            def _(pe):
                def total(u):
                    pe.wait_ge(s["sum_ready"], NC * (u + 1))
                    pe.matmul(SUM(u), self.ONE, self.ZS[:, cols(u)], start=True, stop=True).then_inc(s["kv_ready"], 1)

                for n in range(N + ahead):
                    if n < N:
                        if n >= 4:
                            pe.wait_ge(s["picked"], n - 3)
                        for k in range(3):
                            last = pe.matmul(Z(n), self.PICK[:, 128 * (n % NC):128 * (n % NC) + 128], self.SPLIT[:, n // NC, k, :],
                                             start=(k == 0), stop=(k == 2))
                        last.then_inc(s["dense_ready"], 1)
                    m = n - ahead
                    if m >= 0:
                        c, u = m % NC, m // NC
                        if c == 0 and u >= 2:
                            pe.wait_ge(s["out_done"], u - 1)
                        pe.wait_ge(s["picked"], m + 1)
                        pe.matmul(KV(u), self.TABLES[u // 2][:, 128 * c:128 * c + 128], PK(m),
                                  start=(c == 0), stop=(c == NC - 1)).then_inc(s["pv_ready"], 1)
                        if u and c == lag:
                            total(u - 1)
                total(3)

            @block.scalar
            def _(act):
                for n in range(N):
                    act.wait_ge(s["dense_ready"], n + 1)
                    if n >= 4:
                        act.wait_ge(s["picked"], n - 3)
                    act.activation(E(n), Z(n), ACT.Exp).then_inc(s["exp_ready"], 1)

            @block.vector
            def _(dve):
                link = self.chain(dve, s["step_dve"])

                def finish(u):
                    dve.wait_ge(s["kv_ready"], u + 1)
                    link(dve.reciprocal(self.RZ, SUM(u)))
                    dve.tensor_tensor(self.KVP[u // 2][:, cols(u)], KV(u), self.RZ, ALU.mult).then_inc(s["out_done"], 1)

                for n in range(N):
                    dve.wait_ge(s["exp_ready"], n + 1)
                    if n >= 4:
                        dve.wait_ge(s["pv_ready"], n - 3)
                        dve.wait_ge(s["sum_ready"], n - 3)
                    dve.scalar_tensor_tensor(PK(n), Z(n), 0.0, E(n), ALU.is_ge, ALU.mult).then_inc(s["picked"], 1)
                    if n >= NC and n % NC == lag + ahead:
                        if n >= 2 * NC:
                            dve.wait_ge(s["out_done"], n // NC - 1)
                        finish(n // NC - 1)
                dve.wait_ge(s["out_done"], 3)
                finish(3)

            @block.gpsimd
            def _(pool):
                for n in range(N):
                    c, u = n % NC, n // NC
                    pool.wait_ge(s["picked"], n + 1)
                    z = self.ZS[:, cols(u)]
                    if c == 0:
                        if u >= 2:
                            pool.wait_ge(s["kv_ready"], u - 1)
                        pool.tensor_copy(z, PK(n)).then_inc(s["sum_ready"], 1)
                    else:
                        pool.wait_ge(s["sum_ready"], n)
                        pool.tensor_tensor(z, z, PK(n), ALU.add).then_inc(s["sum_ready"], 1)
        self.project([("t", self.HWH[j][:, 2 * D:3 * D], self.KVP[j], self.VP[j], None) for j in range(2)])
        self.softmax_attention([(self.AQ[j], self.KVP[j], self.VP[j], self.H, self.H) for j in range(2)], float(D) ** -0.5, True,
                               lambda sp: self.load_heads(sp, g + 1, s["loaded"]), 64)

    def product_keys(self):
        s = self.s
        self.norm(self.H, self.X, NT, D, 1e-5)
        self.turn(self.X, self.XT)
        self.pair_cuts()
        self.turn(self.CUT, self.CUTT, rows=PKH)
        with self.block() as block:
            @block.gpsimd
            def _(pool):
                for j in range(2):
                    pool.memset(self.AQ[j][D:128, :], 0.0).then_inc(s["step_pool"], 1)

            @block.vector
            def _(dve):
                eye = self.w("ident")
                dve.tensor_copy(self.PICK[0:NK, :].rearrange("p (a b) -> p a b", b=NK),
                                eye[0:NK, 0:NK].unsqueeze(2).broadcast_to((NK, NK, NK))).then_inc(s["step_dve"], 1)
                dve.tensor_copy(self.PICK[NK:128, :].rearrange("p (a b) -> p a b", b=NK),
                                eye[NK:128, NK:128].unsqueeze(1).broadcast_to((NK, NK, NK))).then_inc(s["step_dve"], 1)
        with self.nc.Fori(0, PKH // 2) as g:
            self.key_pair(g)

    def inner_layer(self, l):
        s, W = self.s, self.LW
        dh = D // 8
        scale = float(dh) ** -0.25
        with self.block() as block:
            @block.sync
            def _(sp):
                sp.dma_start(W, self.dram["layers"][bass.ds(l, 1)].rearrange("o p c -> (o p) c")).then_inc(s["loaded"], 16)
                sp.wait_ge(s["loaded"], 16)
        self.norm(self.R, self.X, NT, D, 1e-5, gamma=W[0:P, 704:768], beta=W[0:P, 768:832])
        self.turn(self.X, self.XT)
        xt = self.XT[:, 0:L]
        self.project([("t", W[:, 0:64], xt, self.A, None), ("c", W[:, 64:128], xt, self.KT, None),
                      ("t", W[:, 128:192], xt, self.V, None)])
        self.softmax_block(self.A.rearrange("p t (h d) -> p (t h) d", d=dh), NT * 8, dh, scale=scale)
        self.turn(self.A, self.C1)
        KM, KT = self.KM, self.KT[0:D, 0:L]
        with self.block() as block:
            @block.vector
            def _(dve):
                link = self.chain(dve, s["step_dve"])
                link(dve.tensor_reduce(KM[:, 0:1], KT, AX.X, ALU.max))
                dve.tensor_scalar(KM[:, 1:2], KM[:, 0:1], -scale, None, ALU.mult).then_inc(s["max_ready"], 1)
                dve.wait_ge(s["exp_ready"], 1)
                link(dve.reciprocal(KM[:, 3:4], KM[:, 2:3]))
                dve.wait_ge(s["turned"], 1)
                dve.tensor_copy(self.Y, self.bank(0)[0:P, 0:NT * D].rearrange("p (t d) -> p t d", d=D)).then_inc(s["copied_d"], 1)
                dve.wait_ge(s["prod_ready"], 1)
                dve.tensor_tensor(self.CT, self.bank(1)[0:D, 0:D], self.w("blocks8"), ALU.mult).then_inc(s["mask_ready"], 1)
                dve.wait_ge(s["prod_ready"], 2)
                dve.tensor_scalar(self.CW[0:D, :], self.bank(2)[0:D, 0:D], KM[:, 3:4], None, ALU.mult).then_inc(s["out_done"], 1)
                dve.tensor_copy(self.CW[D:D + 1, :], W[D:D + 1, 192:256]).then_inc(s["out_done"], 1)

            @block.scalar
            def _(act):
                act.wait_ge(s["max_ready"], 1)
                act.activation(KT, KT, ACT.Exp, bias=KM[:, 1:2], scale=scale, accum_out=KM[:, 2:3]).then_inc(s["exp_ready"], 1)

            @block.tensor
            def _(pe):
                pe.wait_ge(s["exp_ready"], 1)
                for t in range(NT):
                    last = pe.transpose(self.bank(0)[0:P, D * t:D * t + D], KT[:, P * t:P * t + P], self.w("ident")[0:D, 0:D])
                last.then_inc(s["turned"], 1)
                pe.wait_ge(s["copied_d"], 1)
                for t in range(NT):
                    last = pe.matmul(self.bank(1)[0:D, 0:D], self.V[:, t, :], self.Y[:, t, :], start=(t == 0), stop=(t == NT - 1))
                last.then_inc(s["prod_ready"], 1)
                pe.wait_ge(s["mask_ready"], 1)
                pe.matmul(self.bank(2)[0:D, 0:D], self.CT, W[0:D, 192:256], start=True, stop=True).then_inc(s["prod_ready"], 1)
        self.project([("t", self.CW, self.C1[0:D + 1, :], self.A, None)])
        self.add(self.R, self.R, self.A)
        self.norm(self.R, self.X, NT, D, 1e-5, gamma=W[0:P, 832:896], beta=W[0:P, 896:960])
        self.turn(self.X, self.XT)
        self.mixture(self.R, False, 128, lambda e, c: (W[:, 256 + 128 * c:384 + 128 * c],),
                     lambda e, c: W[:, 512 + D * c:576 + D * c], (W[:, 640:704], self.XT), 1, False)

    def inner_transformer(self):
        self.norm(self.H, self.R, NT, D, 1e-5)
        with self.nc.Fori(0, DEPTH) as l:
            self.inner_layer(l)
        self.add(self.H, self.H, self.R)

    def last_part(self):
        s = self.s
        self.norm(self.H, self.R, NT, D, 1e-5)
        self.norm(self.R, self.X, NT, D, 1e-6, center=False, gamma=self.w("f3_1"))
        self.turn(self.X, self.XT)
        xt = self.XT[:, 0:L]
        qs, ks = self.ZS, self.KVT
        self.project([("c", self.wx("f3_q"), xt, self.QT, None), ("c", self.wx("f3_qs"), xt, qs, None),
                      ("c", self.wx("f3_k"), xt, self.KT, None), ("c", self.wx("f3_ks"), xt, ks, None),
                      ("t", self.wx("f3_v")[:, 0:HD], xt, self.VN[:, :, 0:HD], None),
                      ("t", self.wx("f3_v")[:, HD:2 * HD], xt, self.VN[:, :, 32:32 + HD], None)])
        self.zero(self.GB)
        with self.block() as block:
            @block.vector
            def _(dve):
                link = self.chain(dve, s["step_dve"])
                for x, sw in ((self.QT[:, 0:L], qs), (self.KT[:, 0:L], ks)):
                    link(dve.tensor_tensor(x, x, self.w("cos4"), ALU.mult))
                    link(dve.tensor_tensor(sw, sw, self.w("sin4"), ALU.mult))
                    if sw is ks:
                        link(dve.tensor_tensor(x, x, sw, ALU.add))
                    else:
                        for h in range(NH):
                            rows = slice(32 * h, 32 * h + HD)
                            link(dve.tensor_tensor(self.GB[rows, h, :], x[rows, :], sw[rows, :], ALU.add))
        self.softmax_attention([(self.GB[:, h, :], self.KT[:, 0:L], self.VN[:, :, 32 * (h // 2):32 * (h // 2) + 32],
                                 self.A[:, :, HD * h:HD * h + HD], None) for h in range(NH)], float(HD) ** -0.5, True)
        self.turn(self.A, self.C1)
        self.project([("t", self.wx("f3_o"), self.C1, self.A, None)])
        self.add(self.R, self.R, self.A)
        self.norm(self.R, self.X, NT, D, 1e-6, center=False, gamma=self.w("f3_2"))
        self.turn(self.X, self.XT)
        self.project([("t", self.wx("f3_r"), self.XT[:, 0:L], self.RT, None)])
        self.softmax_block(self.RT, NT, 8)
        self.top_two(self.RT, self.GT, 1e-9)
        self.turn_gates()
        w1, w3, w2, ch = self.wx("f3_w1"), self.wx("f3_w3"), self.wx("f3_w2"), F3 // 2
        up = lambda w, e, c: w[:, F3 * e + ch * c:F3 * e + ch * c + ch]
        self.mixture(self.R, True, ch, lambda e, c: (up(w1, e, c), up(w3, e, c)),
                     lambda e, c: w2[:, D * (2 * e + c):D * (2 * e + c) + D], None, E3, True)
        self.add(self.H, self.H, self.R)


def build(nc, where, dram, out, stages=99, bench=None):
    ctx = ExitStack()
    with ctx:
        t = Tower(nc, ctx, where, dram)
        s = t.s
        t.VO = t.sb("a0_vo", [D, D])
        t.RT = t.sb("router", [P, NT, 8])
        t.GT = t.sb("gates", [P, NT, 8])
        t.TOP = t.sb("top", [P, 8 * NT])
        t.TOPF = t.sb("top_at", [P, 8 * NT])
        t.IDX = t.sb("top_index", [P, 8 * NT], U32)
        t.GB = t.sb("hidden", [128, 4, L])
        t.HA = t.sb("h_all", [P, NSEQ, NT * D])
        STREAM = NK // 2 * 128
        t.TABLES = [t.sb(f"tables_{i}", [128, STREAM]) for i in range(2)]
        t.X9 = t.TABLES[0][0:P, 0:NT * WIN * D].rearrange("p (t c) -> p t c", t=NT)
        t.TRIG, t.MP, t.MV, t.MS, t.ONES = (t.TABLES[1][:, i * L:(i + 1) * L] for i in range(5))
        t.AQ = [t.sb(f"attention_queries_{i}", [128, L]) for i in range(2)]
        t.G1 = t.AQ[0][0:HD + 1, :]
        t.ONE = t.sb("ones_square", [128, 128])
        t.HWH = [t.sb(f"key_head_weights_{i}", [128, 7 * D]) for i in range(2)]
        t.V16 = t.sb("key_scores_top", [P, 2 * PKH, 17])
        t.CAND = t.sb("pair_scores", [P, PKH, PAIRED])
        t.T24 = t.sb("pair_scores_top", [P, PKH, 24])
        t.CUT = t.sb("pair_cut", [P, NT, PKH])
        t.CUTT = t.sb("pair_cut_turned", [PKH, L])
        t.PICK = t.sb("pair_of_keys", [128, STREAM], BF16)
        t.SPLIT = t.sb("score_parts", [128, 4, 3, HALF], BF16)
        t.RZ = t.sb("pair_sum_reciprocal", [128, HALF])
        t.ZS = t.sb("pair_sums", [128, L])
        t.KVT = t.sb("picked_kv", [128, L])
        t.KVP = [t.KVT, t.sb("picked_kv_1", [128, L])]
        t.VP = [t.V, t.sb("v_1", [P, NT, D])]
        t.LW = t.sb("layer_weights", [128, 960])
        t.R = t.sb("inner_stream", [P, NT, D])
        t.KM = t.sb("key_stats", [D, 4])
        t.CT = t.sb("context_t", [D, D])
        t.CW = t.sb("context_out", [D + 1, D])
        t.C1 = t.sb("hidden_1", [128, L])
        t.C2 = t.sb("hidden_2", [128, L])
        t.GL2 = t.sb("gate_two", [P, NT, 2])
        t.GL2b = t.sb("gate_heads", [P, NT, NH])
        t.GL = t.sb("gate_experts", [P, NT, NH * NE])
        t.SX = t.sb("head_inputs", [P, NT, D])
        t.RES = t.sb("head_residuals", [P, NH, NT, HD])
        t.HW1 = t.sb("head_weights", [128, 288])
        t.SN = t.ZS
        t.GATES = t.ZS
        t.VN = t.sb("head_values", [P, NT, 64])
        t.QN = t.R
        t.QKV = t.PT.rearrange("p a l -> p (a l)")[0:P, 3 * L:3 * L + NT * NH * D].rearrange("p (t n f) -> p t n f", t=NT, n=NH)
        with t.block() as block:
            @block.sync
            def _(sp):
                first = dram["pack_0"].shape[1]
                sp.dma_start(t.W[:, 0:first], dram["pack_0"]).then_inc(s["loaded"], 16)
                sp.dma_start(t.W[:, first:first + dram["pack_1"].shape[1]], dram["pack_1"]).then_inc(s["loaded"], 16)

            @block.gpsimd
            def _(pool):
                link = t.chain(pool, s["step_pool"])
                for rows in (t.XT[D:128, :], t.C1[D:128, :], t.C2[D:128, :], t.G1, t.ONES, t.ONE):
                    link(pool.memset(rows, 1.0))

            @block.vector
            def _(dve):
                dve.wait_ge(s["loaded"], 32)
                dve.tensor_copy(t.identb[:, :], t.w("ident")[0:P, 0:P]).then_inc(s["step_dve"], 1)
                dve.tensor_copy(t.laterb[:, :], t.w("later")).then_inc(s["step_dve"], 1)
                dve.wait_ge(s["prod_ready"], 1)
                dve.tensor_copy(t.VO[:, :], t.bank(0)[0:D, 0:D]).then_inc(s["step_dve"], 1)

            @block.tensor
            def _(pe):
                pe.wait_ge(s["loaded"], 32)
                pe.matmul(t.bank(0)[0:D, 0:D], t.w("a0_v"), t.w("a0_o"), start=True, stop=True).then_inc(s["prod_ready"], 1)

        if bench is not None:
            return bench(t)
        t.phase_tables()

        def store(b):
            with t.block() as block:
                @block.sync
                def _(sp):
                    sp.dma_start(out[bass.ds(b, 1)].rearrange("o (t p) d -> (o p) t d", p=P), t.H[:, :, :]).then_inc(s["stored"], 16)
                    sp.wait_ge(s["stored"], 16)

        with nc.Fori(0, NSEQ) as b:
            t.window_pool(b)
            if stages >= 2:
                t.relu_attention()
            if stages >= 3:
                t.first_mixture()
            if stages >= 4:
                t.memory()
            if stages >= 5:
                t.head_inputs()
                t.keep_sequence(b)
            else:
                store(b)
        if stages >= 5:
            with t.block() as block:
                @block.gpsimd
                def _(pool):
                    link = t.chain(pool, s["step_pool"])
                    link(pool.memset(t.VN, 0.0))

            with t.block() as block:
                @block.sync
                def _(sp):
                    first = dram["pack_0"].shape[1]
                    sp.dma_start(t.W[:, first:first + dram["pack_2"].shape[1]], dram["pack_2"]).then_inc(s["loaded"], 16)
                    t.load_heads(sp, 0, s["loaded"])
                    sp.wait_ge(s["loaded"], 80)
            with nc.Fori(0, NSEQ) as b:
                t.fetch_sequence(b)
                t.expert_heads()
                if stages >= 6:
                    t.plain_attention()
                if stages >= 7:
                    t.product_keys()
                if stages >= 8:
                    t.inner_transformer()
                if stages >= 9:
                    t.last_part()
                store(b)


def kernel(**inputs):
    import concourse.bacc as bacc
    from concourse.bass_utils import run_bass_kernel_spmd

    where, arrays = layout(inputs)
    nc = bacc.Bacc("TRN2", target_bir_lowering=False, num_devices=1)
    dram = {k: nc.dram_tensor(f"in_{k}", a.shape, F32, kind="ExternalInput").ap() for k, a in arrays.items()}
    out = nc.dram_tensor("out", (NSEQ, L, D), F32, kind="ExternalOutput").ap()
    build(nc, where, dram, out)
    r = run_bass_kernel_spmd(nc, [{f"in_{k}": a for k, a in arrays.items()}], core_ids=[0])
    return r.results[0]["out"]
```

```python
import numpy as np
from contextlib import ExitStack, contextmanager

import concourse.bass as bass
from concourse import mybir

F32 = mybir.dt.float32
BF16 = mybir.dt.bfloat16
U32 = mybir.dt.uint32
ALU = mybir.AluOpType
ACT = mybir.ActivationFunctionType
AX = mybir.AxisListType

NSEQ, LIN, WIN, D = 4, 750, 9, 64
L = LIN - WIN + 1
STEPS = (WIN + 1) // 2
P, NT = 106, 7
HALF = L // 2
assert P * NT == L
NEG = -1e30
E0, F0 = 8, 256
NH, NE, HD = 4, 4, 16
PKH, PKD, NK = 8, 32, 64
E3, F3 = 8, 170
DEPTH = 4
RUNS = [(0, 16), (1, 8), (2, 5), (3, 4), (4, 3)]
PAIRED = 52
LOWEST = -3.0e38
PI_DOWN = 3.1415925


def _spread(a):
    rows, heads = a.shape[0], a.shape[1] // HD
    out = np.zeros((rows, heads, 32), np.float32)
    out[:, :, :HD] = a.reshape(rows, heads, HD)
    return out.reshape(rows, heads * 32)


def _rows(v, n=P):
    return np.ascontiguousarray(np.broadcast_to(np.asarray(v).reshape(1, -1), (n, np.asarray(v).size)))


def _block_diagonal(blocks):
    r, c = blocks[0].shape
    out = np.zeros((r * len(blocks), c * len(blocks)), np.float32)
    for i, b in enumerate(blocks):
        out[i * r:(i + 1) * r, i * c:(i + 1) * c] = b
    return out


def constants():
    pos = np.arange(L)
    tiles = lambda v: v.reshape(NT, P).T.astype(np.float32)
    k, q = np.meshgrid(np.arange(P), np.arange(P), indexing="ij")
    inv = 1.0 / 10000.0 ** (np.arange(0, HD, 2, dtype=np.float32) / HD)
    f = np.outer(np.arange(L, dtype=np.float32), inv)
    f = np.concatenate([f, f], -1)
    sign = np.where(np.arange(HD) < HD // 2, -1.0, 1.0)
    four = lambda t: np.ascontiguousarray(_spread(np.tile(t, (1, 4))).T).astype(np.float32)
    return {
        "ident": np.eye(128, dtype=np.float32),
        "later": np.where(q > k, NEG, 0.0).astype(np.float32),
        "keep_t": (q >= k).astype(np.float32),
        "inv_row": tiles(1.0 / np.maximum(pos.astype(np.float32), 1.0)),
        "inv_pos": tiles(1.0 / np.sqrt((pos + 1).astype(np.float32))),
        "inv_pos32": tiles(1.0 / np.sqrt(((pos + 1) * 32).astype(np.float32))),
        "half_pi": np.full((128, 1), np.pi / 2, np.float32),
        "experts": _rows(np.tile(np.arange(8, dtype=np.float32), NT)),
        "two_eyes": np.concatenate([np.eye(64), np.eye(64)]).astype(np.float32),
        "four_eyes": np.tile(np.eye(32, HD), (4, 1)).astype(np.float32),
        "blocks8": np.kron(np.eye(8), np.ones((8, 8))).astype(np.float32),
        "cos4": four(np.cos(f)),
        "sin4": four(np.sin(f) * sign),
    }


def layout(i):
    i = {k: np.asarray(v) for k, v in i.items()}
    cat = np.concatenate
    aug = lambda w, b: cat([w, b.reshape(1, -1)], 0)
    w = dict(constants())
    tq = aug(i["L0_tok_W_qry"], i["L0_tok_b"])
    w["tok_q"] = cat([tq, tq], 1)
    w["tok_k"] = cat([i["L0_tok_W_key"]] * 2, 1)
    tv = np.zeros((2, D, STEPS, WIN), np.float32)
    for r in range(WIN):
        tv[r % 2, :, r // 2, r] = np.asarray(i["L0_tok_v"]).reshape(D)
    w["tok_v"] = tv.reshape(2 * D, STEPS * WIN)
    w["a0_q"], w["a0_k"], w["a0_v"], w["a0_o"] = i["L0_attn_Wq"].T, i["L0_attn_Wk"].T, i["L0_attn_Wv"], i["L0_attn_Wo"].T
    w["m0_r"] = i["L0_ffn_Wr"]
    w1 = cat([i["L0_ffn_W1p"], i["L0_ffn_W1s"][None]], 0)
    b1 = cat([i["L0_ffn_b1p"], i["L0_ffn_b1s"][None]], 0)
    w["m0_w1"] = cat([w1, b1[:, None]], 1).transpose(1, 0, 2).reshape(D + 1, -1)
    w2 = cat([i["L0_ffn_W2p"], i["L0_ffn_W2s"][None]], 0)
    w["m0_w2"] = w2.reshape(E0 + 1, 2, 128, D).transpose(2, 0, 1, 3).reshape(128, -1)
    w["m0_b2"] = cat([i["L0_ffn_b2p"], i["L0_ffn_b2s"][None]], 0)
    for n in "kq":
        w[f"h1_{n}1"] = aug(i[f"L1_attn_W{n}1"], i[f"L1_attn_b{n}1"])
        one = aug(i[f"L1_attn_W{n}2"], i[f"L1_attn_b{n}2"])
        w[f"h1_{n}2"] = cat([one, one], 1)
    w["h1_vc"] = aug(i["L1_attn_Wvc"], i["L1_attn_bvc"])
    vp = aug(i["L1_attn_Wvp"], i["L1_attn_bvp"])
    w["h1_vp"] = cat([vp, vp], 1)
    w["h1_g1"] = aug(i["L1_attn_Wg1"], i["L1_attn_bg1"])
    w["h1_g2"] = aug(i["L1_attn_Wg2"], i["L1_attn_bg2"])
    w["h1_g"], w["h1_b"] = _rows(i["L1_attn_ln_g"]), _rows(i["L1_attn_ln_b"])
    w["h1_o"] = aug(i["L1_attn_Wo"], i["L1_attn_bo"])
    ph = i["L1_attn_base_phases"][:L].T
    w["phases"] = cat([ph, ph], 0)
    hl = aug(i["L1_ffn_hl_w"].reshape(D, D).T, i["L1_ffn_hl_b"])
    w["f1_hl"] = hl
    heads = []
    for n in range(NH):
        q4 = _spread(cat([i["L1_ffn_wq"][n, e].T for e in range(NE)], 1))
        k4 = _spread(np.tile(i["L1_ffn_wk"][n].T, (1, NE)))
        own = np.zeros((D, 2 * 128 + 32), np.float32)
        own[HD * n:HD * n + HD, :2 * 128 + HD] = cat([q4, k4, i["L1_ffn_wv"][n].T], 1)
        heads.append(own)
    w["f1_heads"] = cat(heads, 1)
    gw = [i["L1_ffn_gate_w"][n].T for n in range(NH)]
    w["f1_gate"] = cat([_block_diagonal(gw[:2]), _block_diagonal(gw[2:])], 1)
    w["f1_gate_b"] = _rows(i["L1_ffn_gate_b"])
    w["f1_g"], w["f1_b"] = _rows(i["L1_ffn_ln_g"]), _rows(i["L1_ffn_ln_b"])
    w["f1_fg"], w["f1_fb"] = _rows(i["L1_ffn_fnorm_g"]), _rows(i["L1_ffn_fnorm_b"])
    for n in "12":
        w[f"f1_fc{n}"] = aug(_block_diagonal([i[f"L1_ffn_fc{n}_w"].T] * NH), np.tile(i[f"L1_ffn_fc{n}_b"], NH))
    w["f1_fgate"] = i["L1_ffn_fgate_w"].T
    w["a2_q"], w["a2_k"] = i["L2_attn_Wq"].T, i["L2_attn_Wk"].T
    pkq, keys = i["L2_ffn_Wq_pk"], i["L2_ffn_pk_keys"]
    w["pk_q"] = pkq
    w["pk_keys"] = cat([_block_diagonal([keys[p, :, h].T for h in range(4 * g, 4 * g + 4)]) for p in range(2) for g in range(2)], 1)
    w["f3_1"], w["f3_2"] = _rows(i["L3_ffn_ln1_w"]), _rows(i["L3_ffn_ln2_w"])
    swap = (np.arange(HD) + HD // 2) % HD
    wq = i["L3_ffn_wq"].T.reshape(D, NH, HD)
    wk = np.repeat(i["L3_ffn_wk"].T.reshape(D, NH // 2, HD), 2, 1)
    for name, m in (("q", wq), ("k", wk)):
        w[f"f3_{name}"] = _spread(m.reshape(D, -1))
        w[f"f3_{name}s"] = _spread(m[:, :, swap].reshape(D, -1))
    w["f3_v"] = i["L3_ffn_wv"].T
    w["f3_o"] = i["L3_ffn_wo"].T
    w["f3_r"] = i["L3_ffn_router_w"].T
    w["f3_w1"] = i["L3_ffn_w1"].transpose(2, 0, 1).reshape(D, -1)
    w["f3_w3"] = i["L3_ffn_w3"].transpose(2, 0, 1).reshape(D, -1)
    w["f3_w2"] = i["L3_ffn_w2"].transpose(0, 2, 1).reshape(E3, 2, F3 // 2, D).transpose(2, 0, 1, 3).reshape(F3 // 2, -1)
    loop_of = lambda k: (1 if k[:3] in ("tok", "a0_", "m0_", "h1_", "pha") else
                         2 if k[:3] in ("a2_", "pk_", "f3_") or k in ("f1_heads", "f1_gate", "cos4", "sin4") else 0)
    where, packs, shared = {}, [], 0
    for part in range(3):
        names = [k for k in w if loop_of(k) == part]
        at = 0
        pack = np.zeros((128, sum(w[k].shape[1] for k in names)), np.float32)
        for k in names:
            r, c = w[k].shape
            pack[:r, at:at + c] = w[k]
            where[k] = (r, shared + at, c)
            at += c
        packs.append(pack)
        shared = packs[0].shape[1]
    pq = pkq.reshape(D, 2, PKH, PKD)
    hw = np.zeros((PKH, 128, 7 * D), np.float32)
    for h in range(PKH):
        hw[h, :D, :D] = i["L2_ffn_Wq"][:, h * D:h * D + D]
        hw[h, :D, D:2 * D] = pq[:, :, h].reshape(D, D)
        hw[h, D:, 2 * D:3 * D] = i["L2_ffn_Wo"][h * D:h * D + D]
        hw[h, D:D + PKD, 3 * D:4 * D] = keys[0, :, h].T
        hw[h, D + PKD:, 4 * D:5 * D] = keys[1, :, h].T
        hw[h, h, 5 * D:6 * D] = 1.0
    kv = cat([i["L2_ffn_keys_table"], i["L2_ffn_values_table"]], 1).reshape(PKH, NK, NK // 2, 2, 2 * D)
    tables = np.ascontiguousarray(kv.transpose(0, 3, 1, 2, 4)).reshape(PKH, 128, (NK // 2) * 2 * D)
    wrap = lambda a: cat([a, a[:2]], 0)
    lw = np.zeros((DEPTH, 128, 3 * D + D + 4 * D + 2 * D + D + 4 * D), np.float32)
    for l in range(DEPTH):
        at = 0
        for a in (i["L3_attn_Wq"][l], i["L3_attn_Wk"][l], i["L3_attn_Wv"][l], aug(i["L3_attn_Wo"][l], i["L3_attn_bo"][l]),
                  aug(i["L3_attn_W1"][l], i["L3_attn_b1"][l]),
                  i["L3_attn_W2"][l].reshape(2, 128, D).transpose(1, 0, 2).reshape(128, -1), aug(np.zeros((D, D), np.float32), i["L3_attn_b2"][l]),
                  _rows(i["L3_attn_ln1_g"][l]), _rows(i["L3_attn_ln1_b"][l]), _rows(i["L3_attn_ln2_g"][l]), _rows(i["L3_attn_ln2_b"][l])):
            lw[l, :a.shape[0], at:at + a.shape[1]] = a
            at += a.shape[1]
    return where, {"x": cat([i["x"], i["x"][:1]], 0), "pack_0": packs[0], "pack_1": packs[1], "pack_2": packs[2], "head_weights": wrap(hw),
                   "tables": wrap(tables), "layers": cat([lw, lw[:1]], 0)}


SEMS = ["step_dve", "step_pool", "step_act", "loaded", "windows_loaded", "stored", "var_ready", "std_ready",
        "normed", "turned_copied_a", "turned_copied_d", "turned", "copied_a",
        "copied_d", "scores_ready", "max_ready", "probs_ready", "probs_turned",
        "turned_a", "turned_d", "pv_ready", "out_done", "hidden_ready", "hidden_act", "hidden_used", "prod_ready",
        "sum_ready", "sum_even", "sum_odd", "tanh_ready", "phase_ready", "mask_ready", "exp_ready", "picked",
        "kv_ready", "queries_copied", "attention_queries_copied", "first_part", "rest_ready", "second_part",
        "third_part", "sides_ranked", "candidates_ready", "pairs_ranked", "reciprocals_ready", "totals_ready",
        "pair_scores_ready", "weights_copied", "queries_turned", "queries_copied_act", "centred",
        "queries_exp_ready", "keys_turned", "keys_copied"]


class Semaphores:

    def __init__(self, nc, ctx):
        self.sets = [{n: ctx.enter_context(nc.semaphore(f"{n}_{i}")) for n in SEMS} for i in range(2)]
        self.turn = 0

    def __getitem__(self, name):
        return self.sets[self.turn][name]

    def numbers(self):
        return [s.num for s in self.sets[self.turn].values()]


class Tower:

    def __init__(self, nc, ctx, where, dram):
        self.nc, self.ctx, self.where, self.dram = nc, ctx, where, dram
        self.s = Semaphores(nc, ctx)
        self.columns = max(o + c for _, o, c in where.values())
        self.W = self.sb("weights", [128, self.columns])
        self.PS = ctx.enter_context(nc.psum_tensor("psum", [128, 8 * 512], F32))
        self.H = self.sb("h", [P, NT, D])
        self.X = self.sb("xn", [P, NT, D])
        self.XT = self.sb("xt", [128, LIN])
        self.QT = self.sb("qt", [128, LIN])
        self.KT = self.sb("kt", [128, LIN])
        self.V = self.sb("v", [P, NT, D])
        self.Y = self.sb("y", [P, NT, D])
        self.A = self.sb("a", [P, NT, D])
        self.SQ = self.sb("sq", [P, NT, D])
        self.ST = self.sb("stat", [P, 128])
        self.ST2 = self.sb("stat2", [P, 128])
        self.PR = self.sb("probs", [P, 2, L])
        self.PT = self.sb("probs_t", [128, NT, L])
        self.NM = self.sb("neg_max", [P, 8])
        self.BN = self.sb("tile_statistics", [P, NT, 6])
        self.MEANVAR = self.sb("mean_variance", [P, NT, 2])
        self.RS = self.sb("row_sum", [P, 16])
        self.OTS = self.sb("out_turned", [128, 2, P])
        self.identb = self.sb("ident_bf16", [P, P], BF16)
        self.laterb = self.sb("later_bf16", [P, P], BF16)

    def sb(self, name, shape, dt=F32):
        return self.ctx.enter_context(self.nc.sbuf_tensor(name, shape, dt))[tuple(slice(0, n) for n in shape)]

    def w(self, name):
        r, o, c = self.where[name]
        return self.W[0:r, o:o + c]

    def wx(self, name):
        _, o, c = self.where[name]
        return self.W[:, o:o + c]

    def bank(self, n, m=1):
        return self.PS[:, 512 * n:512 * (n + m)]

    @contextmanager
    def block(self):
        last = self.s.numbers()
        self.s.turn = 1 - self.s.turn
        with self.nc.Block() as block:
            @block.gpsimd
            def _(pool):
                pool.sem_clear(range(min(last), max(last) + 1))
            yield block

    @contextmanager
    def loop(self, n):
        turn = self.s.turn
        with self.nc.Fori(0, n) as i:
            yield i
            if self.s.turn != turn:
                with self.block():
                    pass

    def chain(self, engine, sem):
        count = [0]

        def link(ins):
            count[0] += 1
            ins.then_inc(sem, 1)
            engine.wait_ge(sem, count[0])
        return link

    def norm(self, src, dst, groups, width, eps, center=True, gamma=None, beta=None, loads=None, turned=None, jobs=None):
        s = self.s
        stat, sq = self.ST[:, 0:groups], self.SQ.rearrange("p t d -> p (t d)").rearrange("p (g w) -> p g w", w=width)
        wide = lambda a: a.unsqueeze(2).broadcast_to((P, groups, width))
        over = lambda a: a.unsqueeze(1).broadcast_to((P, groups, width))
        by_tile = center and groups == NT
        scaled = gamma is not None or beta is not None
        with self.block() as block:
            if loads is not None:
                @block.sync
                def _(sp):
                    loads[0](sp)
                    sp.wait_ge(s["loaded"], loads[1])

            @block.vector
            def _(dve):
                link = self.chain(dve, s["step_dve"])
                if by_tile:
                    for t in range(NT):
                        last = dve.bn_stats(self.BN[:, t, :], src[:, t, :])
                    link(last)
                    for t in range(NT):
                        last = dve.bn_aggr(self.MEANVAR[:, t, :], self.BN[:, t, :])
                    link(last)
                    dve.tensor_scalar(stat.unsqueeze(2), self.MEANVAR[:, :, 1:2], eps, None, ALU.add).then_inc(s["var_ready"], 1)
                    dve.wait_ge(s["std_ready"], 1)
                    link(dve.reciprocal(stat, stat))
                    for t in range(NT):
                        last = dve.tensor_scalar(dst[:, t, :], src[:, t, :], self.MEANVAR[:, t, 0:1], stat[:, t:t + 1],
                                                 ALU.subtract, ALU.mult)
                        if not scaled:
                            last.then_inc(s["normed"], 1)
                    if scaled:
                        link(last)
                else:
                    at = src
                    if center:
                        link(dve.tensor_reduce(stat, src, AX.X, ALU.add))
                        link(dve.tensor_scalar(stat, stat, 1.0 / width, None, ALU.mult))
                        link(dve.tensor_tensor(dst, src, wide(stat), ALU.subtract))
                        at = dst
                    link(dve.tensor_tensor(sq, at, at, ALU.mult))
                    link(dve.tensor_reduce(stat, sq, AX.X, ALU.add))
                    dve.tensor_scalar(stat, stat, 1.0 / width, eps, ALU.mult, ALU.add).then_inc(s["var_ready"], 1)
                    dve.wait_ge(s["std_ready"], 1)
                    link(dve.reciprocal(stat, stat))
                    link(dve.tensor_tensor(dst, at, wide(stat), ALU.mult))
                if gamma is not None:
                    last = dve.tensor_tensor(dst, dst, over(gamma), ALU.mult)
                    if beta is not None:
                        link(last)
                        last = dve.tensor_tensor(dst, dst, over(beta), ALU.add)
                    last.then_inc(s["normed"], NT)
                if turned is not None:
                    dve.wait_ge(s["turned"], NT)
                    dve.tensor_copy(turned[0:D, 4 * P:L], self.bank(1)[0:D, 0:3 * P]).then_inc(s["turned_copied_d"], 1)

            @block.scalar
            def _(act):
                act.wait_ge(s["var_ready"], 1)
                act.activation(stat, stat, ACT.Sqrt).then_inc(s["std_ready"], 1)
                if turned is not None:
                    act.wait_ge(s["turned"], 4)
                    act.activation(turned[0:D, 0:4 * P], self.bank(0)[0:D, 0:4 * P], ACT.Copy).then_inc(s["turned_copied_a"], 1)

            if turned is not None:
                @block.tensor
                def _(pe):
                    for t in range(NT):
                        pe.wait_ge(s["normed"], NT if scaled else t + 1)
                        out = self.bank(t // 4)[0:D, P * (t % 4):P * (t % 4) + P]
                        pe.transpose(out, dst.rearrange("p g w -> p (g w)")[:, D * t:D * t + D], self.w("ident")[0:P, 0:P])\
                          .then_inc(s["turned"], 1)

            if jobs is not None:
                self.products(block, jobs, ("turned_copied_a", "turned_copied_d"))

    def turn(self, src, dst, rows=D):
        s = self.s
        with self.block() as block:
            @block.tensor
            def _(pe):
                for t in range(NT):
                    out = self.bank(t // 4)[0:rows, P * (t % 4):P * (t % 4) + P]
                    pe.transpose(out, src[:, t, :], self.w("ident")[0:P, 0:P]).then_inc(s["turned"], 1)

            @block.scalar
            def _(act):
                act.wait_ge(s["turned"], 4)
                act.activation(dst[0:rows, 0:4 * P], self.bank(0)[0:rows, 0:4 * P], ACT.Copy).then_inc(s["copied_a"], 1)

            @block.vector
            def _(dve):
                dve.wait_ge(s["turned"], NT)
                dve.tensor_copy(dst[0:rows, 4 * P:L], self.bank(1)[0:rows, 0:3 * P]).then_inc(s["copied_d"], 1)

    def project(self, jobs):
        with self.block() as block:
            self.products(block, jobs)

    def products(self, block, jobs, ready=()):
        s = self.s
        steps = []
        for kind, wt, src, dst, what in jobs:
            if kind == "c":
                m = wt.shape[1]
                for h in range(2):
                    steps.append(([(lambda b, m=m: b[0:m, 0:HALF], wt, src[:, h * HALF:(h + 1) * HALF])],
                                  lambda b, m=m: b[0:m, 0:HALF], dst[0:m, h * HALF:(h + 1) * HALF], what))
            else:
                m = wt.shape[1]
                mms = [(lambda b, t=t, m=m: b[0:P, t * m:(t + 1) * m], src[:, P * t:P * t + P], wt) for t in range(NT)]
                steps.append((mms, lambda b, m=m: b[0:P, 0:NT * m].rearrange("p (t m) -> p t m", m=m), dst, what))
        NB = 8

        @block.tensor
        def _(pe):
            for name in ready:
                pe.wait_ge(s[name], 1)
            for n, (mms, _, _, _) in enumerate(steps):
                if n >= NB:
                    pe.wait_ge(s["copied_a"] if n % 2 == 0 else s["copied_d"], (n - NB) // 2 + 1)
                for out, lhs, rhs in mms:
                    last = pe.matmul(out(self.bank(n % NB)), lhs, rhs, start=True, stop=True)
                last.then_inc(s["prod_ready"], 1)

        def evacuate(n, engine, acts):
            _, view, dst, what = steps[n]
            src = view(self.bank(n % NB))
            engine.wait_ge(s["prod_ready"], n + 1)
            if acts:
                return engine.activation(dst, src, what or ACT.Copy)
            if what == ACT.Relu:
                return engine.tensor_scalar(dst, src, 0.0, None, ALU.max)
            return engine.tensor_copy(dst, src)

        assert all(what in (None, ACT.Relu, ACT.Tanh) for *_, what in steps)
        only_act = any(what == ACT.Tanh for *_, what in steps)

        @block.scalar
        def _(act):
            for n in range(len(steps)):
                if only_act or n % 2 == 0:
                    evacuate(n, act, True).then_inc(s["copied_a"] if n % 2 == 0 else s["copied_d"], 1)

        if not only_act:
            @block.vector
            def _(dve):
                for n in range(1, len(steps), 2):
                    evacuate(n, dve, False).then_inc(s["copied_d"], 1)

    def softmax_attention(self, units, scale, causal, loads=None, n_loads=0):
        s = self.s
        order = (6, 0, 5, 1, 4, 2, 3) if causal else range(NT)
        work = [(u, t) for u in range(len(units)) for t in order]
        N = len(work)
        keys = lambda g: (work[g][1] + 1 if causal else NT)
        late = [keys(g) > 4 for g in range(N)]
        n_late = lambda g: sum(late[:max(g, 0)])
        S = lambda g: self.bank(2 * (g % 2), 2)
        T = lambda c: self.bank(4 + c)
        OT, OUT = self.bank(6), self.bank(7)
        PT = [self.PT[0:P, b, :] for b in range(3)]
        wide = units[0][2].shape[2]
        groups = 128 // wide
        d = HD if groups == 4 else D
        eyes = self.w("four_eyes" if groups == 4 else "two_eyes")
        rows = lambda g: wide * min(groups, keys(g))
        sums = lambda u: self.RS[:, 8 * (u % 2):8 * (u % 2) + NT]
        with self.block() as block:
            if loads is not None:
                @block.sync
                def _(sp):
                    loads(sp)
                    sp.wait_ge(s["loaded"], n_loads)

            @block.tensor
            def _(pe):
                def scores(g):
                    u, t = work[g]
                    qT, kT = units[u][:2]
                    if g >= 2:
                        pe.wait_ge(s["probs_ready"], g - 1)
                    width = keys(g) * P
                    for a in range(0, width, 512):
                        e = min(width, a + 512)
                        last = pe.matmul(S(g)[0:P, a:e], qT[:, P * t:P * t + P], kT[:, a:e],
                                         start=True, stop=not (causal and e > P * t))
                        if causal and e > P * t:
                            m = max(a, P * t)
                            last = pe.matmul(S(g)[0:P, m:e], self.identb[:, :], self.laterb[:, m - P * t:e - P * t],
                                             start=False, stop=True)
                    last.then_inc(s["scores_ready"], 1)

                def turn(g):
                    pe.wait_ge(s["probs_ready"], g + 1)
                    for k in range(keys(g)):
                        if k == 0 and g >= 1:
                            pe.wait_ge(s["turned_a"], g)
                        if k == 4 and n_late(g):
                            pe.wait_ge(s["turned_d"], n_late(g))
                        last = pe.transpose(T(k // 4)[0:P, P * (k % 4):P * (k % 4) + P],
                                            self.PR[:, g % 2, P * k:P * k + P], self.w("ident")[0:P, 0:P])
                        if k == min(4, keys(g)) - 1:
                            last.then_inc(s["probs_turned"], 1)
                        elif k == keys(g) - 1:
                            last.then_inc(s["turned"], 1)

                def weigh(g):
                    v = units[work[g][0]][2]
                    pe.wait_ge(s["turned_a"], g + 1)
                    if g >= 1:
                        pe.wait_ge(s["copied_d"], g)
                    for k in range(keys(g)):
                        if k == 4:
                            pe.wait_ge(s["turned_d"], n_late(g + 1))
                        at = wide * (k % groups)
                        last = pe.matmul(OT[at:at + wide, 0:P], v[:, k, :], PT[g % 3][:, P * k:P * k + P],
                                         start=(k < groups), stop=(k >= keys(g) - groups))
                    last.then_inc(s["pv_ready"], 1)

                def unturn(g):
                    u, t = work[g]
                    pe.wait_ge(s["copied_d"], g + 1)
                    if g % NT == 0 and u:
                        pe.wait_ge(s["out_done"], u)
                    pe.matmul(OUT[0:P, d * t:d * t + d], self.OTS[0:rows(g), g % 2, :], eyes[0:rows(g), :],
                              start=True, stop=True).then_inc(s["kv_ready"], 1)

                for i in range(N + 4):
                    if i < N:
                        scores(i)
                    if 0 <= i - 2 < N:
                        turn(i - 2)
                    if 0 <= i - 3 < N:
                        weigh(i - 3)
                    if 0 <= i - 4 < N:
                        unturn(i - 4)

            @block.vector
            def _(dve):
                link = self.chain(dve, s["step_dve"])

                def largest(g):
                    if g >= 2:
                        dve.wait_ge(s["probs_ready"], g - 1)
                    dve.wait_ge(s["scores_ready"], g + 1)
                    link(dve.tensor_reduce(self.NM[:, g % 2:g % 2 + 1], S(g)[0:P, 0:keys(g) * P], AX.X, ALU.max))
                    dve.tensor_scalar(self.NM[:, 2 + g % 2:3 + g % 2], self.NM[:, g % 2:g % 2 + 1], -scale, None,
                                      ALU.mult).then_inc(s["max_ready"], 1)

                def take(g):
                    dve.wait_ge(s["pv_ready"], g + 1)
                    if g >= 2:
                        dve.wait_ge(s["kv_ready"], g - 1)
                    dve.tensor_copy(self.OTS[0:rows(g), g % 2, :], OT[0:rows(g), 0:P]).then_inc(s["copied_d"], 1)

                def finish(u):
                    v, out, add = units[u][2:]
                    dve.wait_ge(s["kv_ready"], NT * (u + 1))
                    dve.wait_ge(s["probs_ready"], NT * (u + 1))
                    o = OUT[0:P, 0:NT * d].rearrange("p (t d) -> p t d", t=NT)
                    link(dve.reciprocal(sums(u), sums(u)))
                    r = sums(u).unsqueeze(2).broadcast_to((P, NT, d))
                    if add is None:
                        dve.tensor_tensor(out, o, r, ALU.mult).then_inc(s["out_done"], 1)
                    else:
                        dve.tensor_tensor(self.SQ, o, r, ALU.mult).then_inc(s["out_done"], 1)
                        dve.wait_ge(s["out_done"], u + 1)
                        link(dve.tensor_tensor(out, self.SQ, add, ALU.add))

                for i in range(N + 5):
                    if i < N:
                        largest(i)
                    if 0 <= i - 3 < N:
                        take(i - 3)
                    if 0 <= i - 5 and (i - 5) % NT == NT - 1:
                        finish((i - 5) // NT)
                    if 0 <= i - 2 < N and late[i - 2]:
                        g = i - 2
                        dve.wait_ge(s["turned"], n_late(g + 1))
                        if g >= 3:
                            dve.wait_ge(s["pv_ready"], g - 2)
                        dve.tensor_copy(PT[g % 3][:, 4 * P:keys(g) * P], T(1)[0:P, 0:(keys(g) - 4) * P])\
                           .then_inc(s["turned_d"], 1)

            @block.scalar
            def _(act):
                for i in range(N + 2):
                    if i >= 2:
                        g = i - 2
                        n = min(4, keys(g)) * P
                        act.wait_ge(s["probs_turned"], g + 1)
                        if g >= 3:
                            act.wait_ge(s["pv_ready"], g - 2)
                        act.activation(PT[g % 3][:, 0:n], T(0)[0:P, 0:n], ACT.Copy).then_inc(s["turned_a"], 1)
                    if i < N:
                        act.wait_ge(s["max_ready"], i + 1)
                        if i >= 2 and late[i - 2]:
                            act.wait_ge(s["turned"], n_late(i - 1))
                        u, t = work[i]
                        if t == order[0] and u >= 2:
                            act.wait_ge(s["out_done"], u - 1)
                        act.activation(self.PR[:, i % 2, 0:keys(i) * P], S(i)[0:P, 0:keys(i) * P], ACT.Exp,
                                       bias=self.NM[:, 2 + i % 2:3 + i % 2], scale=scale, accum_out=sums(u)[:, t:t + 1]).then_inc(s["probs_ready"], 1)

    def causal_product(self, qT, kT, v, relu, out):
        s = self.s
        taken = lambda j: s["copied_a"] if j % 2 == 0 else s["copied_d"]
        O = lambda h: self.bank(6 + h)[0:D, 0:HALF]
        OT = self.PR[0:D, 0, :]
        with self.block() as block:
            @block.tensor
            def _(pe):
                def weigh(k):
                    pe.wait_ge(s["mask_ready"], k + 1)
                    for h in range(2):
                        a, e = max(P * k, HALF * h), HALF * (h + 1)
                        if a < e:
                            last_tile = min(NT - 1, (e - 1) // P)
                            last = pe.matmul(O(h)[:, a - HALF * h:e - HALF * h], v[:, k, :], self.PT[0:P, k, a:e],
                                             start=(k == 0), stop=(k == last_tile))
                    last.then_inc(s["pv_ready"], 1)

                for j in range(NT + 2):
                    if j < NT:
                        if j >= 3:
                            pe.wait_ge(taken(j - 3), (j - 3) // 2 + 1)
                        S = self.bank(2 * (j % 3), 2)
                        for a in range(P * j, L, 512):
                            e = min(L, a + 512)
                            last = pe.matmul(S[0:P, a - P * j:e - P * j], kT[:, P * j:P * j + P], qT[:, a:e],
                                             start=True, stop=True)
                        last.then_inc(s["scores_ready"], 1)
                    if j >= 2:
                        weigh(j - 2)
                pe.wait_ge(s["turned_a"], 1)
                pe.wait_ge(s["turned_d"], 1)
                for t in range(NT):
                    last = pe.transpose(self.bank(0)[0:P, D * t:D * t + D], OT[:, P * t:P * t + P], self.w("ident")[0:D, 0:D])
                last.then_inc(s["out_done"], 1)

            @block.scalar
            def _(act):
                for j in range(0, NT, 2):
                    act.wait_ge(s["scores_ready"], j + 1)
                    act.activation(self.PT[0:P, j, P * j:L], self.bank(2 * (j % 3), 2)[0:P, 0:L - P * j],
                                   ACT.Relu if relu else ACT.Copy).then_inc(s["copied_a"], 1)
                act.wait_ge(s["pv_ready"], NT)
                act.activation(OT[:, 0:HALF], O(0), ACT.Copy).then_inc(s["turned_a"], 1)

            @block.gpsimd
            def _(pool):
                for j in range(NT):
                    pool.wait_ge(taken(j), j // 2 + 1)
                    diagonal = self.PT[0:P, j, P * j:P * j + P]
                    pool.tensor_tensor(diagonal, diagonal, self.w("keep_t"), ALU.mult).then_inc(s["mask_ready"], 1)

            @block.vector
            def _(dve):
                for j in range(1, NT, 2):
                    dve.wait_ge(s["scores_ready"], j + 1)
                    S = self.bank(2 * (j % 3), 2)[0:P, 0:L - P * j]
                    if relu:
                        dve.tensor_scalar(self.PT[0:P, j, P * j:L], S, 0.0, None, ALU.max).then_inc(s["copied_d"], 1)
                    else:
                        dve.tensor_copy(self.PT[0:P, j, P * j:L], S).then_inc(s["copied_d"], 1)
                dve.wait_ge(s["pv_ready"], NT)
                dve.tensor_copy(OT[:, HALF:L], O(1)).then_inc(s["turned_d"], 1)
                dve.wait_ge(s["out_done"], 1)
                out(dve, self.chain(dve, s["step_dve"]), self.bank(0)[0:P, 0:NT * D].rearrange("p (t d) -> p t d", d=D))

    def softmax_block(self, x, groups, width, before=None, after=None):
        s, m = self.s, self.ST[:, 0:groups]
        wide = m.unsqueeze(2).broadcast_to((P, groups, width))
        with self.block() as block:
            @block.vector
            def _(dve):
                link = self.chain(dve, s["step_dve"])
                if before is not None:
                    before(dve, link)
                link(dve.tensor_reduce(m, x, AX.X, ALU.max))
                dve.tensor_tensor(x, x, wide, ALU.subtract).then_inc(s["max_ready"], 1)
                dve.wait_ge(s["exp_ready"], 1)
                link(dve.tensor_reduce(m, x, AX.X, ALU.add))
                link(dve.reciprocal(m, m))
                link(dve.tensor_tensor(x, x, wide, ALU.mult))
                if after is not None:
                    after(dve, link)

            @block.scalar
            def _(act):
                act.wait_ge(s["max_ready"], 1)
                act.activation(x, x, ACT.Exp).then_inc(s["exp_ready"], 1)

    def zero(self, *views):
        with self.block() as block:
            @block.gpsimd
            def _(pool):
                link = self.chain(pool, self.s["step_pool"])
                for v in views:
                    link(pool.memset(v, 0.0))

    def head_operands(self, n):
        s, HW, x = self.s, self.HW1, self.SN
        cols = lambda h: slice(h * HALF, h * HALF + HALF)
        with self.block() as block:
            @block.tensor
            def _(pe):
                pe.wait_ge(s["weights_copied"], 1)
                for h in range(2):
                    pe.matmul(self.bank(h)[:, 0:HALF], HW[:, 0:128], x[:, cols(h)], start=True, stop=True).then_inc(s["prod_ready"], 1)
                for h in range(2):
                    pe.matmul(self.bank(2 + h)[:, 0:HALF], HW[:, 128:256], x[:, cols(h)], start=True, stop=True).then_inc(s["prod_ready"], 1)
                for t in range(NT):
                    last = pe.matmul(self.bank(4)[0:P, 32 * t:32 * t + 32], x[:, P * t:P * t + P], HW[:, 256:288], start=True, stop=True)
                last.then_inc(s["prod_ready"], 1)

            @block.scalar
            def _(act):
                act.wait_ge(s["prod_ready"], 1)
                for e in range(NE):
                    rows = slice(32 * e, 32 * e + HD)
                    act.activation(self.GB[rows, e, cols(0)], self.bank(0)[rows, 0:HALF], ACT.Copy).then_inc(s["copied_a"], 1)
                act.wait_ge(s["prod_ready"], 3)
                act.activation(self.KT[:, cols(0)], self.bank(2)[:, 0:HALF], ACT.Copy).then_inc(s["copied_a"], 1)

            @block.vector
            def _(dve):
                dve.tensor_copy(HW, self.wx("f1_heads")[:, bass.ds(n * 288, 288)]).then_inc(s["weights_copied"], 1)
                dve.wait_ge(s["prod_ready"], 2)
                for e in range(NE):
                    rows = slice(32 * e, 32 * e + HD)
                    dve.tensor_copy(self.GB[rows, e, cols(1)], self.bank(1)[rows, 0:HALF]).then_inc(s["copied_d"], 1)
                dve.wait_ge(s["prod_ready"], 4)
                dve.tensor_copy(self.KT[:, cols(1)], self.bank(3)[:, 0:HALF]).then_inc(s["copied_d"], 1)
                dve.wait_ge(s["prod_ready"], 5)
                dve.tensor_copy(self.VN[:, :, 0:32], self.bank(4)[0:P, 0:32 * NT].rearrange("p (t d) -> p t d", t=NT)).then_inc(s["copied_d"], 1)

    def add(self, dst, a, b):
        with self.block() as block:
            @block.vector
            def _(dve):
                dve.tensor_tensor(dst, a, b, ALU.add).then_inc(self.s["step_dve"], 1)

    def top_two(self, probs, gates, eps):
        s = self.s
        top, idx, pick = self.TOP, self.IDX, self.TOPF
        g3 = lambda a: a.rearrange("p (t e) -> p t e", e=8)
        with self.block() as block:
            @block.vector
            def _(dve):
                link = self.chain(dve, s["step_dve"])
                for t in range(NT):
                    dve.max(top[:, 8 * t:8 * t + 8], probs[:, t, :]).then_inc(s["max_ready"], 1)
                dve.wait_ge(s["max_ready"], NT)
                for t in range(NT):
                    dve.max_index(idx[:, 8 * t:8 * t + 8], top[:, 8 * t:8 * t + 8], probs[:, t, :]).then_inc(s["mask_ready"], 1)
                dve.wait_ge(s["mask_ready"], NT)
                link(dve.tensor_copy(pick, idx))
                at = lambda j: g3(pick)[:, :, j:j + 1].broadcast_to((P, NT, 8))
                e = g3(self.w("experts"))
                m0, m1 = g3(self.ST[:, 0:56]), g3(self.ST2[:, 0:56])
                link(dve.tensor_tensor(m0, e, at(0), ALU.is_equal))
                link(dve.tensor_tensor(m1, e, at(1), ALU.is_equal))
                link(dve.tensor_tensor(m0, m0, m1, ALU.add))
                den = self.ST2[:, 64:64 + NT]
                t3 = g3(top)
                link(dve.tensor_tensor(den.unsqueeze(2), t3[:, :, 0:1], t3[:, :, 1:2], ALU.add))
                if eps:
                    link(dve.tensor_scalar(den, den, eps, None, ALU.add))
                link(dve.reciprocal(den, den))
                link(dve.tensor_tensor(m0, m0, probs, ALU.mult))
                link(dve.tensor_tensor(gates, m0, den.unsqueeze(2).broadcast_to((P, NT, 8)), ALU.mult))

    def load_windows(self, sp, b, sem):
        x = self.dram["x"]
        for t in range(NT):
            src = bass.AP(x.tensor, x.offset + t * P * D, [[LIN * D, NSEQ + 1], [D, P], [1, WIN * D]])
            sp.dma_start(self.X9[:, t, :], src[bass.ds(b, 1)].rearrange("o p c -> (o p) c")).then_inc(sem, 16)

    def window_pool(self):
        s, X9, SC = self.s, self.X9, self.ST2[:, 0:NT * WIN]
        with self.block() as block:
            @block.tensor
            def _(pe):
                for t in range(NT + 1):
                    src = X9[:, t, 0:D] if t < NT else X9[:, NT - 1, (WIN - 1) * D:]
                    out = self.bank(t // 4)[0:D, P * (t % 4):P * (t % 4) + P]
                    pe.transpose(out, src, self.w("ident")[0:P, 0:P]).then_inc(s["turned"], 1)

            @block.scalar
            def _(act):
                act.wait_ge(s["turned"], 4)
                act.activation(self.XT[0:D, 0:4 * P], self.bank(0)[0:D, 0:4 * P], ACT.Copy).then_inc(s["copied_a"], 1)

            @block.vector
            def _(dve):
                dve.wait_ge(s["turned"], NT + 1)
                dve.tensor_copy(self.XT[0:D, 4 * P:L], self.bank(1)[0:D, 0:3 * P]).then_inc(s["copied_d"], 1)
                dve.tensor_copy(self.XT[0:D, L:LIN], self.bank(1)[0:D, 4 * P - WIN + 1:4 * P]).then_inc(s["copied_d"], 1)
        hk = LIN // 2
        T = [self.PT[:, 0, :], self.PT[:, 1, :]]
        rows = self.C2[0:WIN, :]
        cols = lambda h: slice(h * HALF, (h + 1) * HALF)
        with self.block() as block:
            @block.tensor
            def _(pe):
                for h in range(2):
                    pe.matmul(self.bank(h)[:, 0:hk], self.w("tok_k"), self.XT[0:D, h * hk:(h + 1) * hk],
                              start=True, stop=True).then_inc(s["prod_ready"], 1)
                for h in range(2):
                    a = WIN // 2 + h * HALF
                    pe.matmul(self.bank(2 + h)[:, 0:HALF], self.w("tok_q"), self.XT[0:D + 1, a:a + HALF],
                              start=True, stop=True).then_inc(s["prod_ready"], 1)
                for j in range(STEPS):
                    pe.wait_ge(s["tanh_ready"], j + 1)
                    for h in range(2):
                        last = pe.matmul(self.bank(4 + h)[0:WIN, 0:HALF], self.w("tok_v")[:, WIN * j:WIN * j + WIN], T[j % 2][:, cols(h)],
                                         start=(j == 0), stop=(j == STEPS - 1))
                    last.then_inc(s["scores_ready"], 1)
                pe.wait_ge(s["copied_a"], 1)
                pe.wait_ge(s["out_done"], 1)
                for t in range(NT):
                    last = pe.transpose(self.bank(6)[0:P, WIN * t:WIN * t + WIN], rows[:, P * t:P * t + P], self.w("ident")[0:WIN, 0:WIN])
                last.then_inc(s["turned"], 1)

            @block.vector
            def _(dve):
                dve.wait_ge(s["prod_ready"], 1)
                dve.tensor_copy(self.KT[0:D, 0:hk], self.bank(0)[0:D, 0:hk]).then_inc(s["copied_d"], 1)
                dve.tensor_copy(self.KT[D:128, 0:hk - 1], self.bank(0)[D:128, 1:hk]).then_inc(s["copied_d"], 1)
                dve.wait_ge(s["prod_ready"], 2)
                dve.tensor_copy(self.KT[0:D, hk:LIN], self.bank(1)[0:D, 0:hk]).then_inc(s["copied_d"], 1)
                dve.tensor_copy(self.KT[D:128, hk - 1:LIN - 1], self.bank(1)[D:128, 0:hk]).then_inc(s["copied_d"], 1)
                dve.tensor_copy(self.KT[D:128, LIN - 1:LIN], self.bank(1)[D:128, 0:1]).then_inc(s["copied_d"], 1)
                dve.wait_ge(s["copied_d"], 5)
                dve.wait_ge(s["turned_a"], 2)
                for j in range(STEPS):
                    if j >= 2:
                        dve.wait_ge(s["scores_ready"], j - 1)
                    dve.tensor_tensor(T[j % 2], self.QT[:, 0:L], self.KT[:, 2 * j:2 * j + L], ALU.add).then_inc(s["sum_ready"], 1)
                dve.wait_ge(s["scores_ready"], STEPS)
                dve.tensor_copy(rows[:, cols(1)], self.bank(5)[0:WIN, 0:HALF]).then_inc(s["out_done"], 1)
                dve.wait_ge(s["turned"], 1)
                dve.tensor_copy(SC, self.bank(6)[0:P, 0:NT * WIN]).then_inc(s["out_done"], 1)

            @block.scalar
            def _(act):
                for h in range(2):
                    act.wait_ge(s["prod_ready"], h + 3)
                    act.activation(self.QT[:, cols(h)], self.bank(2 + h)[:, 0:HALF], ACT.Copy).then_inc(s["turned_a"], 1)
                for j in range(STEPS):
                    act.wait_ge(s["sum_ready"], j + 1)
                    act.activation(T[j % 2], T[j % 2], ACT.Tanh).then_inc(s["tanh_ready"], 1)
                act.wait_ge(s["scores_ready"], STEPS)
                act.activation(rows[:, cols(0)], self.bank(4)[0:WIN, 0:HALF], ACT.Copy).then_inc(s["copied_a"], 1)

        sc3 = SC.rearrange("p (t w) -> p t w", w=WIN)

        def weigh(dve, link):
            x3 = X9.rearrange("p t (w c) -> p (t w) c", c=D)
            link(dve.tensor_tensor(x3, x3, SC.unsqueeze(2).broadcast_to((P, NT * WIN, D)), ALU.mult))
            link(dve.tensor_reduce(self.H, X9.rearrange("p t (w c) -> p t c w", c=D), AX.X, ALU.add))
        self.softmax_block(sc3, NT, WIN, after=weigh)

    def relu_attention(self, b):
        s = self.s
        xt = self.XT[:, 0:L]
        self.norm(self.H, self.X, NT, D, 1e-5, loads=(lambda sp: self.load_windows(sp, b + 1, s["loaded"]), 16 * NT), turned=self.XT,
                  jobs=[("c", self.wx("a0_q"), xt, self.QT[0:D, :], None), ("c", self.wx("a0_k"), xt, self.KT[0:D, :], None),
                      ("t", self.VO[:, :], self.XT[0:D, 0:L], self.V, None)])

        def out(dve, link, acc):
            link(dve.tensor_tensor(self.A, acc, self.w("inv_row").unsqueeze(2).broadcast_to((P, NT, D)), ALU.mult))
            link(dve.tensor_tensor(self.H, self.H, self.A, ALU.add))
        self.causal_product(self.QT[0:D, 0:L], self.KT[0:D, 0:L], self.V, True, out)

    def mixture(self, into, gated, chunk, hidden, out_w, bias, experts, glu):
        s = self.s
        N = 4 * experts
        U = lambda n: self.bank(2 * (n % 2), 2)
        B = lambda j: self.bank(4 + j % 2)[0:chunk, 0:HALF]
        O = lambda h: self.bank(6 + h)[0:D, 0:HALF]
        G = lambda n: self.GB[:, n % 4, 0:HALF]
        cols = lambda h: slice(h * HALF, (h + 1) * HALF)
        ready = "hidden_used" if gated or glu else "hidden_act"
        with self.block() as block:
            @block.tensor
            def _(pe):
                if bias is not None:
                    for h in range(2):
                        pe.matmul(O(h), bias[0], bias[1][:, cols(h)], start=True, stop=False)
                for n in range(N + 2):
                    if n < N:
                        e, h, c, j = n // 4, n // 2 % 2, n % 2, n // 2
                        if n >= 2:
                            pe.wait_ge(s["hidden_used"] if glu else s["hidden_act"], n - 1)
                        for i, wt in enumerate(hidden(e, c)):
                            last = pe.matmul(U(n)[0:chunk, 512 * i:512 * i + HALF], wt, self.XT[:, cols(h)], start=True, stop=True)
                        last.then_inc(s["hidden_ready"], 1)
                        if gated and c == 0:
                            if j >= 2:
                                pe.wait_ge(s["hidden_used"], 2 * j - 2)
                            pe.matmul(B(j), self.w("ident")[:, e:e + 1].broadcast_to((128, chunk)), self.GATES[:, cols(h)],
                                      start=True, stop=True).then_inc(s["scores_ready"], 1)
                    m = n - 2
                    if m >= 0:
                        e, h, c = m // 4, m // 2 % 2, m % 2
                        pe.wait_ge(s[ready], m + 1)
                        pe.matmul(O(h), out_w(e, c), G(m), start=(bias is None and e == 0 and c == 0),
                                  stop=(e == experts - 1 and c == 1)).then_inc(s["pv_ready"], 1)
                pe.wait_ge(s["copied_a"], 1)
                pe.wait_ge(s["copied_d"], 1)
                for t in range(NT):
                    last = pe.transpose(self.bank(0)[0:P, D * t:D * t + D], self.C2[0:D, P * t:P * t + P], self.w("ident")[0:D, 0:D])
                last.then_inc(s["turned"], 1)

            @block.scalar
            def _(act):
                for n in range(N):
                    act.wait_ge(s["hidden_ready"], n + 1)
                    if n >= 4:
                        act.wait_ge(s["pv_ready"], n - 3)
                    act.activation(G(n)[0:chunk, :], U(n)[0:chunk, 0:HALF], ACT.Silu if glu else ACT.Gelu)\
                       .then_inc(s["hidden_act"], 1)
                act.wait_ge(s["pv_ready"], N)
                act.activation(self.C2[0:D, cols(0)], O(0), ACT.Copy).then_inc(s["copied_a"], 1)

            @block.vector
            def _(dve):
                link = self.chain(dve, s["step_dve"])
                for n in range(N):
                    g = G(n)[0:chunk, :]
                    if gated or glu:
                        dve.wait_ge(s["hidden_act"], n + 1)
                    if glu:
                        link(dve.tensor_tensor(g, g, U(n)[0:chunk, 512:512 + HALF], ALU.mult))
                    if gated:
                        dve.wait_ge(s["scores_ready"], n // 2 + 1)
                        dve.tensor_tensor(g, g, B(n // 2), ALU.mult).then_inc(s["hidden_used"], 1)
                dve.wait_ge(s["pv_ready"], N)
                dve.tensor_copy(self.C2[0:D, cols(1)], O(1)).then_inc(s["copied_d"], 1)
                dve.wait_ge(s["turned"], 1)
                link(dve.tensor_tensor(into, into, self.bank(0)[0:P, 0:NT * D].rearrange("p (t d) -> p t d", d=D), ALU.add))

    def turn_gates(self):
        with self.block() as block:
            @block.gpsimd
            def _(pool):
                pool.memset(self.GATES, 1.0).then_inc(self.s["step_pool"], 1)
        self.turn(self.GT, self.GATES, rows=8)

    def first_mixture(self):
        self.norm(self.H, self.X, NT, D, 1e-5, turned=self.XT,
                  jobs=[("t", self.wx("m0_r"), self.XT[:, 0:L], self.RT, None)])
        self.softmax_block(self.RT, NT, 8)
        self.top_two(self.RT, self.GT, 0.0)
        self.turn_gates()
        w1, w2 = self.wx("m0_w1"), self.w("m0_w2")
        self.mixture(self.H, True, 128, lambda e, c: (w1[:, F0 * e + 128 * c:F0 * e + 128 * c + 128],),
                     lambda e, c: w2[:, D * (2 * e + c):D * (2 * e + c) + D], (self.wx("m0_b2"), self.GATES), E0 + 1, False)

    def phase_tables(self):
        s, ph, k, r = self.s, self.w("phases"), self.QT[:, 0:L], self.TRIG
        round_up = 12582912.0
        parts = [6.28125, 0.0019352436065673828, 6.357301884918343e-08]
        with self.block() as block:
            @block.vector
            def _(dve):
                link = self.chain(dve, s["step_dve"])
                link(dve.tensor_scalar(k, ph, 0.15915494309189535, None, ALU.mult))
                link(dve.tensor_scalar(k, k, round_up, None, ALU.add))
                link(dve.tensor_scalar(k, k, -round_up, None, ALU.add))
                link(dve.scalar_tensor_tensor(r, k, -parts[0], ph, ALU.mult, ALU.add))
                link(dve.scalar_tensor_tensor(r, k, -parts[1], r, ALU.mult, ALU.add))
                link(dve.scalar_tensor_tensor(r, k, -parts[2], r, ALU.mult, ALU.add))
                dve.tensor_scalar(r, r, PI_DOWN, -PI_DOWN, ALU.min, ALU.max).then_inc(s["phase_ready"], 1)

            @block.scalar
            def _(act):
                act.wait_ge(s["phase_ready"], 1)
                act.activation(r[0:D, :], r[0:D, :], ACT.Abs).then_inc(s["step_act"], 1)
                act.wait_ge(s["step_act"], 1)
                act.activation(r[0:D, :], r[0:D, :], ACT.Sin, bias=self.w("half_pi")[0:D, :], scale=-1.0).then_inc(s["step_act"], 1)
                act.activation(r[D:128, :], r[D:128, :], ACT.Sin).then_inc(s["step_act"], 1)

    def memory(self):
        s = self.s
        xt1 = self.XT[:, 0:L]
        self.norm(self.H, self.X, NT, D, 1e-5, turned=self.XT,
                  jobs=[("c", self.wx("h1_k1"), xt1, self.C1, ACT.Tanh), ("c", self.wx("h1_q1"), xt1, self.C2, ACT.Tanh)])
        self.project([("c", self.wx("h1_k2"), self.C1, self.KT, ACT.Tanh), ("c", self.wx("h1_q2"), self.C2, self.QT, ACT.Tanh)])
        with self.block() as block:
            @block.scalar
            def _(act):
                for u in (self.KT, self.QT):
                    act.activation(u[0:32, 0:L], u[0:32, 0:L], ACT.Abs).then_inc(s["step_act"], 1)
                act.wait_ge(s["step_act"], 2)
                for u in (self.KT, self.QT):
                    act.activation(u[0:32, 0:L], u[0:32, 0:L], ACT.Sin, bias=self.w("half_pi")[0:32, :],
                                   scale=-PI_DOWN).then_inc(s["step_act"], 1)
                    act.activation(u[32:64, 0:L], u[32:64, 0:L], ACT.Sin, scale=PI_DOWN).then_inc(s["step_act"], 1)
        self.project([("t", self.wx("h1_vc"), xt1, self.V, None), ("c", self.wx("h1_vp"), xt1, self.MV, None),
                      ("c", self.wx("h1_g1"), xt1, self.G1, ACT.Relu)])

        def content(dve, link, acc):
            link(dve.tensor_tensor(self.Y, acc, self.w("inv_pos32").unsqueeze(2).broadcast_to((P, NT, D)), ALU.mult))
        M = self.MP
        with self.block() as block:
            @block.vector
            def _(dve):
                link = self.chain(dve, s["step_dve"])
                link(dve.tensor_tensor(M, self.MV, self.TRIG, ALU.mult))
                link(dve.tensor_tensor_scan(self.MS, self.ONES, M, 0.0, ALU.mult, ALU.add))
                link(dve.tensor_tensor(M, self.MS, self.TRIG, ALU.mult))
        self.project([("t", self.w("two_eyes"), M, self.A, None), ("t", self.w("h1_g2"), self.G1, self.GL2, None)])
        self.causal_product(self.QT[0:D, 0:L], self.KT[0:D, 0:L], self.V, False, content)

        def combine(dve, link):
            g = lambda j: self.GL2[:, :, j:j + 1].broadcast_to((P, NT, D))
            link(dve.tensor_tensor(self.A, self.A, self.w("inv_pos").unsqueeze(2).broadcast_to((P, NT, D)), ALU.mult))
            link(dve.tensor_tensor(self.A, self.A, g(0), ALU.mult))
            link(dve.tensor_tensor(self.Y, self.Y, g(1), ALU.mult))
            link(dve.tensor_tensor(self.Y, self.Y, self.A, ALU.add))
        self.softmax_block(self.GL2, NT, 2, after=combine)
        self.norm(self.Y, self.A, NT, D, 1e-5, gamma=self.w("h1_g"), beta=self.w("h1_b"), turned=self.C1,
                  jobs=[("t", self.wx("h1_o"), self.C1, self.A, None)])
        with self.block() as block:
            @block.vector
            def _(dve):
                link = self.chain(dve, s["step_dve"])
                link(dve.tensor_tensor(self.H, self.H, self.X, ALU.add))
                link(dve.tensor_tensor(self.H, self.H, self.A, ALU.add))

    def head_inputs(self):
        self.norm(self.H, self.X, NT, D, 1e-5, turned=self.XT,
                  jobs=[("t", self.wx("f1_hl"), self.XT[:, 0:L], self.SX, None)])

    def keep_sequence(self, b):
        s = self.s
        with self.block() as block:
            @block.vector
            def _(dve):
                dve.tensor_copy(self.HA[:, bass.ds(b, 1)], self.H.rearrange("p t d -> p (t d)").unsqueeze(1)).then_inc(s["step_dve"], 1)
                dve.tensor_copy(self.RES[:, bass.ds(b, 1)].rearrange("p o t d -> p (o t) d"), self.SX[:, :, bass.ds(b * HD, HD)]).then_inc(s["step_dve"], 1)

    def fetch_sequence(self, b):
        s = self.s
        with self.block() as block:
            @block.vector
            def _(dve):
                dve.tensor_copy(self.H.rearrange("p t d -> p (t d)").unsqueeze(1), self.HA[:, bass.ds(b, 1)]).then_inc(s["step_dve"], 1)

    def expert_heads(self):
        s = self.s
        self.head_inputs()
        self.project([("c", self.wx("f1_hl"), self.XT[:, 0:L], self.SN, None)])
        self.zero(self.GB)
        with self.loop(NH) as n:
            self.head_operands(n)
            self.softmax_attention([(self.GB[:, e, :], self.KT[:, 0:L], self.VN[:, :, 0:32],
                                     self.QKV[:, :, bass.ds(n, 1), HD * e:HD * e + HD].rearrange("p t n d -> p t (n d)"), None)
                                    for e in range(NE)], float(HD) ** 0.5, True)
        with self.block() as block:
            @block.vector
            def _(dve):
                link = self.chain(dve, s["step_dve"])
                link(dve.tensor_scalar(self.A, self.SX, 0.0, None, ALU.not_equal))
                for e in range(NE):
                    q = self.QKV.rearrange("p t n (e d) -> p (t n) e d", e=NE)[:, :, e, :]
                    dve.tensor_tensor(q, q, self.A.rearrange("p t (n d) -> p (t n) d", d=HD), ALU.mult).then_inc(s["mask_ready"], 1)
        for g in range(2):
            self.turn(self.QKV[:, :, 2 * g:2 * g + 2, :].rearrange("p t n f -> p t (n f)"), self.QT if g == 0 else self.KT, rows=128)
        gate = self.w("f1_gate")
        self.project([("t", gate[:, 0:8], self.QT, self.GL[:, :, 0:8], None), ("t", gate[:, 8:16], self.KT, self.GL[:, :, 8:16], None)])
        over = lambda a, m: a.unsqueeze(1).broadcast_to((P, m, a.shape[1]))

        def bias(dve, link):
            link(dve.tensor_tensor(self.GL, self.GL, over(self.w("f1_gate_b"), NT), ALU.add))

        def mix(dve, link):
            q = self.QKV.rearrange("p t n (e d) -> p (t n e) d", e=NE)
            g = self.GL.rearrange("p t g -> p (t g)").unsqueeze(2).broadcast_to((P, NT * NH * NE, HD))
            link(dve.tensor_tensor(q, q, g, ALU.mult))
            link(dve.tensor_reduce(self.A.rearrange("p t (n d) -> p (t n) d", d=HD),
                                   self.QKV.rearrange("p t n (e d) -> p (t n) d e", e=NE), AX.X, ALU.add))
            a4 = self.A.rearrange("p t (n d) -> p t n d", d=HD)
            link(dve.tensor_tensor(a4, a4, self.RES.rearrange("p n t d -> p t n d"), ALU.add))
        self.softmax_block(self.GL.rearrange("p t (n e) -> p (t n) e", e=NE), NT * NH, NE, before=bias, after=mix)
        heads = lambda a: a.rearrange("p t (n d) -> p (t n) d", d=HD)
        self.norm(heads(self.A), heads(self.Y), NT * NH, HD, 1e-8, gamma=self.w("f1_g"), beta=self.w("f1_b"), turned=self.C1,
                  jobs=[("c", self.wx("f1_fc1"), self.C1, self.C2, ACT.Relu)])
        with self.block() as block:
            @block.vector
            def _(dve):
                dve.scalar_tensor_tensor(self.C2[0:D, :], self.C1[0:D, :], 0.0, self.C2[0:D, :], ALU.not_equal, ALU.mult)\
                   .then_inc(s["step_dve"], 1)
        self.project([("t", self.wx("f1_fc2"), self.C2, self.A, None)])
        with self.block() as block:
            @block.vector
            def _(dve):
                link = self.chain(dve, s["step_dve"])
                link(dve.scalar_tensor_tensor(self.A, self.Y, 0.0, self.A, ALU.not_equal, ALU.mult))
                link(dve.tensor_tensor(self.A, self.A, self.Y, ALU.add))
        self.norm(heads(self.A), heads(self.Y), NT * NH, HD, 1e-8, gamma=self.w("f1_fg"), beta=self.w("f1_fb"), turned=self.C1,
                  jobs=[("t", self.wx("f1_fgate"), self.C1, self.GL2b, None)])

        def out(dve, link):
            g = self.GL2b.rearrange("p t n -> p (t n)").unsqueeze(2).broadcast_to((P, NT * NH, HD))
            link(dve.tensor_tensor(heads(self.Y), heads(self.Y), g, ALU.mult))
            link(dve.tensor_tensor(self.H, self.H, self.Y, ALU.add))
        self.softmax_block(self.GL2b, NT, NH, after=out)

    def plain_attention(self):
        self.zero(self.QT[D:128, :], self.KT[D:128, :])
        xt = self.XT[:, 0:L]
        self.norm(self.H, self.X, NT, D, 1e-5, turned=self.XT,
                  jobs=[("c", self.wx("a2_q"), xt, self.QT, None), ("c", self.wx("a2_k"), xt, self.KT, None)])
        self.softmax_attention([(self.QT, self.KT[:, 0:L], self.X, self.H, self.H)], float(D) ** -0.5, False)

    def pair_cuts(self):
        s = self.s
        q = [self.PT[:, c, :] for c in range(4)]
        self.project([("c", self.wx("pk_q")[:, 128 * c:128 * c + 128], self.XT[:, 0:L], q[c], None) for c in range(4)])
        sims = [self.PT[0:P, 4 + i, :] for i in range(3)]
        SIM = self.PT[0:P, 4:7, :].rearrange("p a l -> p (a l)")
        sim = lambda t: SIM[:, 1024 * (t % 2):1024 * (t % 2) + 1024]
        keys = self.w("pk_keys")
        room = self.GB.rearrange("p a l -> p (a l)")[0:P, :]
        n_top, n_side, n_cand = NT * PKH * 24, 2 * PKH * 17, PKH * PAIRED
        TOP = room[:, 0:n_top].rearrange("p (t h k) -> p t h k", t=NT, h=PKH)
        V16 = [room[:, n_top + i * n_side:n_top + (i + 1) * n_side].rearrange("p (g k) -> p g k", k=17) for i in range(2)]
        at_cand = n_top + 2 * n_side
        CAND = [room[:, at_cand + i * n_cand:at_cand + (i + 1) * n_cand].rearrange("p (h k) -> p h k", h=PKH) for i in range(2)]
        with self.block() as block:
            @block.tensor
            def _(pe):
                for t in range(NT):
                    if t >= 2:
                        pe.wait_ge(s["copied_a"], t - 1)
                    for c in range(4):
                        last = pe.matmul(self.bank(2 * (t % 2) + c // 2)[0:P, 256 * (c % 2):256 * (c % 2) + 256],
                                         q[c][:, P * t:P * t + P], keys[:, 256 * c:256 * c + 256], start=True, stop=True)
                    last.then_inc(s["scores_ready"], 1)

            @block.scalar
            def _(act):
                for t in range(NT):
                    act.wait_ge(s["scores_ready"], t + 1)
                    if t >= 2:
                        act.wait_ge(s["sides_ranked"], t - 1)
                    act.activation(sim(t), self.bank(2 * (t % 2), 2)[0:P, :], ACT.Copy).then_inc(s["copied_a"], 1)

            @block.vector
            def _(dve):
                link = self.chain(dve, s["step_dve"])
                sides, heads = range(2 * PKH), range(PKH)

                def side_tops(t):
                    x = lambda g: sim(t)[:, NK * g:NK * g + NK]
                    v16 = V16[t % 2]
                    dve.wait_ge(s["copied_a"], t + 1)
                    if t >= 2:
                        dve.wait_ge(s["candidates_ready"], t - 1)
                    for r in range(2):
                        for g in sides:
                            last = dve.max(v16[:, g, 8 * r:8 * r + 8], x(g))
                        link(last)
                        for g in sides:
                            last = dve.match_replace(out=x(g), in_to_replace=v16[:, g, 8 * r:8 * r + 8], in_values=x(g), imm_value=LOWEST)
                        link(last)
                    dve.tensor_reduce(v16[:, :, 16], sim(t).rearrange("p (g k) -> p g k", k=NK), AX.X, ALU.max)\
                       .then_inc(s["sides_ranked"], 1)

                def pair_tops(t):
                    cand, top = CAND[t % 2], TOP[:, t]
                    dve.wait_ge(s["candidates_ready"], t + 1)
                    for r in range(3):
                        for h in heads:
                            last = dve.max(top[:, h, 8 * r:8 * r + 8], cand[:, h, :])
                        if r < 2:
                            link(last)
                            for h in heads:
                                last = dve.match_replace(out=cand[:, h, :], in_to_replace=top[:, h, 8 * r:8 * r + 8],
                                                         in_values=cand[:, h, :], imm_value=LOWEST)
                            link(last)
                        else:
                            last.then_inc(s["pairs_ranked"], 1)

                for t in range(NT + 1):
                    if t < NT:
                        side_tops(t)
                    if t >= 1:
                        pair_tops(t - 1)
                dve.wait_ge(s["pairs_ranked"], NT)
                cut, top = self.CUT.rearrange("p t h -> p (t h)").unsqueeze(2), TOP.rearrange("p t h k -> p (t h) k")
                link(dve.tensor_tensor(cut, top[:, :, 15:16], top[:, :, 16:17], ALU.add))
                link(dve.tensor_scalar(cut, cut, 0.5, None, ALU.mult))
                link(dve.tensor_scalar(top[:, :, 0:1], top[:, :, 0:1], -80.0, None, ALU.add))
                link(dve.tensor_tensor(cut, cut, top[:, :, 0:1], ALU.max))
                link(dve.tensor_scalar(cut, cut, -1.0, None, ALU.mult))

            @block.gpsimd
            def _(pool):
                for t in range(NT):
                    pool.wait_ge(s["sides_ranked"], t + 1)
                    if t >= 2:
                        pool.wait_ge(s["pairs_ranked"], t - 1)
                    s0, s1, cand = V16[t % 2][:, 0:PKH, :], V16[t % 2][:, PKH:, :], CAND[t % 2]
                    at = 0
                    for a, n in RUNS:
                        pool.tensor_tensor(cand[:, :, at:at + n], s0[:, :, a:a + 1].broadcast_to((P, PKH, n)), s1[:, :, 0:n], ALU.add)
                        at += n
                    pool.tensor_tensor(cand[:, :, at:at + 11], s0[:, :, 5:16],
                                       s1[:, :, 0:1].broadcast_to((P, PKH, 11)), ALU.add)
                    at += 11
                    pool.tensor_tensor(cand[:, :, at:at + 3], s0[:, :, 5:8], s1[:, :, 1:2].broadcast_to((P, PKH, 3)), ALU.add)
                    at += 3
                    for a in (0, 16):
                        last = pool.tensor_tensor(cand[:, :, at:at + 1], s0[:, :, a:a + 1], s1[:, :, 16 - a:17 - a], ALU.add)
                        at += 1
                    last.then_inc(s["candidates_ready"], 1)

    def load_heads(self, sp, g, sem):
        for j in range(2):
            sp.dma_start(self.TABLES[j], self.dram["tables"][bass.ds(2 * g + j, 1)].rearrange("o p c -> (o p) c")).then_inc(sem, 16)
            sp.dma_start(self.HWH[j], self.dram["head_weights"][bass.ds(2 * g + j, 1)].rearrange("o p c -> (o p) c")).then_inc(sem, 16)

    def key_scores(self):
        s = self.s
        QM = [self.ZS, self.KT[:, 0:L]]
        units = [(j, h) for j in range(2) for h in range(2)]
        cols = lambda h: slice(h * HALF, h * HALF + HALF)
        part = lambda u, k: self.SPLIT[:, u, k, :]
        rest = lambda u: self.GB.rearrange("p a l -> p (a l)")[:, HALF * u:HALF * u + HALF]
        with self.block() as block:
            @block.tensor
            def _(pe):
                for u, (j, h) in enumerate(units):
                    pe.matmul(self.bank(4 + u)[0:128, 0:HALF], self.HWH[j][:, 0:2 * D], self.XT[:, cols(h)],
                              start=True, stop=True).then_inc(s["prod_ready"], 1)
                for u, (j, h) in enumerate(units):
                    out, hw = self.bank(u)[0:128, 0:HALF], self.HWH[j]
                    pe.wait_ge(s["queries_copied"], u + 1)
                    pe.matmul(out, hw[:, 3 * D:5 * D], QM[j][:, cols(h)], start=True, stop=False)
                    pe.matmul(out, hw[0:PKH, 5 * D:7 * D], self.CUTT[:, cols(h)], start=False, stop=True)\
                      .then_inc(s["scores_ready"], 1)

            @block.scalar
            def _(act):
                for u, (j, h) in enumerate(units):
                    act.wait_ge(s["queries_copied"], u + 1)
                    act.activation(self.AQ[j][0:D, cols(h)], QM[j][0:D, cols(h)], ACT.Copy).then_inc(s["attention_queries_copied"], 1)
                for u in range(4):
                    act.wait_ge(s["scores_ready"], u + 1)
                    act.activation(part(u, 0), self.bank(u)[0:128, 0:HALF], ACT.Copy).then_inc(s["first_part"], 1)
                for u in range(4):
                    act.wait_ge(s["rest_ready"], u + 1)
                    act.activation(part(u, 1), rest(u), ACT.Copy).then_inc(s["second_part"], 1)

            @block.vector
            def _(dve):
                for u, (j, h) in enumerate(units):
                    dve.wait_ge(s["prod_ready"], u + 1)
                    dve.tensor_copy(QM[j][:, cols(h)], self.bank(4 + u)[0:128, 0:HALF]).then_inc(s["queries_copied"], 1)
                for u in range(4):
                    dve.wait_ge(s["first_part"], u + 1)
                    dve.tensor_tensor(rest(u), self.bank(u)[0:128, 0:HALF], part(u, 0), ALU.subtract).then_inc(s["rest_ready"], 1)
                for u in range(4):
                    dve.wait_ge(s["second_part"], u + 1)
                    dve.tensor_tensor(part(u, 2), rest(u), part(u, 1), ALU.subtract).then_inc(s["third_part"], 1)

    def key_pair(self, g):
        s = self.s
        self.key_scores()
        NC = NK // 2
        N = 4 * NC
        GBF = self.GB.rearrange("p a l -> p (a l)")
        E = lambda n: GBF[:, HALF * (n % 4):HALF * (n % 4) + HALF]
        PK = lambda n: GBF[:, HALF * (4 + n % 4):HALF * (4 + n % 4) + HALF]
        Z = lambda n: self.bank(n % 4)[0:128, 0:HALF]
        KV = lambda u: self.bank(4 + u % 2)[0:128, 0:HALF]
        SUM = lambda u: self.bank(6 + u % 2)[0:128, 0:HALF]
        cols = lambda u: slice((u % 2) * HALF, (u % 2) * HALF + HALF)
        ODD = lambda u: self.KT[:, cols(u)]
        ahead, lag = 3, 3
        PIECES = [slice(a, min(a + 93, HALF)) for a in range(0, HALF, 93)]
        with self.block() as block:
            @block.tensor
            def _(pe):
                def total(u):
                    pe.wait_ge(s["sum_even"], NC // 2 * (u + 1))
                    pe.matmul(SUM(u), self.ONE, self.ZS[:, cols(u)], start=True, stop=False)
                    pe.wait_ge(s["sum_odd"], NC // 2 * (u + 1))
                    pe.matmul(SUM(u), self.ONE, ODD(u), start=False, stop=True).then_inc(s["totals_ready"], 1)

                for n in range(N + ahead):
                    if n < N:
                        if n >= 4:
                            pe.wait_ge(s["picked"], n - 3)
                        for k in range(3):
                            last = pe.matmul(Z(n), self.PICK[:, 128 * (n % NC):128 * (n % NC) + 128], self.SPLIT[:, n // NC, k, :],
                                             start=(k == 0), stop=(k == 2))
                        last.then_inc(s["pair_scores_ready"], 1)
                    m = n - ahead
                    if m >= 0:
                        c, u = m % NC, m // NC
                        if c == 0 and u >= 2:
                            pe.wait_ge(s["out_done"], u - 1)
                        pe.wait_ge(s["picked"], m + 1)
                        pe.matmul(KV(u), self.TABLES[u // 2][:, 128 * c:128 * c + 128], PK(m),
                                  start=(c == 0), stop=(c == NC - 1)).then_inc(s["pv_ready"], 1)
                        if u and c == lag:
                            total(u - 1)
                total(3)

            @block.scalar
            def _(act):
                for n in range(N):
                    act.wait_ge(s["pair_scores_ready"], n + 1)
                    if n >= 4:
                        act.wait_ge(s["picked"], n - 3)
                    act.activation(E(n), Z(n), ACT.Exp).then_inc(s["exp_ready"], 1)

            @block.vector
            def _(dve):
                link = self.chain(dve, s["step_dve"])

                def finish(u, k):
                    if k == 0:
                        dve.wait_ge(s["totals_ready"], u + 1)
                        if u:
                            dve.wait_ge(s["out_done"], u)
                    dve.reciprocal(self.RZ[:, PIECES[k]], SUM(u)[:, PIECES[k]]).then_inc(s["reciprocals_ready"], 1)
                    if k == len(PIECES) - 1:
                        dve.wait_ge(s["reciprocals_ready"], len(PIECES) * (u + 1))
                        dve.tensor_tensor(self.KVP[u // 2][:, cols(u)], KV(u), self.RZ, ALU.mult).then_inc(s["out_done"], 1)

                for n in range(N):
                    c, u = n % NC, n // NC
                    dve.wait_ge(s["exp_ready"], n + 1)
                    if n >= 4:
                        dve.wait_ge(s["pv_ready"], n - 3)
                        dve.wait_ge(s["sum_even" if n % 2 == 0 else "sum_odd"], (n - 4) // 2 + 1)
                    dve.scalar_tensor_tensor(PK(n), Z(n), 0.0, E(n), ALU.is_ge, ALU.mult).then_inc(s["picked"], 1)
                    if c % 2 == 1:
                        dve.wait_ge(s["picked"], n + 1)
                        if c == 1:
                            if u >= 2:
                                dve.wait_ge(s["totals_ready"], u - 1)
                            dve.tensor_copy(ODD(u), PK(n)).then_inc(s["sum_odd"], 1)
                        else:
                            dve.wait_ge(s["sum_odd"], n // 2)
                            dve.tensor_tensor(ODD(u), ODD(u), PK(n), ALU.add).then_inc(s["sum_odd"], 1)
                    k = (c - lag - ahead) // 2
                    if u and c % 2 == 0 and 0 <= k < len(PIECES):
                        finish(u - 1, k)
                for k in range(len(PIECES)):
                    finish(3, k)

            @block.gpsimd
            def _(pool):
                for n in range(0, N, 2):
                    c, u = n % NC, n // NC
                    pool.wait_ge(s["picked"], n + 1)
                    z = self.ZS[:, cols(u)]
                    if c == 0:
                        if u >= 2:
                            pool.wait_ge(s["totals_ready"], u - 1)
                        pool.tensor_copy(z, PK(n)).then_inc(s["sum_even"], 1)
                    else:
                        pool.wait_ge(s["sum_even"], n // 2)
                        pool.tensor_tensor(z, z, PK(n), ALU.add).then_inc(s["sum_even"], 1)
        self.project([("t", self.HWH[j][:, 2 * D:3 * D], self.KVP[j], self.VP[j], None) for j in range(2)])
        self.softmax_attention([(self.AQ[j], self.KVP[j], self.VP[j], self.H, self.H) for j in range(2)], float(D) ** -0.5, True,
                               lambda sp: self.load_heads(sp, g + 1, s["loaded"]), 64)

    def product_keys(self):
        s = self.s
        self.norm(self.H, self.X, NT, D, 1e-5, turned=self.XT)
        self.pair_cuts()
        self.turn(self.CUT, self.CUTT, rows=PKH)
        with self.block() as block:
            @block.gpsimd
            def _(pool):
                for j in range(2):
                    pool.memset(self.AQ[j][D:128, :], 0.0).then_inc(s["step_pool"], 1)

            @block.vector
            def _(dve):
                eye = self.w("ident")
                dve.tensor_copy(self.PICK[0:NK, :].rearrange("p (a b) -> p a b", b=NK),
                                eye[0:NK, 0:NK].unsqueeze(2).broadcast_to((NK, NK, NK))).then_inc(s["step_dve"], 1)
                dve.tensor_copy(self.PICK[NK:128, :].rearrange("p (a b) -> p a b", b=NK),
                                eye[NK:128, NK:128].unsqueeze(1).broadcast_to((NK, NK, NK))).then_inc(s["step_dve"], 1)
        with self.loop(PKH // 2) as g:
            self.key_pair(g)

    def load_layer(self, sp, l, i):
        sp.dma_start(self.LW[i], self.dram["layers"][bass.ds(l, 1)].rearrange("o p c -> (o p) c")).then_inc(self.s["loaded"], 16)

    def inner_layer(self, l, i):
        s, W = self.s, self.LW[i]
        dh = D // 8
        scale = float(dh) ** -0.25
        xt = self.XT[:, 0:L]
        self.norm(self.R, self.X, NT, D, 1e-5, gamma=W[0:P, 704:768], beta=W[0:P, 768:832],
                  loads=(lambda sp: self.load_layer(sp, l + 1, 1 - i), 16), turned=self.XT,
                  jobs=[("t", W[:, 0:64], xt, self.A, None), ("c", W[:, 64:128], xt, self.KT, None),
                      ("t", W[:, 128:192], xt, self.V, None)])
        KM, KT, A, C1 = self.KM, self.KT[0:D, 0:L], self.A, self.C1
        queries = A.rearrange("p t (h d) -> p (t h) d", d=dh)
        stat = self.ST[:, 0:NT * 8]
        wide = stat.unsqueeze(2).broadcast_to((P, NT * 8, dh))
        tiles = lambda b: self.bank(b)[0:P, 0:NT * D].rearrange("p (t d) -> p t d", d=D)
        with self.block() as block:
            @block.vector
            def _(dve):
                link = self.chain(dve, s["step_dve"])
                link(dve.tensor_reduce(KM[:, 0:1], KT, AX.X, ALU.max))
                dve.tensor_scalar(KM[:, 1:2], KM[:, 0:1], -scale, None, ALU.mult).then_inc(s["max_ready"], 1)
                link(dve.tensor_reduce(stat, queries, AX.X, ALU.max))
                dve.tensor_tensor(queries, queries, wide, ALU.subtract).then_inc(s["centred"], 1)
                dve.wait_ge(s["keys_turned"], 1)
                dve.tensor_copy(self.Y, tiles(0)).then_inc(s["keys_copied"], 1)
                dve.wait_ge(s["queries_exp_ready"], 1)
                link(dve.tensor_reduce(stat, queries, AX.X, ALU.add))
                link(dve.reciprocal(stat, stat))
                dve.tensor_tensor(queries, queries, wide, ALU.mult).then_inc(s["normed"], 1)
                dve.wait_ge(s["exp_ready"], 1)
                link(dve.reciprocal(KM[:, 3:4], KM[:, 2:3]))
                dve.wait_ge(s["prod_ready"], 1)
                dve.tensor_tensor(self.CT, self.bank(1)[0:D, 0:D], self.w("blocks8"), ALU.mult).then_inc(s["mask_ready"], 1)
                dve.wait_ge(s["queries_turned"], NT)
                dve.tensor_copy(C1[0:D, 4 * P:L], self.bank(4)[0:D, 0:3 * P]).then_inc(s["queries_copied"], 1)
                dve.tensor_copy(self.CW[D:D + 1, :], W[D:D + 1, 192:256]).then_inc(s["out_done"], 1)
                dve.wait_ge(s["prod_ready"], 2)
                dve.tensor_scalar(self.CW[0:D, :], self.bank(2)[0:D, 0:D], KM[:, 3:4], None, ALU.mult).then_inc(s["out_done"], 1)
                dve.wait_ge(s["prod_ready"], 3)
                dve.tensor_tensor(self.R, self.R, tiles(5), ALU.add).then_inc(s["out_done"], 1)

            @block.scalar
            def _(act):
                act.wait_ge(s["max_ready"], 1)
                act.activation(KT, KT, ACT.Exp, bias=KM[:, 1:2], scale=scale, accum_out=KM[:, 2:3]).then_inc(s["exp_ready"], 1)
                act.wait_ge(s["centred"], 1)
                act.activation(queries, queries, ACT.Exp, scale=scale).then_inc(s["queries_exp_ready"], 1)
                act.wait_ge(s["queries_turned"], 4)
                act.activation(C1[0:D, 0:4 * P], self.bank(3)[0:D, 0:4 * P], ACT.Copy).then_inc(s["queries_copied_act"], 1)

            @block.tensor
            def _(pe):
                pe.wait_ge(s["exp_ready"], 1)
                for t in range(NT):
                    last = pe.transpose(self.bank(0)[0:P, D * t:D * t + D], KT[:, P * t:P * t + P], self.w("ident")[0:D, 0:D])
                last.then_inc(s["keys_turned"], 1)
                pe.wait_ge(s["keys_copied"], 1)
                for t in range(NT):
                    last = pe.matmul(self.bank(1)[0:D, 0:D], self.V[:, t, :], self.Y[:, t, :], start=(t == 0), stop=(t == NT - 1))
                last.then_inc(s["prod_ready"], 1)
                pe.wait_ge(s["normed"], 1)
                for t in range(NT):
                    pe.transpose(self.bank(3 + t // 4)[0:D, P * (t % 4):P * (t % 4) + P], A[:, t, :], self.w("ident")[0:P, 0:P])\
                      .then_inc(s["queries_turned"], 1)
                pe.wait_ge(s["mask_ready"], 1)
                pe.matmul(self.bank(2)[0:D, 0:D], self.CT, W[0:D, 192:256], start=True, stop=True).then_inc(s["prod_ready"], 1)
                pe.wait_ge(s["out_done"], 2)
                pe.wait_ge(s["queries_copied_act"], 1)
                pe.wait_ge(s["queries_copied"], 1)
                for t in range(NT):
                    last = pe.matmul(self.bank(5)[0:P, D * t:D * t + D], C1[0:D + 1, P * t:P * t + P], self.CW, start=True, stop=True)
                last.then_inc(s["prod_ready"], 1)
        self.norm(self.R, self.X, NT, D, 1e-5, gamma=W[0:P, 832:896], beta=W[0:P, 896:960], turned=self.XT)
        self.mixture(self.R, False, 128, lambda e, c: (W[:, 256 + 128 * c:384 + 128 * c],),
                     lambda e, c: W[:, 512 + D * c:576 + D * c], (W[:, 640:704], self.XT), 1, False)

    def inner_transformer(self):
        self.norm(self.H, self.R, NT, D, 1e-5)
        with self.loop(DEPTH // 2) as g:
            self.inner_layer(g * 2, 0)
            self.inner_layer(g * 2 + 1, 1)
        self.add(self.H, self.H, self.R)

    def last_part(self):
        s = self.s
        self.norm(self.H, self.R, NT, D, 1e-5)
        xt = self.XT[:, 0:L]
        qs, ks = self.ZS, self.KVT
        self.norm(self.R, self.X, NT, D, 1e-6, center=False, gamma=self.w("f3_1"), turned=self.XT,
                  jobs=[("c", self.wx("f3_q"), xt, self.QT, None), ("c", self.wx("f3_qs"), xt, qs, None),
                      ("c", self.wx("f3_k"), xt, self.KT, None), ("c", self.wx("f3_ks"), xt, ks, None),
                      ("t", self.wx("f3_v")[:, 0:HD], xt, self.VN[:, :, 0:HD], None),
                      ("t", self.wx("f3_v")[:, HD:2 * HD], xt, self.VN[:, :, 32:32 + HD], None)])
        self.zero(self.GB)
        with self.block() as block:
            @block.vector
            def _(dve):
                link = self.chain(dve, s["step_dve"])
                for x, sw in ((self.QT[:, 0:L], qs), (self.KT[:, 0:L], ks)):
                    link(dve.tensor_tensor(x, x, self.w("cos4"), ALU.mult))
                    link(dve.tensor_tensor(sw, sw, self.w("sin4"), ALU.mult))
                    if sw is ks:
                        link(dve.tensor_tensor(x, x, sw, ALU.add))
                    else:
                        for h in range(NH):
                            rows = slice(32 * h, 32 * h + HD)
                            link(dve.tensor_tensor(self.GB[rows, h, :], x[rows, :], sw[rows, :], ALU.add))
        self.softmax_attention([(self.GB[:, h, :], self.KT[:, 0:L], self.VN[:, :, 32 * (h // 2):32 * (h // 2) + 32],
                                 self.A[:, :, HD * h:HD * h + HD], None) for h in range(NH)], float(HD) ** -0.5, True)
        self.turn(self.A, self.C1)
        self.project([("t", self.wx("f3_o"), self.C1, self.A, None)])
        self.add(self.R, self.R, self.A)
        self.norm(self.R, self.X, NT, D, 1e-6, center=False, gamma=self.w("f3_2"), turned=self.XT,
                  jobs=[("t", self.wx("f3_r"), self.XT[:, 0:L], self.RT, None)])
        self.softmax_block(self.RT, NT, 8)
        self.top_two(self.RT, self.GT, 1e-9)
        self.turn_gates()
        w1, w3, w2, ch = self.wx("f3_w1"), self.wx("f3_w3"), self.wx("f3_w2"), F3 // 2
        up = lambda w, e, c: w[:, F3 * e + ch * c:F3 * e + ch * c + ch]
        self.mixture(self.R, True, ch, lambda e, c: (up(w1, e, c), up(w3, e, c)),
                     lambda e, c: w2[:, D * (2 * e + c):D * (2 * e + c) + D], None, E3, True)
        self.add(self.H, self.H, self.R)


def build(nc, where, dram, out):
    ctx = ExitStack()
    with ctx:
        t = Tower(nc, ctx, where, dram)
        s = t.s
        t.VO = t.sb("a0_vo", [D, D])
        t.RT = t.sb("router", [P, NT, 8])
        t.GT = t.sb("gates", [P, NT, 8])
        t.TOP = t.sb("top", [P, 8 * NT])
        t.TOPF = t.sb("top_at", [P, 8 * NT])
        t.IDX = t.sb("top_index", [P, 8 * NT], U32)
        t.GB = t.sb("hidden", [128, 4, L])
        t.HA = t.sb("h_all", [P, NSEQ, NT * D])
        STREAM = NK // 2 * 128
        t.TABLES = [t.sb(f"tables_{i}", [128, STREAM]) for i in range(2)]
        t.X9 = t.TABLES[0][0:P, 0:NT * WIN * D].rearrange("p (t c) -> p t c", t=NT)
        t.TRIG, t.MP, t.MV, t.MS, t.ONES = (t.TABLES[1][:, i * L:(i + 1) * L] for i in range(5))
        t.AQ = [t.sb(f"attention_queries_{i}", [128, L]) for i in range(2)]
        t.G1 = t.AQ[0][0:HD + 1, :]
        t.ONE = t.sb("ones_square", [128, 128])
        t.HWH = [t.sb(f"key_head_weights_{i}", [128, 7 * D]) for i in range(2)]
        t.CUT = t.sb("pair_cut", [P, NT, PKH])
        t.CUTT = t.sb("pair_cut_turned", [PKH, L])
        t.PICK = t.sb("pair_of_keys", [128, STREAM], BF16)
        t.SPLIT = t.sb("score_parts", [128, 4, 3, HALF], BF16)
        t.RZ = t.QT[:, 0:HALF]
        t.ZS = t.sb("pair_sums", [128, L])
        t.KVT = t.sb("picked_kv", [128, L])
        t.KVP = [t.KVT, t.sb("picked_kv_1", [128, L])]
        t.VP = [t.V, t.sb("v_1", [P, NT, D])]
        t.LW = [t.sb(f"layer_weights_{i}", [128, 960]) for i in range(2)]
        t.R = t.sb("inner_stream", [P, NT, D])
        t.KM = t.sb("key_stats", [D, 4])
        t.CT = t.sb("context_t", [D, D])
        t.CW = t.sb("context_out", [D + 1, D])
        t.C1 = t.sb("hidden_1", [128, L])
        t.C2 = t.sb("hidden_2", [128, L])
        t.GL2 = t.sb("gate_two", [P, NT, 2])
        t.GL2b = t.sb("gate_heads", [P, NT, NH])
        t.GL = t.sb("gate_experts", [P, NT, NH * NE])
        t.SX = t.sb("head_inputs", [P, NT, D])
        t.RES = t.sb("head_residuals", [P, NH, NT, HD])
        t.HW1 = t.sb("head_weights", [128, 288])
        t.SN = t.ZS
        t.GATES = t.ZS
        t.VN = t.sb("head_values", [P, NT, 64])
        t.QKV = t.PT.rearrange("p a l -> p (a l)")[0:P, 3 * L:3 * L + NT * NH * D].rearrange("p (t n f) -> p t n f", t=NT, n=NH)
        with t.block() as block:
            @block.sync
            def _(sp):
                first = dram["pack_0"].shape[1]
                sp.dma_start(t.W[:, 0:first], dram["pack_0"]).then_inc(s["loaded"], 16)
                sp.dma_start(t.W[:, first:first + dram["pack_1"].shape[1]], dram["pack_1"]).then_inc(s["loaded"], 16)
                t.load_windows(sp, 0, s["windows_loaded"])
                sp.wait_ge(s["windows_loaded"], 16 * NT)

            @block.gpsimd
            def _(pool):
                link = t.chain(pool, s["step_pool"])
                for rows in (t.XT[D:128, :], t.C1[D:128, :], t.C2[D:128, :], t.G1, t.ONES, t.ONE):
                    link(pool.memset(rows, 1.0))

            @block.vector
            def _(dve):
                dve.wait_ge(s["loaded"], 32)
                dve.tensor_copy(t.identb[:, :], t.w("ident")[0:P, 0:P]).then_inc(s["step_dve"], 1)
                dve.tensor_copy(t.laterb[:, :], t.w("later")).then_inc(s["step_dve"], 1)
                dve.wait_ge(s["prod_ready"], 1)
                dve.tensor_copy(t.VO[:, :], t.bank(0)[0:D, 0:D]).then_inc(s["step_dve"], 1)

            @block.tensor
            def _(pe):
                pe.wait_ge(s["loaded"], 32)
                pe.matmul(t.bank(0)[0:D, 0:D], t.w("a0_v"), t.w("a0_o"), start=True, stop=True).then_inc(s["prod_ready"], 1)

        t.phase_tables()

        def store(b):
            with t.block() as block:
                @block.sync
                def _(sp):
                    sp.dma_start(out[bass.ds(b, 1)].rearrange("o (t p) d -> (o p) t d", p=P), t.H).then_inc(s["stored"], 16)
                    sp.wait_ge(s["stored"], 16)

        with t.loop(NSEQ) as b:
            t.window_pool()
            t.relu_attention(b)
            t.first_mixture()
            t.memory()
            t.head_inputs()
            t.keep_sequence(b)
        with t.block() as block:
            @block.gpsimd
            def _(pool):
                link = t.chain(pool, s["step_pool"])
                link(pool.memset(t.VN, 0.0))

        with t.block() as block:
            @block.sync
            def _(sp):
                first = dram["pack_0"].shape[1]
                sp.dma_start(t.W[:, first:first + dram["pack_2"].shape[1]], dram["pack_2"]).then_inc(s["loaded"], 16)
                t.load_heads(sp, 0, s["loaded"])
                t.load_layer(sp, 0, 0)
                sp.wait_ge(s["loaded"], 96)
        with t.loop(NSEQ) as b:
            t.fetch_sequence(b)
            t.expert_heads()
            t.plain_attention()
            t.product_keys()
            t.inner_transformer()
            t.last_part()
            store(b)


def kernel(**inputs):
    import concourse.bacc as bacc
    from concourse.bass_utils import run_bass_kernel_spmd

    where, arrays = layout(inputs)
    nc = bacc.Bacc("TRN2", target_bir_lowering=False, num_devices=1)
    dram = {k: nc.dram_tensor(f"in_{k}", a.shape, F32, kind="ExternalInput").ap() for k, a in arrays.items()}
    out = nc.dram_tensor("out", (NSEQ, L, D), F32, kind="ExternalOutput").ap()
    build(nc, where, dram, out)
    r = run_bass_kernel_spmd(nc, [{f"in_{k}": a for k, a in arrays.items()}], core_ids=[0])
    return r.results[0]["out"]
```
